# Optimizing a Trainium2 kernel written in Bass

```python
import numpy as np
import jax
import jax.numpy as jnp

def _softmax(x, axis=-1):
    return jax.nn.softmax(x, axis=axis)

def _gelu(x):
    return jax.nn.gelu(x, approximate=True)

def _silu(x):
    return jax.nn.silu(x)

def _sigmoid(x):
    return jax.nn.sigmoid(x)

def _layernorm(x, axis=-1, eps=1e-05):
    m = jnp.mean(x, axis=axis, keepdims=True)
    v = jnp.var(x, axis=axis, keepdims=True)
    return (x - m) / jnp.sqrt(v + eps)

def _scatter_add(tgt, idx, src, axis=0):
    return tgt.at[idx].add(src)

def _segment_sum(src, seg, n):
    return jax.ops.segment_sum(src, seg, n)
kernel_name = 'mk_decoder_postln_d2_seqx_r4_30f02d'

def setup_inputs(seed: int=0):
    np.random.seed(seed)
    _w = jnp.asarray

    def _rec_inputs():
        import jax
        import jax.numpy as jnp
        _rk = jax.random.key(seed)
        x = 0.000341 + 1 * jax.random.normal(jax.random.fold_in(_rk, 1), (8, 256, 512), jnp.float32)
        _lenS = 256 - jax.random.randint(jax.random.fold_in(_rk, 7), (8,), 0, max(1, 256 // 4) + 1, jnp.int32)
        _lenS2 = 256 - jax.random.randint(jax.random.fold_in(_rk, 8), (8,), 0, max(1, 256 // 4) + 1, jnp.int32)
        _ctx_2048P = jax.random.normal(jax.random.fold_in(_rk, 11), (8, 16, 512), jnp.float32)
        _ctx_2048c = jax.random.dirichlet(jax.random.fold_in(_rk, 511), 0.3 * jnp.ones((16,), jnp.float32), (8, 256))
        _ctx_2048t = jnp.einsum('bsk,bkd->bsd', _ctx_2048c, _ctx_2048P)
        _ctx_2048t = _ctx_2048t * jax.lax.rsqrt(jnp.mean(jnp.square(_ctx_2048t)) + 1e-12) * 0.953939
        ctx_2048 = -1.47943e-05 + 1.00017 * (_ctx_2048t + 0.3 * jax.random.normal(jax.random.fold_in(_rk, 611), (8, 256, 512), jnp.float32))
        return (x, ctx_2048)
    x, ctx_2048 = _rec_inputs()

    def _L0_attn_setup():
        import jax, jax.numpy as jnp
        import numpy as np
        import math
        NUM_HEADS = 16
        SPARSITY_THRESHOLD = 0.2
        MIN_TOKENS = 32

        def _forward(x, Wq, bq, Wk, bk, Wv, bv, Wo, bo, Wi, bi):
            B, S, H = x.shape
            nh = NUM_HEADS
            hd = H // nh
            importance = (x @ Wi + bi)[..., 0]
            sorted_desc = jnp.sort(importance, axis=-1)[:, ::-1]
            tidx = min(max(1, int(S * SPARSITY_THRESHOLD)), S - 1)
            threshold = sorted_desc[:, tidx][:, None]
            sparse_mask = (importance > threshold).astype(x.dtype)
            if MIN_TOKENS > 0 and S > MIN_TOKENS:
                _, top_idx = jax.lax.top_k(importance, min(MIN_TOKENS, S))
                rows = jnp.arange(B)[:, None]
                min_mask = jnp.zeros_like(importance).at[rows, top_idx].set(1.0)
                sparse_mask = jnp.maximum(sparse_mask, min_mask)
            mask = sparse_mask[:, :, None, None]
            q = (x @ Wq + bq).reshape(B, S, nh, hd)
            k = (x @ Wk + bk).reshape(B, S, nh, hd) * mask
            v = (x @ Wv + bv).reshape(B, S, nh, hd) * mask
            scale = 1.0 / math.sqrt(hd)
            scores = jnp.einsum('bqhd,bkhd->bhqk', q, k) * scale
            attn = jax.nn.softmax(scores, axis=-1)
            out = jnp.einsum('bhqk,bkhd->bqhd', attn, v).reshape(B, S, H)
            return out @ Wo + bo
        key = jax.random.key(seed)
        ks = jax.random.split(key, 11)
        B, S, H = (4, 512, 512)
        s = 0.02
        return {'x': jax.random.normal(ks[0], (B, S, H), jnp.float32), 'Wq': jax.random.normal(ks[1], (H, H), jnp.float32) * s, 'bq': jax.random.normal(ks[2], (H,), jnp.float32) * s, 'Wk': jax.random.normal(ks[3], (H, H), jnp.float32) * s, 'bk': jax.random.normal(ks[4], (H,), jnp.float32) * s, 'Wv': jax.random.normal(ks[5], (H, H), jnp.float32) * s, 'bv': jax.random.normal(ks[6], (H,), jnp.float32) * s, 'Wo': jax.random.normal(ks[7], (H, H), jnp.float32) * s, 'bo': jax.random.normal(ks[8], (H,), jnp.float32) * s, 'Wi': jax.random.normal(ks[9], (H, 1), jnp.float32) * s, 'bi': jax.random.normal(ks[10], (1,), jnp.float32) * s}
    _L0_attn_all = _L0_attn_setup()
    _L0_attn_in = {k: v for k, v in _L0_attn_all.items() if k in ('Wq', 'bq', 'Wk', 'bk', 'Wv', 'bv', 'Wo', 'bo', 'Wi', 'bi')}
    del _L0_attn_all

    def _L0_xattn_setup():
        import jax, jax.numpy as jnp
        import numpy as np

        def _wkv(time_decay, time_first, k, v):
            w = -jnp.exp(time_decay)
            u = time_first
            B, T, C = k.shape
            aa = jnp.zeros((B, C), dtype=k.dtype)
            bb = jnp.zeros((B, C), dtype=k.dtype)
            pp = jnp.full((B, C), -1e+38, dtype=k.dtype)

            def step(carry, kv_t):
                aa, bb, pp = carry
                kt, vt = kv_t
                ww = u + kt
                q = jnp.maximum(pp, ww)
                e1 = jnp.exp(pp - q)
                e2 = jnp.exp(ww - q)
                y_t = (e1 * aa + e2 * vt) / (e1 * bb + e2)
                ww2 = pp + w
                q2 = jnp.maximum(ww2, kt)
                e1b = jnp.exp(ww2 - q2)
                e2b = jnp.exp(kt - q2)
                new_carry = (e1b * aa + e2b * vt, e1b * bb + e2b, q2)
                return (new_carry, y_t)
            ks = jnp.transpose(k, (1, 0, 2))
            vs = jnp.transpose(v, (1, 0, 2))
            _, ys = jax.lax.scan(step, (aa, bb, pp), (ks, vs))
            return jnp.transpose(ys, (1, 0, 2))
        key = jax.random.key(seed)
        k1, k2, k3, k4 = jax.random.split(key, 4)
        B, T, C = (8, 256, 512)
        return {'batch_size': B, 'seq_len': T, 'embedding_dim': C, 'time_decay': jax.random.normal(k1, (C,), dtype=jnp.float32), 'time_first': jax.random.normal(k2, (C,), dtype=jnp.float32), 'k': jax.random.normal(k3, (B, T, C), dtype=jnp.float32), 'v': jax.random.normal(k4, (B, T, C), dtype=jnp.float32)}
    _L0_xattn_all = _L0_xattn_setup()
    _L0_xattn_in = {k: v for k, v in _L0_xattn_all.items() if k in ('time_decay', 'time_first')}
    del _L0_xattn_all

    def _L0_ffn_setup():
        import jax, jax.numpy as jnp
        import numpy as np
        E, K, H, I, GS = (16, 4, 512, 384, 128)
        B, S = (1, 256)
        FP4_LUT = jnp.array([0.0, 0.5, 1.0, 1.5, 2.0, 3.0, 4.0, 6.0, -0.0, -0.5, -1.0, -1.5, -2.0, -3.0, -4.0, -6.0], jnp.float32)

        def dequant_fp4(packed, scales, gs=GS):
            shifts = jnp.arange(8, dtype=jnp.int32) * 4
            codes = packed[..., :, None, :] >> shifts[:, None] & 15
            w = FP4_LUT[codes]
            new_shape = codes.shape[:-3] + (codes.shape[-3] * 8, codes.shape[-1])
            w = w.reshape(new_shape)
            return w * jnp.repeat(scales, gs, axis=-2)

        def swiglu(h):
            g, u = jnp.split(h, 2, axis=-1)
            return jax.nn.silu(g) * u
        key = jax.random.key(seed)
        ks = jax.random.split(key, 10)

        def packed(k, shape):
            return jax.random.randint(k, shape, 0, 2147483647, dtype=jnp.int32)

        def scale(k, shape):
            return 0.01 + 0.04 * jax.random.uniform(k, shape, dtype=jnp.float32)
        return {'hidden': jax.random.normal(ks[0], (B, S, H), jnp.float32), 'gate_w': jax.random.normal(ks[1], (E, H), jnp.float32) * H ** (-0.5), 'gate_up_packed': packed(ks[2], (E, H // 8, 2 * I)), 'gate_up_scales': scale(ks[3], (E, H // GS, 2 * I)), 'down_packed': packed(ks[4], (E, I // 8, H)), 'down_scales': scale(ks[5], (E, I // GS, H)), 'shared_gate_up_packed': packed(ks[6], (H // 8, 2 * I)), 'shared_gate_up_scales': scale(ks[7], (H // GS, 2 * I)), 'shared_down_packed': packed(ks[8], (I // 8, H)), 'shared_down_scales': scale(ks[9], (I // GS, H))}
    _L0_ffn_all = _L0_ffn_setup()
    _L0_ffn_in = {k: v for k, v in _L0_ffn_all.items() if k in ('gate_w', 'gate_up_packed', 'gate_up_scales', 'down_packed', 'down_scales', 'shared_gate_up_packed', 'shared_gate_up_scales', 'shared_down_packed', 'shared_down_scales')}
    del _L0_ffn_all

    def _L1_attn_setup():
        import jax, jax.numpy as jnp
        import numpy as np
        EMBED = 512
        HEADS = 16
        ROPE_BASE = 10000.0
        NORM_EPS = 1e-12

        def _rope_sincos(seq, dim, dtype):
            inv_freq = ROPE_BASE ** (-(jnp.arange(0, dim, 2, dtype=jnp.float32) / dim))
            emb = jnp.repeat(inv_freq, 2)
            return (jnp.sin(seq * emb).astype(dtype), jnp.cos(seq * emb).astype(dtype))

        def _rotate(x, sin, cos):
            x1 = x[..., :-1:2]
            x2 = x[..., 1::2]
            x_rot = jnp.concatenate((-x2, x1), axis=-1)
            return x * cos + x_rot * sin

        def _l2_normalize(x):
            n = jnp.linalg.norm(x, axis=-1, keepdims=True)
            return x / jnp.maximum(n, NORM_EPS)
        key = jax.random.key(seed)
        ks = jax.random.split(key, 5)
        B, S, E = (2, 512, EMBED)
        std = 1.0 / np.sqrt(E)
        return {'x': jax.random.normal(ks[0], (B, S, E), dtype=jnp.float32), 'Wqkv': jax.random.normal(ks[1], (3 * E, E), dtype=jnp.float32) * std, 'bqkv': jax.random.normal(ks[2], (3 * E,), dtype=jnp.float32) * 0.02, 'Wout': jax.random.normal(ks[3], (E, E), dtype=jnp.float32) * std, 'bout': jax.random.normal(ks[4], (E,), dtype=jnp.float32) * 0.02}
    _L1_attn_all = _L1_attn_setup()
    _L1_attn_in = {k: v for k, v in _L1_attn_all.items() if k in ('Wqkv', 'bqkv', 'Wout', 'bout')}
    del _L1_attn_all

    def _L1_xattn_setup():
        import jax, jax.numpy as jnp
        import numpy as np
        DIM = 512
        NHEADS = 32
        HEAD_DIM = DIM // NHEADS
        EPS = 1e-06

        def _rmsnorm(t):
            return t * jax.lax.rsqrt(jnp.mean(t * t, axis=-1, keepdims=True) + EPS)
        key = jax.random.key(seed)
        kx, kc, kq, kk, kv = jax.random.split(key, 5)
        x = jax.random.normal(kx, (2, 1024, DIM), dtype=jnp.float32)
        context = jax.random.normal(kc, (2, 128, DIM), dtype=jnp.float32)
        std = 0.02
        Wq = jax.random.normal(kq, (DIM, DIM), dtype=jnp.float32) * std
        Wk = jax.random.normal(kk, (DIM, DIM), dtype=jnp.float32) * std
        Wv = jax.random.normal(kv, (DIM, DIM), dtype=jnp.float32) * std
        return {'x': x, 'context': context, 'Wq': Wq, 'Wk': Wk, 'Wv': Wv}
    _L1_xattn_all = _L1_xattn_setup()
    _L1_xattn_in = {k: v for k, v in _L1_xattn_all.items() if k in ('Wq', 'Wk', 'Wv')}
    del _L1_xattn_all

    def _L1_ffn_setup():
        import jax, jax.numpy as jnp
        import numpy as np
        _FP4_LUT = jnp.array([0.0, 0.5, 1.0, 1.5, 2.0, 3.0, 4.0, 6.0, -0.0, -0.5, -1.0, -1.5, -2.0, -3.0, -4.0, -6.0], dtype=jnp.float32)
        GROUP_SIZE = 128
        EPS = 1e-06

        def _dequant_fp4(packed_i32, scales_f16, group_size):
            out_f, in_p = packed_i32.shape
            w = packed_i32.astype(jnp.uint32)
            shifts = jnp.arange(8, dtype=jnp.uint32) * 4
            nib = w[:, :, None] >> shifts & jnp.uint32(15)
            vals = _FP4_LUT[nib.astype(jnp.int32)].reshape(out_f, in_p * 8)
            s = scales_f16.astype(jnp.float32).T
            s_full = jnp.repeat(s, group_size, axis=1)
            return vals * s_full
        key = jax.random.key(seed)
        k1, k2, k3, k4, k5 = jax.random.split(key, 5)
        B, S, H, I = (4, 512, 512, 1408)
        x = jax.random.normal(k1, (B, S, H), dtype=jnp.float32)
        gate_up_packed = jax.random.randint(k2, (2 * I, H // 8), 0, 2147483647, dtype=jnp.int32)
        gate_up_scales = jax.random.uniform(k3, (H // GROUP_SIZE, 2 * I), dtype=jnp.float32).astype(jnp.float16)
        down_packed = jax.random.randint(k4, (H, I // 8), 0, 2147483647, dtype=jnp.int32)
        down_scales = jax.random.uniform(k5, (I // GROUP_SIZE, H), dtype=jnp.float32).astype(jnp.float16)
        return {'x': x, 'gate_up_packed': gate_up_packed, 'gate_up_scales': gate_up_scales, 'down_packed': down_packed, 'down_scales': down_scales}
    _L1_ffn_all = _L1_ffn_setup()
    _L1_ffn_in = {k: v for k, v in _L1_ffn_all.items() if k in ('gate_up_packed', 'gate_up_scales', 'down_packed', 'down_scales')}
    del _L1_ffn_all
    return {'x': x, 'ctx_2048': ctx_2048, 'L0_attn_Wq': _L0_attn_in['Wq'], 'L0_attn_bq': _L0_attn_in['bq'], 'L0_attn_Wk': _L0_attn_in['Wk'], 'L0_attn_bk': _L0_attn_in['bk'], 'L0_attn_Wv': _L0_attn_in['Wv'], 'L0_attn_bv': _L0_attn_in['bv'], 'L0_attn_Wo': _L0_attn_in['Wo'], 'L0_attn_bo': _L0_attn_in['bo'], 'L0_attn_Wi': _L0_attn_in['Wi'], 'L0_attn_bi': _L0_attn_in['bi'], 'L0_xattn_time_decay': _L0_xattn_in['time_decay'], 'L0_xattn_time_first': _L0_xattn_in['time_first'], 'L0_ffn_gate_w': _L0_ffn_in['gate_w'], 'L0_ffn_gate_up_packed': _L0_ffn_in['gate_up_packed'], 'L0_ffn_gate_up_scales': _L0_ffn_in['gate_up_scales'], 'L0_ffn_down_packed': _L0_ffn_in['down_packed'], 'L0_ffn_down_scales': _L0_ffn_in['down_scales'], 'L0_ffn_shared_gate_up_packed': _L0_ffn_in['shared_gate_up_packed'], 'L0_ffn_shared_gate_up_scales': _L0_ffn_in['shared_gate_up_scales'], 'L0_ffn_shared_down_packed': _L0_ffn_in['shared_down_packed'], 'L0_ffn_shared_down_scales': _L0_ffn_in['shared_down_scales'], 'L1_attn_Wqkv': _L1_attn_in['Wqkv'], 'L1_attn_bqkv': _L1_attn_in['bqkv'], 'L1_attn_Wout': _L1_attn_in['Wout'], 'L1_attn_bout': _L1_attn_in['bout'], 'L1_xattn_Wq': _L1_xattn_in['Wq'], 'L1_xattn_Wk': _L1_xattn_in['Wk'], 'L1_xattn_Wv': _L1_xattn_in['Wv'], 'L1_ffn_gate_up_packed': _L1_ffn_in['gate_up_packed'], 'L1_ffn_gate_up_scales': _L1_ffn_in['gate_up_scales'], 'L1_ffn_down_packed': _L1_ffn_in['down_packed'], 'L1_ffn_down_scales': _L1_ffn_in['down_scales']}

def reference(x, ctx_2048, L0_attn_Wq, L0_attn_bq, L0_attn_Wk, L0_attn_bk, L0_attn_Wv, L0_attn_bv, L0_attn_Wo, L0_attn_bo, L0_attn_Wi, L0_attn_bi, L0_xattn_time_decay, L0_xattn_time_first, L0_ffn_gate_w, L0_ffn_gate_up_packed, L0_ffn_gate_up_scales, L0_ffn_down_packed, L0_ffn_down_scales, L0_ffn_shared_gate_up_packed, L0_ffn_shared_gate_up_scales, L0_ffn_shared_down_packed, L0_ffn_shared_down_scales, L1_attn_Wqkv, L1_attn_bqkv, L1_attn_Wout, L1_attn_bout, L1_xattn_Wq, L1_xattn_Wk, L1_xattn_Wv, L1_ffn_gate_up_packed, L1_ffn_gate_up_scales, L1_ffn_down_packed, L1_ffn_down_scales):
    import jax
    import jax.numpy as jnp

    def _L0_attn_ref(x, Wq, bq, Wk, bk, Wv, bv, Wo, bo, Wi, bi):
        import jax, jax.numpy as jnp
        import numpy as np
        import math
        NUM_HEADS = 16
        SPARSITY_THRESHOLD = 0.2
        MIN_TOKENS = 32

        def _forward(x, Wq, bq, Wk, bk, Wv, bv, Wo, bo, Wi, bi):
            B, S, H = x.shape
            nh = NUM_HEADS
            hd = H // nh
            importance = (x @ Wi + bi)[..., 0]
            sorted_desc = jnp.sort(importance, axis=-1)[:, ::-1]
            tidx = min(max(1, int(S * SPARSITY_THRESHOLD)), S - 1)
            threshold = sorted_desc[:, tidx][:, None]
            sparse_mask = (importance > threshold).astype(x.dtype)
            if MIN_TOKENS > 0 and S > MIN_TOKENS:
                _, top_idx = jax.lax.top_k(importance, min(MIN_TOKENS, S))
                rows = jnp.arange(B)[:, None]
                min_mask = jnp.zeros_like(importance).at[rows, top_idx].set(1.0)
                sparse_mask = jnp.maximum(sparse_mask, min_mask)
            mask = sparse_mask[:, :, None, None]
            q = (x @ Wq + bq).reshape(B, S, nh, hd)
            k = (x @ Wk + bk).reshape(B, S, nh, hd) * mask
            v = (x @ Wv + bv).reshape(B, S, nh, hd) * mask
            scale = 1.0 / math.sqrt(hd)
            scores = jnp.einsum('bqhd,bkhd->bhqk', q, k) * scale
            attn = jax.nn.softmax(scores, axis=-1)
            out = jnp.einsum('bhqk,bkhd->bqhd', attn, v).reshape(B, S, H)
            return out @ Wo + bo
        return _forward(x, Wq, bq, Wk, bk, Wv, bv, Wo, bo, Wi, bi)

    def _L0_xattn_ref(batch_size, seq_len, embedding_dim, time_decay, time_first, k, v):
        import jax, jax.numpy as jnp
        import numpy as np

        def _wkv(time_decay, time_first, k, v):
            w = -jnp.exp(time_decay)
            u = time_first
            B, T, C = k.shape
            aa = jnp.zeros((B, C), dtype=k.dtype)
            bb = jnp.zeros((B, C), dtype=k.dtype)
            pp = jnp.full((B, C), -1e+38, dtype=k.dtype)

            def step(carry, kv_t):
                aa, bb, pp = carry
                kt, vt = kv_t
                ww = u + kt
                q = jnp.maximum(pp, ww)
                e1 = jnp.exp(pp - q)
                e2 = jnp.exp(ww - q)
                y_t = (e1 * aa + e2 * vt) / (e1 * bb + e2)
                ww2 = pp + w
                q2 = jnp.maximum(ww2, kt)
                e1b = jnp.exp(ww2 - q2)
                e2b = jnp.exp(kt - q2)
                new_carry = (e1b * aa + e2b * vt, e1b * bb + e2b, q2)
                return (new_carry, y_t)
            ks = jnp.transpose(k, (1, 0, 2))
            vs = jnp.transpose(v, (1, 0, 2))
            _, ys = jax.lax.scan(step, (aa, bb, pp), (ks, vs))
            return jnp.transpose(ys, (1, 0, 2))
        assert seq_len <= 256
        return _wkv(time_decay, time_first, k, v)

    def _L0_ffn_ref(hidden, gate_w, gate_up_packed, gate_up_scales, down_packed, down_scales, shared_gate_up_packed, shared_gate_up_scales, shared_down_packed, shared_down_scales):
        import jax, jax.numpy as jnp
        import numpy as np
        E, K, H, I, GS = (16, 4, 512, 384, 128)
        B, S = (1, 256)
        FP4_LUT = jnp.array([0.0, 0.5, 1.0, 1.5, 2.0, 3.0, 4.0, 6.0, -0.0, -0.5, -1.0, -1.5, -2.0, -3.0, -4.0, -6.0], jnp.float32)

        def dequant_fp4(packed, scales, gs=GS):
            shifts = jnp.arange(8, dtype=jnp.int32) * 4
            codes = packed[..., :, None, :] >> shifts[:, None] & 15
            w = FP4_LUT[codes]
            new_shape = codes.shape[:-3] + (codes.shape[-3] * 8, codes.shape[-1])
            w = w.reshape(new_shape)
            return w * jnp.repeat(scales, gs, axis=-2)

        def swiglu(h):
            g, u = jnp.split(h, 2, axis=-1)
            return jax.nn.silu(g) * u
        b, s, h = hidden.shape
        x = hidden.reshape(-1, h)
        probs = jax.nn.softmax(x @ gate_w.T, axis=-1)
        vals, idx = jax.lax.top_k(probs, K)
        w = vals / jnp.sum(vals, axis=-1, keepdims=True)
        combine = jnp.einsum('tke,tk->te', jax.nn.one_hot(idx, E, dtype=x.dtype), w)
        w_gu = dequant_fp4(gate_up_packed, gate_up_scales)
        act = swiglu(jnp.einsum('th,ehi->eti', x, w_gu))
        w_d = dequant_fp4(down_packed, down_scales)
        y_e = jnp.einsum('eti,eih->eth', act, w_d)
        out = jnp.einsum('te,eth->th', combine, y_e)
        act_s = swiglu(x @ dequant_fp4(shared_gate_up_packed, shared_gate_up_scales))
        out = out + act_s @ dequant_fp4(shared_down_packed, shared_down_scales)
        return out.reshape(b, s, h)

    def _L1_attn_ref(x, Wqkv, bqkv, Wout, bout):
        import jax, jax.numpy as jnp
        import numpy as np
        EMBED = 512
        HEADS = 16
        ROPE_BASE = 10000.0
        NORM_EPS = 1e-12

        def _rope_sincos(seq, dim, dtype):
            inv_freq = ROPE_BASE ** (-(jnp.arange(0, dim, 2, dtype=jnp.float32) / dim))
            emb = jnp.repeat(inv_freq, 2)
            return (jnp.sin(seq * emb).astype(dtype), jnp.cos(seq * emb).astype(dtype))

        def _rotate(x, sin, cos):
            x1 = x[..., :-1:2]
            x2 = x[..., 1::2]
            x_rot = jnp.concatenate((-x2, x1), axis=-1)
            return x * cos + x_rot * sin

        def _l2_normalize(x):
            n = jnp.linalg.norm(x, axis=-1, keepdims=True)
            return x / jnp.maximum(n, NORM_EPS)
        B, S, E = x.shape
        H = HEADS
        D = E // H
        scale = E ** (-0.25)
        qkv = jnp.einsum('bse,fe->bsf', x, Wqkv) + bqkv
        q, k, v = jnp.split(qkv, 3, axis=-1)
        sin, cos = _rope_sincos(S, E, x.dtype)
        q = _rotate(q, sin, cos)
        k = _rotate(k, sin, cos)
        q = _l2_normalize(q) * scale
        k = _l2_normalize(k) * scale

        def split_heads(t):
            return t.reshape(B, S, H, D).transpose(0, 2, 1, 3)
        q, k, v = (split_heads(q), split_heads(k), split_heads(v))
        scores = jnp.einsum('bhqd,bhkd->bhqk', q, k)
        causal = jnp.tril(jnp.ones((S, S), dtype=bool))
        mask_value = jnp.finfo(scores.dtype).min
        scores = jnp.where(causal, scores, mask_value)
        attn_w = jax.nn.softmax(scores, axis=-1)
        attn = jnp.einsum('bhqk,bhkd->bhqd', attn_w, v)
        attn = attn.transpose(0, 2, 1, 3).reshape(B, S, E)
        return jnp.einsum('bse,fe->bsf', attn, Wout) + bout

    def _L1_xattn_ref(x, context, Wq, Wk, Wv):
        import jax, jax.numpy as jnp
        import numpy as np
        DIM = 512
        NHEADS = 32
        HEAD_DIM = DIM // NHEADS
        EPS = 1e-06

        def _rmsnorm(t):
            return t * jax.lax.rsqrt(jnp.mean(t * t, axis=-1, keepdims=True) + EPS)
        b, n, _ = x.shape
        m = context.shape[1]
        q = x @ Wq.T
        k_raw = context @ Wk.T
        v_raw = context @ Wv.T
        q = q.reshape(b, n, NHEADS, HEAD_DIM).transpose(0, 2, 1, 3)
        kv = jnp.concatenate([k_raw, v_raw], axis=-1)
        kv = kv.reshape(b, m, NHEADS, HEAD_DIM, 2)
        k = kv[..., 0].transpose(0, 2, 1, 3)
        v = kv[..., 1].transpose(0, 2, 1, 3)
        q = _rmsnorm(q)
        k = _rmsnorm(k)
        scale = HEAD_DIM ** (-0.5)
        scores = jnp.einsum('bhnd,bhmd->bhnm', q, k) * scale
        attn = jax.nn.softmax(scores, axis=-1)
        out = jnp.einsum('bhnm,bhmd->bhnd', attn, v)
        return out.transpose(0, 2, 1, 3).reshape(b, n, NHEADS * HEAD_DIM)

    def _L1_ffn_ref(x, gate_up_packed, gate_up_scales, down_packed, down_scales):
        import jax, jax.numpy as jnp
        import numpy as np
        _FP4_LUT = jnp.array([0.0, 0.5, 1.0, 1.5, 2.0, 3.0, 4.0, 6.0, -0.0, -0.5, -1.0, -1.5, -2.0, -3.0, -4.0, -6.0], dtype=jnp.float32)
        GROUP_SIZE = 128
        EPS = 1e-06

        def _dequant_fp4(packed_i32, scales_f16, group_size):
            out_f, in_p = packed_i32.shape
            w = packed_i32.astype(jnp.uint32)
            shifts = jnp.arange(8, dtype=jnp.uint32) * 4
            nib = w[:, :, None] >> shifts & jnp.uint32(15)
            vals = _FP4_LUT[nib.astype(jnp.int32)].reshape(out_f, in_p * 8)
            s = scales_f16.astype(jnp.float32).T
            s_full = jnp.repeat(s, group_size, axis=1)
            return vals * s_full
        I = gate_up_packed.shape[0] // 2
        w_gu = _dequant_fp4(gate_up_packed, gate_up_scales, GROUP_SIZE)
        w_down = _dequant_fp4(down_packed, down_scales, GROUP_SIZE)
        gate_up = jnp.einsum('bsh,oh->bso', x, w_gu)
        gate, up = (gate_up[..., :I], gate_up[..., I:])
        h = jax.nn.silu(gate) * up
        y = jnp.einsum('bsi,hi->bsh', h, w_down)
        rms = jnp.sqrt(jnp.mean(y * y, axis=-1, keepdims=True) + EPS)
        return y / rms
    x = _layernorm(x + _L0_attn_ref(x, L0_attn_Wq, L0_attn_bq, L0_attn_Wk, L0_attn_bk, L0_attn_Wv, L0_attn_bv, L0_attn_Wo, L0_attn_bo, L0_attn_Wi, L0_attn_bi), axis=-1)
    x = _layernorm(x + _L0_xattn_ref(8, 256, 512, L0_xattn_time_decay, L0_xattn_time_first, x, ctx_2048), axis=-1)
    x = _layernorm(x + _L0_ffn_ref(x, L0_ffn_gate_w, L0_ffn_gate_up_packed, L0_ffn_gate_up_scales, L0_ffn_down_packed, L0_ffn_down_scales, L0_ffn_shared_gate_up_packed, L0_ffn_shared_gate_up_scales, L0_ffn_shared_down_packed, L0_ffn_shared_down_scales), axis=-1)
    x = _layernorm(x + _L1_attn_ref(x, L1_attn_Wqkv, L1_attn_bqkv, L1_attn_Wout, L1_attn_bout), axis=-1)
    x = _layernorm(x + _L1_xattn_ref(x, ctx_2048, L1_xattn_Wq, L1_xattn_Wk, L1_xattn_Wv), axis=-1)
    x = _layernorm(x + _L1_ffn_ref(x, L1_ffn_gate_up_packed, L1_ffn_gate_up_scales, L1_ffn_down_packed, L1_ffn_down_scales), axis=-1)
    return x

_drawn_inputs = setup_inputs


def setup_inputs(seed=0):
    import zlib

    import numpy as np

    out = dict(_drawn_inputs(seed))
    spreads = {}
    factors = {'L0_attn_Wq': 4.879,
     'L0_attn_bq': 8.0,
     'L0_attn_Wk': 4.872,
     'L0_attn_bk': 49.984,
     'L0_attn_bv': 8.0}
    for name, (base, spread) in spreads.items():
        noise = np.random.default_rng([zlib.crc32(name.encode()), seed]).standard_normal(out[name].shape)
        drawn = base * np.exp(spread * noise) if base else spread * noise
        out[name] = jnp.asarray(drawn.astype(out[name].dtype))
    for name, factor in factors.items():
        out[name] = (out[name] * factor).astype(out[name].dtype)
    return out
```

```python
from contextlib import ExitStack

import numpy as np

import concourse.bass as bass
from concourse import mybir

F32 = mybir.dt.float32
F16 = mybir.dt.float16
F8 = mybir.dt.float8e4
I32 = mybir.dt.int32
ALU = mybir.AluOpType
ACT = mybir.ActivationFunctionType
AX = mybir.AxisListType

P = 128
B, S, D = 8, 256, 512
T = B * S
C = D // P
TT = 512
NT = T // TT
LN_EPS = 1e-5

H0, HD0 = 16, 32
KEEP = min(max(1, int(S * 0.2)), S - 1)
MIN_TOKENS = 32
SLOTS = 64
assert max(KEEP, MIN_TOKENS) <= SLOTS

E_ROUTED, TOP_K, I_MOE, GS = 16, 4, 384, 128
G_D, G_I = D // GS, I_MOE // GS
I_FFN = 1408
G_F = I_FFN // GS
H1, HD1 = 16, 32
HX, HDX = 32, 16

_WIDTHS = [("ident", P), ("ones", P), ("mean", P), ("tri", 2 * S), ("slot", P), ("causal", P),
           ("head4", 4), ("head8", 8), ("blk16", P), ("perm", P), ("den16", 64), ("expert_lt", 256),
           ("cos", D), ("sin", D), ("cosc", 4), ("sinc", 4), ("eps", 3)]
COL = {}
_at = 0
for _n, _w in _WIDTHS:
    COL[_n] = (_at, _at + _w)
    _at += _w
N_CONST = _at


def feature_order():
    p = np.arange(P)
    return 2 * (p % 64) + p // 64


def constants():
    c = np.zeros((P, N_CONST), np.float32)

    def put(name, value):
        a, b = COL[name]
        c[:, a:b] = value

    p = np.arange(P)
    order = feature_order()
    put("ident", np.eye(P))
    put("ones", 1.0)
    put("mean", 1.0 / D)
    j = np.arange(S)
    put("tri", np.concatenate([(j[None, :] < (q * P + p)[:, None]) for q in range(2)], axis=1))
    put("slot", np.tile(np.arange(SLOTS), P // SLOTS)[None, :])
    put("causal", p[None, :] >= p[:, None])
    put("head4", (p[:, None] // 32 == np.arange(4)[None, :]) * (D ** -0.5))
    put("head8", p[:, None] // 16 == np.arange(8)[None, :])
    put("blk16", (p[:, None] // 16 == p[None, :] // 16) / 16.0)
    put("perm", p[:, None] == order[None, :])
    put("den16", np.concatenate([np.arange(32) < 16, np.arange(32) >= 16])[None, :])
    e = np.arange(E_ROUTED)
    put("expert_lt", (e[None, :] < e[:, None]).reshape(1, 256))
    freq = (np.float32(10000.0) ** (-(np.arange(0, D, 2, dtype=np.float32) / np.float32(D)))).astype(np.float32)
    angle = (np.float32(S) * np.repeat(freq, 2)).astype(np.float32)
    cos, sin = np.cos(angle), np.sin(angle)
    sin = np.where(np.arange(D) < D // 2, -sin, sin)
    put("cos", cos[None, :])
    put("sin", sin[None, :])
    put("cosc", cos.reshape(4, P).T)
    put("sinc", sin.reshape(4, P).T)
    put("eps", np.array([[LN_EPS, 1e-6, 0.0]]))
    return c


class Chain:

    def __init__(self, eng, sem, base=0):
        self.eng, self.sem, self.base, self.n = eng, sem, base, 0

    def __call__(self, ins):
        self.n += 1
        ins.then_inc(self.sem, 1)
        self.eng.wait_ge(self.sem, self.base + self.n)


class Shared:
    pass


def bc(ap, axis, shape):
    return ap.unsqueeze(axis).to_broadcast(shape)


def layer_norm(nc, g, src, dst, layer, out_dram=None):
    with ExitStack() as ctx:
        def sb(name, shape, dt=F32):
            return ctx.enter_context(nc.sbuf_tensor(f"{name}_n{layer}", shape, dt))

        mean_ps = [ctx.enter_context(nc.psum_tensor(f"mean{i}_n{layer}", [P, TT], F32)) for i in range(2)]
        var_ps = [ctx.enter_context(nc.psum_tensor(f"var{i}_n{layer}", [P, TT], F32)) for i in range(2)]
        centred = [sb(f"centred{i}", [P, C, TT]) for i in range(2)]
        squares = [sb(f"squares{i}", [P, C, TT]) for i in range(2)]
        sd = [sb(f"sd{i}", [P, TT]) for i in range(2)]
        rs = [sb(f"rs{i}", [P, TT]) for i in range(2)]
        base = NT * layer
        mean_ready, centred_ready, squares_ready, var_ready, sd_ready, rs_ready, normed = g.ln_sems
        eps = g.const("eps")[:, 0:1]

        def tile(x, t):
            return x[:, :, t * TT:(t + 1) * TT]

        block = ctx.enter_context(nc.Block())

        @block.tensor
        def _(pe):
            def mean(t):
                if t >= 2:
                    pe.wait_ge(centred_ready, base + t - 1)
                for c in range(C):
                    mm = pe.matmul(mean_ps[t % 2][:, :], g.const("mean"), tile(src, t)[:, c, :],
                                   start=c == 0, stop=c == C - 1)
                mm.then_inc(mean_ready, 1)

            def var(t):
                pe.wait_ge(squares_ready, base + t + 1)
                if t >= 2:
                    pe.wait_ge(sd_ready, base + t - 1)
                for c in range(C):
                    mm = pe.matmul(var_ps[t % 2][:, :], g.const("mean"), squares[t % 2][:, c, :],
                                   start=c == 0, stop=c == C - 1)
                mm.then_inc(var_ready, 1)

            mean(0)
            for t in range(NT):
                if t + 1 < NT:
                    mean(t + 1)
                var(t)

        @block.vector
        def _(dve):
            def centre(t):
                dve.wait_ge(mean_ready, base + t + 1)
                if t >= 2:
                    dve.wait_ge(normed, base + t - 1)
                dve.tensor_tensor(centred[t % 2][:, :, :], tile(src, t), bc(mean_ps[t % 2][:, :], 1, [P, C, TT]),
                                  ALU.subtract).then_inc(centred_ready, 1)

            centre(0)
            for t in range(NT):
                if t + 1 < NT:
                    centre(t + 1)
                dve.wait_ge(sd_ready, base + t + 1)
                dve.reciprocal(rs[t % 2][:, :], sd[t % 2][:, :]).then_inc(rs_ready, 1)
                dve.wait_ge(rs_ready, base + t + 1)
                dve.tensor_tensor(tile(dst, t), centred[t % 2][:, :, :], bc(rs[t % 2][:, :], 1, [P, C, TT]),
                                  ALU.mult).then_inc(normed, 1)

        @block.scalar
        def _(act):
            def square(t):
                act.wait_ge(centred_ready, base + t + 1)
                if t >= 2:
                    act.wait_ge(var_ready, base + t - 1)
                act.activation(squares[t % 2][:, :, :], centred[t % 2][:, :, :], ACT.Square).then_inc(squares_ready, 1)

            square(0)
            for t in range(NT):
                if t + 1 < NT:
                    square(t + 1)
                act.wait_ge(var_ready, base + t + 1)
                if t >= 2:
                    act.wait_ge(rs_ready, base + t - 1)
                act.activation(sd[t % 2][:, :], var_ps[t % 2][:, :], ACT.Sqrt, bias=eps).then_inc(sd_ready, 1)

        @block.sync
        def _(sp):
            sp.wait_ge(normed, base + NT)
            if out_dram is not None:
                sp.dma_start(out_dram, dst[:, :, :]).then_inc(g.stored, 16)
                sp.wait_ge(g.stored, g.stored_base + 16)


def sparse_select(nc, g, a):
    with ExitStack() as ctx:
        def sb(name, shape, dt=F32):
            return ctx.enter_context(nc.sbuf_tensor("s_" + name, shape, dt))

        def sem(name):
            return ctx.enter_context(nc.semaphore("s_" + name))

        wi = sb("wi", [P, C])
        wib = sb("wib", [P, C, P])
        bi = sb("bi", [P, 1])
        wk = sb("wk", [P, C, D])
        wv = sb("wv", [P, C, D])
        bk = sb("bk", [P, C])
        bv = sb("bv", [1, D])
        imp = sb("imp", [P, B, S])
        ge = sb("ge", [P, B, 2, S])
        gt = sb("gt", [P, B, 2, S])
        own = sb("own", [P, 2 * B])
        small = sb("small", [P, 4, 2 * B])
        sel = sb("sel", [P, 2 * B, P])
        xtok = [sb(f"xtok{i}", [P, 2, D]) for i in range(2)]
        xsel = sb("xsel", [P, C, B, P])
        valid = sb("valid", [P, B, P])
        imp_ps = ctx.enter_context(nc.psum_tensor("s_imp_ps", [P, T], F32))
        row_ps = [ctx.enter_context(nc.psum_tensor(f"s_row{i}", [P, 512], F32)) for i in range(2)]
        xsel_ps = [ctx.enter_context(nc.psum_tensor(f"s_xs{i}", [P, 512], F32)) for i in range(2)]

        loaded, weights, wib_ready = sem("loaded"), sem("weights"), sem("wib_ready")
        imp_done, imp_copied, dve_step, sel_ready = sem("imp_done"), sem("imp_copied"), sem("dve_step"), sem("sel_ready")
        zeroed = sem("zeroed")
        tok_loaded = [sem(f"tok_loaded{i}") for i in range(2)]
        gathered, xsel_copied = sem("gathered"), sem("xsel_copied")
        row_done, row_used = sem("row_done"), sem("row_used")

        block = ctx.enter_context(nc.Block())

        @block.sync
        def _(sp):
            sp.dma_start(g.consts[:, :], a["consts"]).then_inc(loaded, 16)
            sp.dma_start(g.shift[:, :], a["shift"]).then_inc(loaded, 16)
            sp.dma_start(wi[:, :], a["wi0"]).then_inc(loaded, 16)
            sp.dma_start(bi[:, :], a["bi0"].to_broadcast([P, 1])).then_inc(loaded, 16)
            for t in range(NT):
                sp.dma_start(g.xt[:, :, t * TT:(t + 1) * TT], a["xt"][:, :, t * TT:(t + 1) * TT]).then_inc(loaded, 16)
            for dst, src in ((wk[:, :, :], a["wk0"]), (wv[:, :, :], a["wv0"]), (bk[:, :], a["bk0"]), (bv[:, :], a["bv0"])):
                sp.dma_start(dst, src).then_inc(weights, 16)
            with sp.Fori(0, B // 2) as i:
                for u in range(2):
                    sp.wait_ge(gathered, 2 * i + u + 1)
                    sp.dma_start(xtok[u][:, :, :], a["xtok"][:, bass.ds(4 * i + 2 * u, 2), :]).then_inc(tok_loaded[u], 16)

        @block.gpsimd
        def _(pool):
            pool.memset(g.keys[:, :, :, :], 0.0).then_inc(zeroed, 1)
            pool.memset(g.values[:, :, :, :], 0.0).then_inc(zeroed, 1)

        @block.scalar
        def _(act):
            for t in range(NT):
                act.wait_ge(imp_done, t + 1)
                act.activation(imp[:, 2 * t:2 * t + 2, :], imp_ps[:, t * TT:(t + 1) * TT].rearrange("p (b s) -> p b s", b=2),
                               ACT.Identity, bias=bi[:, :]).then_inc(imp_copied, 1)
            with act.Fori(0, B // 2) as i:
                for u in range(2):
                    act.wait_ge(gathered, 2 * i + u + 3)
                    act.activation(xsel[:, :, bass.ds(2 * i + u, 1), :],
                                   xsel_ps[u][:, :].rearrange("p (c o s) -> p c o s", c=C, o=1),
                                   ACT.Copy).then_inc(xsel_copied, 1)

        @block.vector
        def _(dve):
            step = Chain(dve, dve_step)
            dve.wait_ge(loaded, 16 * (4 + NT))
            dve.tensor_copy(wib[:, :, :], bc(wi[:, :], 2, [P, C, P])).then_inc(wib_ready, 1)
            dve.wait_ge(imp_copied, NT)
            step(dve.tensor_tensor(sel[:, :, :], imp[:, :, :].rearrange("p b (q i) -> p (b q) i", q=2),
                                   bc(g.const("ident"), 1, [P, 2 * B, P]), ALU.mult))
            step(dve.tensor_reduce(own[:, :], sel[:, :, :], AX.X, ALU.add))
            own_v = own[:, :].rearrange("p (b q) -> p b q", q=2)
            for q in range(2):
                mine = bc(own_v[:, :, q], 2, [P, B, S])
                dve.tensor_tensor(ge[:, :, q, :], imp[:, :, :], mine, ALU.is_ge)
                last = dve.tensor_tensor(gt[:, :, q, :], imp[:, :, :], mine, ALU.is_gt)
            step(last)
            n_ge, n_gt, ties, keep = (small[:, k, :] for k in range(4))
            dve.tensor_reduce(n_ge, ge[:, :, :, :].rearrange("p b q j -> p (b q) j"), AX.X, ALU.add)
            step(dve.tensor_reduce(n_gt, gt[:, :, :, :].rearrange("p b q j -> p (b q) j"), AX.X, ALU.add))
            step(dve.tensor_tensor(ge[:, :, :, :], ge[:, :, :, :], gt[:, :, :, :], ALU.subtract))
            step(dve.tensor_tensor(ge[:, :, :, :].rearrange("p b q j -> p b (q j)"),
                                   ge[:, :, :, :].rearrange("p b q j -> p b (q j)"),
                                   bc(g.const("tri"), 1, [P, B, 2 * S]), ALU.mult))
            step(dve.tensor_reduce(ties, ge[:, :, :, :].rearrange("p b q j -> p (b q) j"), AX.X, ALU.add))
            step(dve.tensor_tensor(ties, ties, n_gt, ALU.add))
            dve.tensor_scalar(n_ge, n_ge, float(KEEP) + 0.5, None, ALU.is_lt)
            step(dve.tensor_scalar(keep, ties, float(MIN_TOKENS) - 0.5, None, ALU.is_lt))
            step(dve.tensor_tensor(keep, keep, n_ge, ALU.max))
            step(dve.tensor_tensor(sel[:, :, :], bc(g.const("slot"), 1, [P, 2 * B, P]), bc(ties, 2, [P, 2 * B, P]),
                                   ALU.is_equal))
            dve.tensor_tensor(sel[:, :, :], sel[:, :, :], bc(keep, 2, [P, 2 * B, P]), ALU.mult).then_inc(sel_ready, 1)
            for n in range(2):
                dve.wait_ge(row_done, n + 1)
                dve.tensor_copy(valid[:, 4 * n:4 * n + 4, :], row_ps[n][:, :].rearrange("p (b s) -> p b s", b=4))\
                   .then_inc(row_used, 1)
            dve.wait_ge(row_used, 2)
            dve.wait_ge(weights, 64)
            dve.wait_ge(zeroed, 2)
            for m in range(C):
                dve.wait_ge(row_done, 3 + m)
                ps = row_ps[m % 2][:, :].rearrange("p (b s) -> p b s", b=B)
                for j in range(4):
                    r = slice(32 * j, 32 * j + 32)
                    last = dve.scalar_tensor_tensor(g.keys[r, m, :, j * SLOTS:(j + 1) * SLOTS], valid[r, :, 0:SLOTS],
                                                    bk[r, m:m + 1], ps[r, :, :], ALU.mult, ALU.add)
                last.then_inc(row_used, 1)
            for b in range(B):
                dve.wait_ge(row_done, 3 + C + b)
                ps = row_ps[b % 2][:, :].rearrange("p (n two d) -> p n two d", two=2, d=HD0)
                for u in range(2):
                    r = slice(64 * u, 64 * u + 64)
                    last = dve.tensor_copy(g.values[r, b, :, 32 * u:32 * u + 32], ps[r, :, u, :])
                last.then_inc(row_used, 1)

        @block.tensor
        def _(pe):
            pe.wait_ge(wib_ready, 1)
            for t in range(NT):
                for c in range(C):
                    mm = pe.matmul(imp_ps[:, t * TT:(t + 1) * TT], wib[:, c, :], g.xt[:, c, t * TT:(t + 1) * TT],
                                   start=c == 0, stop=c == C - 1)
                mm.then_inc(imp_done, 1)
            pe.wait_ge(sel_ready, 1)
            sel_v = sel[:, :, :].rearrange("p (b q) s -> p b q s", q=2)
            for n in range(2):
                for q in range(2):
                    mm = pe.matmul(row_ps[n][:, :], g.const("ones"), sel_v[:, 4 * n:4 * n + 4, q, :],
                                   start=q == 0, stop=q == 1)
                mm.then_inc(row_done, 1)
            pe.sem_inc(gathered, 2)
            pe.sem_inc(xsel_copied, 2)
            with pe.Fori(0, B // 2) as i:
                for u in range(2):
                    pe.wait_ge(tok_loaded[u], 16 * i + 16)
                    pe.wait_ge(xsel_copied, 2 * i + u + 1)
                    for c in range(C):
                        for q in range(2):
                            mm = pe.matmul(xsel_ps[u][:, c * P:(c + 1) * P], xtok[u][:, q, c * P:(c + 1) * P],
                                           sel[:, bass.ds(4 * i + 2 * u + q, 1), :], start=q == 0, stop=q == 1)
                    mm.then_inc(gathered, 1)
            pe.wait_ge(xsel_copied, B + 2)
            pe.wait_ge(weights, 64)
            for m in range(C):
                pe.wait_ge(row_used, m + 1)
                for c in range(C):
                    mm = pe.matmul(row_ps[m % 2][:, :], wk[:, c, m * P:(m + 1) * P], xsel[:, c, :, 0:SLOTS],
                                   start=c == 0, stop=c == C - 1)
                mm.then_inc(row_done, 1)
            for b in range(B):
                pe.wait_ge(row_used, C + b + 1)
                for c in range(C):
                    pe.matmul(row_ps[b % 2][:, :], xsel[:, c, b, :], wv[:, c, :], start=c == 0, stop=False)
                pe.matmul(row_ps[b % 2][:, :], valid[0:1, b, :], bv[:, :], start=False, stop=True).then_inc(row_done, 1)


def sparse_attention(nc, g, a):
    scale = HD0 ** -0.5
    with ExitStack() as ctx:
        def sb(name, shape, dt=F32):
            return ctx.enter_context(nc.sbuf_tensor("a0_" + name, shape, dt))

        def sem(name):
            return ctx.enter_context(nc.semaphore("a0_" + name))

        def ps(name, shape):
            return ctx.enter_context(nc.psum_tensor("a0_" + name, shape, F32))

        wq = sb("wq", [P, C, D])
        wo = sb("wo", [P, C, D])
        bq = sb("bq", [P, C])
        bo = sb("bo", [P, C])
        q_sb = sb("q", [P, C, S])
        v_sb = sb("v", [P, H0 // 2, 64])
        e_sb = [sb(f"e{i}", [P, H0, SLOTS]) for i in range(2)]
        mx = [sb(f"mx{i}", [P, H0]) for i in range(2)]
        e0 = [sb(f"e0{i}", [P, H0]) for i in range(2)]
        den = [sb(f"den{i}", [P, H0]) for i in range(2)]
        pt = sb("pt", [P, H0 // 2, S])
        at = sb("at", [P, C, S])
        head_ps = ps("head", [P, C, S])
        s_ps = [ps(f"s{i}", [P, H0, SLOTS]) for i in range(2)]
        pt_ps = ps("pt_ps", [P, H0 // 2, P])
        o_ps = s_ps[0][:, :, :].rearrange("p h s -> p (h s)").rearrange("p (c q) -> p c q", c=C)

        weights = sem("weights")
        q_done, q_copied, s_done, shifted, exped, p_ready = (sem(n) for n in ("q_done", "q_copied", "s_done", "shifted", "exped", "p_ready"))
        t_done, t_copied, v_copied, av_done, av_copied, o_done, added, step_sem = (
            sem(n) for n in ("t_done", "t_copied", "v_copied", "av_done", "av_copied", "o_done", "added", "step"))

        block = ctx.enter_context(nc.Block())

        @block.sync
        def _(sp):
            for dst, src in ((wq[:, :, :], a["wq0"]), (wo[:, :, :], a["wo0"]), (bq[:, :], a["bq0"]), (bo[:, :], a["bo0"])):
                sp.dma_start(dst, src).then_inc(weights, 16)

        @block.gpsimd
        def _(pool):
            with pool.Fori(0, B) as b:
                pool.wait_ge(av_done, b + 1)
                pool.tensor_copy(v_sb[:, :, :].rearrange("p n d -> p (n d)"),
                                 g.values[:, bass.ds(b, 1), :, :].rearrange("p b n d -> p (b n d)"))\
                    .then_inc(v_copied, 1)

        @block.tensor
        def _(pe):
            pe.wait_ge(weights, 64)
            pe.sem_inc(av_done, 1)
            with pe.Fori(0, B) as b:
                pe.wait_ge(av_copied, b + 1)
                for m in range(C):
                    for c in range(C):
                        mm = pe.matmul(head_ps[:, m, :], wq[:, c, m * P:(m + 1) * P], g.xt[:, c, bass.ts(b, S)],
                                       start=c == 0, stop=c == C - 1)
                mm.then_inc(q_done, 1)
                pe.wait_ge(q_copied, b + 1)
                pe.wait_ge(added, b + 1)
                for q in range(2):
                    for c in range(C):
                        mm = pe.matmul(s_ps[q][:, 4 * c:4 * c + 4, :], q_sb[:, c, q * P:(q + 1) * P],
                                       g.keys[:, c, bass.ds(b, 1), :], start=True, stop=True)
                    mm.then_inc(s_done, 1)
                for q in range(2):
                    pe.wait_ge(p_ready, 2 * b + q + 1)
                    pe.wait_ge(t_copied, 2 * b + q + 1)
                    for n in range(H0 // 2):
                        mm = pe.transpose(pt_ps[:, n, :], e_sb[q][:, 2 * n:2 * n + 2, :].rearrange("p h s -> p (h s)"),
                                          g.const("ident"))
                    mm.then_inc(t_done, 1)
                pe.wait_ge(t_copied, 2 * b + 3)
                pe.wait_ge(v_copied, b + 1)
                for n in range(H0 // 2):
                    r = 64 * (n % 2)
                    mm = pe.matmul(head_ps[r:r + 64, n // 2, :], v_sb[:, n, :], pt[:, n, :], start=True, stop=True)
                mm.then_inc(av_done, 1)
                pe.wait_ge(av_copied, b + 2)
                for m in range(C):
                    for c in range(C):
                        mm = pe.matmul(o_ps[:, m, :], wo[:, c, m * P:(m + 1) * P], at[:, c, :],
                                       start=c == 0, stop=c == C - 1)
                mm.then_inc(o_done, 1)

        @block.scalar
        def _(act):
            act.wait_ge(weights, 64)
            act.sem_inc(av_copied, 1)
            act.sem_inc(t_copied, 1)
            with act.Fori(0, B) as b:
                act.wait_ge(q_done, b + 1)
                for m in range(C):
                    last = act.activation(q_sb[:, m, :], head_ps[:, m, :], ACT.Identity, bias=bq[:, m:m + 1])
                last.then_inc(q_copied, 1)
                for q in range(2):
                    act.wait_ge(shifted, 2 * b + q + 1)
                    act.activation(e0[q][:, :], mx[q][:, :], ACT.Exp, scale=-scale)
                    act.activation(e_sb[q][:, :, :], e_sb[q][:, :, :], ACT.Exp, scale=scale).then_inc(exped, 1)
                for q in range(2):
                    act.wait_ge(t_done, 2 * b + q + 1)
                    act.activation(pt[:, :, q * P:(q + 1) * P], pt_ps[:, :, :], ACT.Copy).then_inc(t_copied, 1)
                act.wait_ge(av_done, b + 2)
                act.activation(at[:, :, :], head_ps[:, :, :], ACT.Copy).then_inc(av_copied, 1)

        @block.vector
        def _(dve):
            dve.wait_ge(weights, 64)
            dve.sem_inc(added, 1)
            steps = 2 * 2 + 2 * 3
            with dve.Fori(0, B) as b:
                step = Chain(dve, step_sem, b * steps)
                for q in range(2):
                    dve.wait_ge(s_done, 2 * b + q + 1)
                    step(dve.tensor_reduce(mx[q][:, :], s_ps[q][:, :, :], AX.X, ALU.max))
                    step(dve.tensor_scalar(mx[q][:, :], mx[q][:, :], 0.0, None, ALU.max))
                    dve.tensor_tensor(e_sb[q][:, :, :], s_ps[q][:, :, :], bc(mx[q][:, :], 2, [P, H0, SLOTS]),
                                      ALU.subtract).then_inc(shifted, 1)
                for q in range(2):
                    dve.wait_ge(exped, 2 * b + q + 1)
                    step(dve.tensor_reduce(den[q][:, :], e_sb[q][:, :, :], AX.X, ALU.add))
                    step(dve.scalar_tensor_tensor(den[q][:, :], e0[q][:, :], float(S - SLOTS), den[q][:, :],
                                                  ALU.mult, ALU.add))
                    step(dve.reciprocal(den[q][:, :], den[q][:, :]))
                    dve.tensor_tensor(e_sb[q][:, :, :], e_sb[q][:, :, :], bc(den[q][:, :], 2, [P, H0, SLOTS]),
                                      ALU.mult).then_inc(p_ready, 1)
                assert step.n == steps
                dve.wait_ge(o_done, b + 1)
                for m in range(C):
                    x = g.xt[:, m, bass.ts(b, S)]
                    last = dve.scalar_tensor_tensor(x, o_ps[:, m, :], bo[:, m:m + 1], x, ALU.add, ALU.add)
                last.then_inc(added, 1)


def wkv(nc, g, a):
    FAR = -1e38
    BP = 4
    PIECES = C * (B // BP)
    with ExitStack() as ctx:
        def sb(name, shape, dt=F32):
            return ctx.enter_context(nc.sbuf_tensor("w_" + name, shape, dt))

        def sem(name):
            return ctx.enter_context(nc.semaphore("w_" + name))

        decay = sb("decay", [P, C])
        first = sb("first", [P, C])
        w_dec = sb("w_dec", [P, C])
        w_row = sb("w_row", [P, C, BP, S])
        names = ("pp", "prev", "eb", "kb", "kv", "aa", "bb", "e1", "e2", "num")
        buf = {n: [sb(f"{n}{i}", [P, BP, S]) for i in range(2)] for n in names}

        loaded, w_ready, row_ready = sem("loaded"), sem("w_ready"), sem("row_ready")
        pp_done, prev_ready, diffs, exps_a, kv_ready, scanned, yexp, done, step_sem, kb_sub, e2v = (
            sem(n) for n in ("pp_done", "prev_ready", "diffs", "exps_a", "kv_ready", "scanned", "yexp", "done", "step",
                             "kb_sub", "e2v"))

        def piece(n):
            c, h = n // (B // BP), n % (B // BP)
            sl = slice(h * BP * S, (h + 1) * BP * S)
            k = g.xt[:, c, sl].rearrange("p (b s) -> p b s", b=BP)
            v = g.aux[:, c, sl].rearrange("p (b s) -> p b s", b=BP)
            return c, k, v

        def flat(x):
            return x[:, :, :].rearrange("p b s -> p (b s)")

        block = ctx.enter_context(nc.Block())

        @block.sync
        def _(sp):
            sp.dma_start(decay[:, :], a["decay"]).then_inc(loaded, 16)
            sp.dma_start(first[:, :], a["first"]).then_inc(loaded, 16)
            sp.dma_start(g.aux[:, :, :], a["ct"]).then_inc(loaded, 16)

        @block.scalar
        def _(act):
            act.wait_ge(loaded, 48)
            act.activation(w_dec[:, :], decay[:, :], ACT.Exp).then_inc(w_ready, 1)
            def early(n):
                i = n % 2
                c, k, v = piece(n)
                act.wait_ge(pp_done, n + 1)
                if n >= 2:
                    act.wait_ge(done, n - 1)
                act.activation(buf["prev"][i][:, :, 1:S], buf["pp"][i][:, :, 0:S - 1], ACT.Copy).then_inc(prev_ready, 1)
                act.wait_ge(diffs, n + 1)
                act.activation(buf["eb"][i][:, :, :], buf["eb"][i][:, :, :], ACT.Exp, bias=w_dec[:, c:c + 1])
                act.wait_ge(kb_sub, n + 1)
                act.activation(buf["kb"][i][:, :, :], buf["kb"][i][:, :, :], ACT.Exp).then_inc(exps_a, 1)
                act.activation(buf["e2"][i][:, :, :], buf["e2"][i][:, :, :], ACT.Exp)
                act.activation(buf["e1"][i][:, :, :], buf["e1"][i][:, :, :], ACT.Exp, scale=-1.0).then_inc(yexp, 1)
            for n in range(PIECES):
                early(n)

        @block.gpsimd
        def _(pool):
            for i in range(2):
                pool.memset(buf["prev"][i][:, :, 0:1], FAR).then_inc(prev_ready, 1)
            pool.memset(w_row[:, :, :, :], 0.0).then_inc(row_ready, 1)
            for n in range(PIECES):
                i = n % 2
                c, k, v = piece(n)
                pool.wait_ge(pp_done, n + 1)
                if n >= 2:
                    pool.wait_ge(done, n - 1)
                pool.tensor_tensor(buf["kb"][i][:, :, :], k, buf["pp"][i][:, :, :], ALU.subtract).then_inc(kb_sub, 1)
                pool.wait_ge(exps_a, n + 1)
                pool.tensor_tensor(buf["kv"][i][:, :, :], buf["kb"][i][:, :, :], v, ALU.mult).then_inc(kv_ready, 1)
                pool.wait_ge(yexp, n + 1)
                pool.tensor_tensor(buf["num"][i][:, :, :], buf["e2"][i][:, :, :], v, ALU.mult).then_inc(e2v, 1)

        @block.vector
        def _(dve):
            step = Chain(dve, step_sem)
            dve.wait_ge(w_ready, 1)
            step(dve.tensor_scalar(w_dec[:, :], w_dec[:, :], -1.0, None, ALU.mult))
            dve.wait_ge(row_ready, 1)
            for c in range(C):
                last = dve.tensor_scalar(w_row[:, c, :, :], w_row[:, c, :, :], w_dec[:, c:c + 1], None, ALU.add)
            step(last)
            step(dve.memset(w_row[:, :, :, 0:1], 3 * FAR))
            dve.wait_ge(prev_ready, 2)

            def front(n):
                i = n % 2
                c, k, v = piece(n)
                if n >= 2:
                    dve.wait_ge(kb_sub, n - 1)
                    dve.wait_ge(prev_ready, 2 + n - 1)
                    dve.wait_ge(diffs, n - 1)
                dve.tensor_tensor_scan(flat(buf["pp"][i]), w_row[:, c, :, :].rearrange("p b s -> p (b s)"),
                                       k.rearrange("p b s -> p (b s)"), FAR, ALU.add, ALU.max).then_inc(pp_done, 1)

            def middle(n):
                i = n % 2
                c, k, v = piece(n)
                dve.wait_ge(prev_ready, 2 + n + 1)
                dve.wait_ge(pp_done, n + 1)
                if n >= 2:
                    dve.wait_ge(done, n - 1)
                prev = buf["prev"][i][:, :, :]
                step(dve.scalar_tensor_tensor(flat(buf["e1"][i]), k.rearrange("p b s -> p (b s)"), first[:, c:c + 1],
                                              flat(buf["prev"][i]), ALU.add, ALU.subtract))
                step(dve.tensor_scalar(flat(buf["e2"][i]), flat(buf["e1"][i]), 0.0, None, ALU.min))
                dve.tensor_scalar(flat(buf["e1"][i]), flat(buf["e1"][i]), 0.0, None, ALU.max)
                dve.tensor_tensor(buf["eb"][i][:, :, :], prev, buf["pp"][i][:, :, :], ALU.subtract).then_inc(diffs, 1)

            def scans(n):
                i = n % 2
                dve.wait_ge(exps_a, n + 1)
                dve.tensor_tensor_scan(flat(buf["bb"][i]), flat(buf["eb"][i]), flat(buf["kb"][i]), 0.0, ALU.mult, ALU.add)
                dve.wait_ge(kv_ready, n + 1)
                step(dve.tensor_tensor_scan(flat(buf["aa"][i]), flat(buf["eb"][i]), flat(buf["kv"][i]), 0.0,
                                            ALU.mult, ALU.add))

            def back(n):
                i = n % 2
                c, k, v = piece(n)
                e1, e2, aa, bb, num = (buf[x][i] for x in ("e1", "e2", "aa", "bb", "num"))
                dve.wait_ge(yexp, n + 1)
                t1, t2 = buf["kb"][i], buf["kv"][i]
                dve.tensor_tensor(t1[:, :, 1:S], e1[:, :, 1:S], aa[:, :, 0:S - 1], ALU.mult)
                dve.tensor_tensor(t2[:, :, 1:S], e1[:, :, 1:S], bb[:, :, 0:S - 1], ALU.mult)
                dve.memset(t1[:, :, 0:1], 0.0)
                step(dve.memset(t2[:, :, 0:1], 0.0))
                dve.wait_ge(e2v, n + 1)
                dve.tensor_tensor(t1[:, :, :], t1[:, :, :], num[:, :, :], ALU.add)
                step(dve.tensor_tensor(t2[:, :, :], t2[:, :, :], e2[:, :, :], ALU.add))
                step(dve.reciprocal(flat(t2), flat(t2)))
                step(dve.tensor_tensor(flat(t1), flat(t1), flat(t2), ALU.mult))
                dve.tensor_tensor(k, k, t1[:, :, :], ALU.add).then_inc(done, 1)

            front(0)
            middle(0)
            for n in range(PIECES):
                if n + 1 < PIECES:
                    front(n + 1)
                scans(n)
                if n + 1 < PIECES:
                    middle(n + 1)
                back(n)


def route(nc, g, a):
    NTOK = T // P
    E = E_ROUTED
    with ExitStack() as ctx:
        def sb(name, shape, dt=F32):
            return ctx.enter_context(nc.sbuf_tensor("r_" + name, shape, dt))

        def sem(name):
            return ctx.enter_context(nc.semaphore("r_" + name))

        wg = sb("wg", [P, C, E])
        lt = sb("lt", [E, T])
        p = sb("p", [P, NTOK, E])
        big = [sb(f"big{i}", [P, NTOK, E, E]) for i in range(2)]
        m = sb("m", [P, NTOK])
        rank = sb("rank", [P, NTOK, E])
        ct = sb("ct", [E, T])
        logit_ps = ctx.enter_context(nc.psum_tensor("r_logit", [E, T], F32))
        tok_ps = ctx.enter_context(nc.psum_tensor("r_tok", [P, NTOK, E], F32))
        loaded, logits, copied, turned, shifted, exped, ready, back, ct_ready, stored, step_sem = (
            sem(n) for n in ("loaded", "logits", "copied", "turned", "shifted", "exped", "ready", "back", "ct_ready",
                             "stored", "step"))
        block = ctx.enter_context(nc.Block())

        @block.sync
        def _(sp):
            sp.dma_start(wg[:, :, :], a["gate"]).then_inc(loaded, 16)
            sp.dma_start(g.combine_dram[E:E + 1, :], a["one_row"]).then_inc(stored, 16)
            sp.wait_ge(ct_ready, NT)
            sp.dma_start(g.combine_dram[0:E, :], ct[:, :]).then_inc(stored, 16)
            sp.wait_ge(stored, 32)

        @block.tensor
        def _(pe):
            pe.wait_ge(loaded, 16)
            for t in range(NT):
                for c in range(C):
                    mm = pe.matmul(logit_ps[:, t * TT:(t + 1) * TT], wg[:, c, :], g.xt[:, c, t * TT:(t + 1) * TT],
                                   start=c == 0, stop=c == C - 1)
                mm.then_inc(logits, 1)
            pe.wait_ge(copied, NT)
            for n in range(NTOK):
                mm = pe.transpose(tok_ps[:, n, :], lt[:, n * P:(n + 1) * P], g.const("ident")[0:E, 0:E])
            mm.then_inc(turned, 1)
            pe.wait_ge(ready, 1)
            for n in range(NTOK):
                mm = pe.transpose(logit_ps[:, n * P:(n + 1) * P], p[:, n, :], g.const("ident"))
                if n % 4 == 3:
                    mm.then_inc(back, 1)

        @block.scalar
        def _(act):
            for t in range(NT):
                act.wait_ge(logits, t + 1)
                act.activation(lt[:, t * TT:(t + 1) * TT], logit_ps[:, t * TT:(t + 1) * TT], ACT.Copy).then_inc(copied, 1)
            act.wait_ge(shifted, 1)
            act.activation(p[:, :, :], p[:, :, :], ACT.Exp).then_inc(exped, 1)
            for t in range(NT):
                act.wait_ge(back, t + 1)
                act.activation(ct[:, t * TT:(t + 1) * TT], logit_ps[:, t * TT:(t + 1) * TT], ACT.Copy).then_inc(ct_ready, 1)

        @block.vector
        def _(dve):
            step = Chain(dve, step_sem)
            full, small = [P, NTOK, E, E], [P, NTOK, E]
            dve.wait_ge(turned, 1)
            step(dve.tensor_reduce(m[:, :], tok_ps[:, :, :], AX.X, ALU.max))
            dve.tensor_tensor(p[:, :, :], tok_ps[:, :, :], bc(m[:, :], 2, small), ALU.subtract).then_inc(shifted, 1)
            dve.wait_ge(exped, 1)
            step(dve.tensor_reduce(m[:, :], p[:, :, :], AX.X, ALU.add))
            step(dve.reciprocal(m[:, :], m[:, :]))
            step(dve.tensor_tensor(p[:, :, :], p[:, :, :], bc(m[:, :], 2, small), ALU.mult))
            other, mine = bc(p[:, :, :], 2, full), bc(p[:, :, :], 3, full)
            dve.tensor_tensor(big[0][:, :, :, :], other, mine, ALU.is_gt)
            step(dve.tensor_tensor(big[1][:, :, :, :], other, mine, ALU.is_equal))
            step(dve.tensor_tensor(big[1][:, :, :, :].rearrange("p n e f -> p n (e f)"),
                                   big[1][:, :, :, :].rearrange("p n e f -> p n (e f)"),
                                   bc(g.const("expert_lt"), 1, [P, NTOK, E * E]), ALU.mult))
            step(dve.tensor_tensor(big[0][:, :, :, :], big[0][:, :, :, :], big[1][:, :, :, :], ALU.add))
            step(dve.tensor_reduce(rank[:, :, :], big[0][:, :, :, :], AX.X, ALU.add))
            step(dve.tensor_scalar(rank[:, :, :], rank[:, :, :], TOP_K - 0.5, None, ALU.is_lt))
            step(dve.tensor_tensor(p[:, :, :], p[:, :, :], rank[:, :, :], ALU.mult))
            step(dve.tensor_reduce(m[:, :], p[:, :, :], AX.X, ALU.add))
            step(dve.reciprocal(m[:, :], m[:, :]))
            dve.tensor_tensor(p[:, :, :], p[:, :, :], bc(m[:, :], 2, small), ALU.mult).then_inc(ready, 1)


def decode_fp4(dve, step, g, raw, tmp):
    step(dve.tensor_scalar(raw, raw, g.shift[:, 0:1], None, ALU.logical_shift_left))
    step(dve.tensor_scalar(tmp, raw, g.shift[:, 1:2], g.shift[:, 2:3], ALU.logical_shift_right, ALU.bitwise_and))
    step(dve.scalar_tensor_tensor(raw, raw, g.shift[:, 3:4], tmp, ALU.bitwise_and, ALU.bitwise_or))


FP8_GAIN = 64.0


def experts(nc, g, a):
    N_GU, N_D = 2 * I_MOE, D
    with ExitStack() as ctx:
        def sb(name, shape, dt=F32):
            return [ctx.enter_context(nc.sbuf_tensor(f"x_{name}{i}", shape, dt)) for i in range(2)]

        def sem(name):
            return ctx.enter_context(nc.semaphore("x_" + name))

        def ps(name, shape):
            return ctx.enter_context(nc.psum_tensor("x_" + name, shape, F32))

        raw_gu, raw_d = sb("raw_gu", [P, G_D, N_GU // 4], I32), sb("raw_d", [P, G_I, N_D // 4], I32)
        sc_gu, sc_d = sb("sc_gu", [P, G_D, N_GU]), sb("sc_d", [P, G_I, N_D])
        cmb = sb("cmb", [P, T])
        w_gu, w_d = sb("w_gu", [P, G_D, N_GU]), sb("w_d", [P, G_I, N_D])
        tmp = ctx.enter_context(nc.sbuf_tensor("x_tmp", [P, G_D, N_GU // 4], I32))
        mark = ctx.enter_context(nc.sbuf_tensor("x_mark", [P, 1], I32))
        silu = sb("silu", [P, TT])
        h = sb("h", [P, G_I, TT])
        gate_ps = [ps(f"gate{i}", [P, TT]) for i in range(2)]
        up_ps = [ps(f"up{i}", [P, TT]) for i in range(2)]
        y_ps = ps("y", [P, C, TT])
        landed = [sem(f"landed{i}") for i in range(2)]
        cmb_landed = [sem(f"cmb_landed{i}") for i in range(2)]
        raw_free, cmb_free, w_ready, gu_done, silu_done, hu_done, h_ready, y_done, y_added, step_sem, acc_ready = (
            sem(n) for n in ("raw_free", "cmb_free", "w_ready", "gu_done", "silu_done", "hu_done", "h_ready",
                             "y_done", "y_added", "step", "acc_ready"))
        DMAS = 6
        block = ctx.enter_context(nc.Block())

        def each_expert(eng, body):
            with eng.Fori(0, E_ROUTED // 2) as i:
                for u in range(2):
                    body(2 * i + u, u, i)
            body(E_ROUTED, 0, E_ROUTED // 2)

        def tile_of(e, t):
            return e * NT + t

        def bank(t, n):
            return (t * G_I + n) % 2

        @block.sync
        def _(sp):
            def load(e, u, i):
                sp.wait_ge(raw_free, e + 1)
                for half in range(2):
                    r = slice(64 * half, 64 * half + 64)
                    sp.dma_start(raw_gu[u][r, :, :], a["gu"][bass.ds(e, 1)].rearrange("o r g n -> (o r) g n"))\
                      .then_inc(landed[u], 16)
                    sp.dma_start(raw_d[u][r, :, :], a["d"][bass.ds(e, 1)].rearrange("o r g n -> (o r) g n"))\
                      .then_inc(landed[u], 16)
                sp.dma_start(sc_gu[u][:, :, :].rearrange("p g n -> p (g n)"),
                             a["gu_s"][bass.ds(e, 1), :].to_broadcast([P, G_D * N_GU])).then_inc(landed[u], 16)
                sp.dma_start(sc_d[u][:, :, :].rearrange("p g n -> p (g n)"),
                             a["d_s"][bass.ds(e, 1), :].to_broadcast([P, G_I * N_D])).then_inc(landed[u], 16)
                sp.wait_ge(cmb_free, e + 1)
                sp.dma_start(cmb[u][:, :], g.combine_dram[bass.ds(e, 1), :].to_broadcast([P, T]))\
                  .then_inc(cmb_landed[u], 16)

            each_expert(sp, load)

        @block.tensor
        def _(pe):
            def expert(e, u, i):
                pe.wait_ge(w_ready, e + 1)

                def gate_up(t):
                    for n in range(G_I):
                        pe.wait_ge(hu_done, tile_of(e, t) * G_I + n + 1)
                        k = bank(t, n)
                        for out, off in ((gate_ps[k], 0), (up_ps[k], I_MOE)):
                            for c in range(C):
                                mm = pe.matmul(out[:, :], w_gu[u][:, c, off + n * P:off + (n + 1) * P],
                                               g.xt[:, c, t * TT:(t + 1) * TT], start=c == 0, stop=c == C - 1)
                        mm.then_inc(gu_done, 1)

                def down(t):
                    pe.wait_ge(h_ready, tile_of(e, t) * G_I + G_I)
                    pe.wait_ge(y_added, tile_of(e, t) + 1)
                    for n in range(C):
                        for c in range(G_I):
                            mm = pe.matmul(y_ps[:, n, :], w_d[u][:, c, n * P:(n + 1) * P], h[t % 2][:, c, :],
                                           start=c == 0, stop=c == G_I - 1)
                    mm.then_inc(y_done, 1)

                gate_up(0)
                for t in range(NT):
                    if t + 1 < NT:
                        gate_up(t + 1)
                    down(t)

            each_expert(pe, expert)

        @block.scalar
        def _(act):
            act.activation(g.aux[:, :, :], g.xt[:, :, :], ACT.Copy).then_inc(acc_ready, 1)

            def expert(e, u, i):
                for t in range(NT):
                    for n in range(G_I):
                        k = bank(t, n)
                        act.wait_ge(gu_done, tile_of(e, t) * G_I + n + 1)
                        act.wait_ge(hu_done, tile_of(e, t) * G_I + n + 1)
                        act.activation(silu[k][:, :], gate_ps[k][:, :], ACT.Silu).then_inc(silu_done, 1)

            each_expert(act, expert)

        @block.gpsimd
        def _(pool):
            pool.sem_inc(cmb_free, 2)

            def expert(e, u, i):
                pool.wait_ge(cmb_landed[u], 16 * i + 16)
                for t in range(NT):
                    for n in range(G_I):
                        pool.wait_ge(hu_done, tile_of(e, t) * G_I + n + 3)
                        x = h[t % 2][:, n, :]
                        last = pool.tensor_tensor(x, x, cmb[u][:, t * TT:(t + 1) * TT], ALU.mult)
                        last.then_inc(h_ready, 1)
                pool.wait_ge(h_ready, (e + 1) * NT * G_I)
                pool.sem_inc(cmb_free, 1)

            each_expert(pool, expert)

        @block.vector
        def _(dve):
            dve.sem_inc(raw_free, 2)
            dve.sem_inc(hu_done, 2)
            dve.sem_inc(y_added, 1)
            steps = 6

            def dequantize(e, u, i):
                step = Chain(dve, step_sem, e * steps)
                dve.wait_ge(landed[u], 16 * DMAS * i + 16 * DMAS)
                decode_fp4(dve, step, g, raw_gu[u][:, :, :], tmp[:, :, :])
                decode_fp4(dve, step, g, raw_d[u][:, :, :], tmp[:, 0:G_I, 0:N_D // 4])
                assert step.n == steps
                dve.tensor_copy(mark[:, :], raw_d[u][:, 0, 0:1])
                dve.scalar_tensor_tensor(w_gu[u][:, :, :], raw_gu[u][:, :, :].bitcast(F8), FP8_GAIN, sc_gu[u][:, :, :],
                                         ALU.mult, ALU.mult)
                dve.scalar_tensor_tensor(w_d[u][:, :, :], raw_d[u][:, :, :].bitcast(F8), FP8_GAIN, sc_d[u][:, :, :],
                                         ALU.mult, ALU.mult).then_inc(w_ready, 1)
                dve.wait_ge(w_ready, e + 1)
                dve.sem_inc(raw_free, 1)

            def products(e, t):
                for n in range(G_I):
                    k = bank(t, n)
                    dve.wait_ge(silu_done, tile_of(e, t) * G_I + n + 1)
                    dve.tensor_tensor(h[t % 2][:, n, :], silu[k][:, :], up_ps[k][:, :], ALU.mult).then_inc(hu_done, 1)

            def add(e, t):
                dve.wait_ge(y_done, tile_of(e, t) + 1)
                dve.wait_ge(y_added, tile_of(e, t) + 1)
                acc = g.aux[:, :, t * TT:(t + 1) * TT]
                dve.tensor_tensor(acc, acc, y_ps[:, :, :], ALU.add).then_inc(y_added, 1)

            def expert(e, u, i):
                for t in range(NT):
                    products(e, t)
                    if t >= 1:
                        add(e, t - 1)
                    if t == 1 and not (isinstance(e, int) and e == E_ROUTED):
                        dequantize(e + 1, 1 - u, i + u)
                add(e, NT - 1)

            dve.wait_ge(acc_ready, 1)
            dequantize(0, 0, 0)
            each_expert(dve, expert)


LAG = 3
RING = 4


def causal_attention(nc, g, a):
    with ExitStack() as ctx:
        def sb(name, shape, dt=F32):
            return ctx.enter_context(nc.sbuf_tensor("c_" + name, shape, dt))

        def sem(name):
            return ctx.enter_context(nc.semaphore("c_" + name))

        def ps(name, shape):
            return ctx.enter_context(nc.psum_tensor("c_" + name, shape, F32))

        w = {n: sb(n, [P, C, D]) for n in ("wq", "wqr", "wk", "wkr", "wv", "wo")}
        bias = {n: sb(n, [P, C]) for n in ("bq", "bqr", "bk", "bkr", "bo")}
        bv = sb("bv", [P, D])
        xb = sb("xb", [P, C, S])
        q_sb, k_sb = sb("q", [P, C, S]), sb("k", [P, C, S])
        sq, sk = sb("sq", [P, C, S]), sb("sk", [P, C, S])
        nrm = sb("nrm", [P, 2, S])
        kp = [sb(f"kp{j}", [P, C, S]) for j in range(4)]
        v_sb = sb("v", [P, 2, D])
        pt = [sb(f"pt{i}", [P, 3, P]) for i in range(RING)]
        rec = sb("rec", [P, C, S])
        at = sb("at", [P, C, S])
        q_ps, k_ps = ps("q_ps", [P, C, S]), ps("k_ps", [P, C, S])
        v_ps = ps("v_ps", [P, 2, D])
        s_ps = [ps(f"s{i}", [P, 3, P]) for i in range(2)]
        n_ps = v_ps[:, 0, :].rearrange("p (n s) -> p n s", n=2)
        o_ps = v_ps[:, :, :].rearrange("p a (b s) -> p (a b) s", b=2)
        (loaded, folded, xb_ready, q_done, k_done, v_done, sq_ready, v_ready, n_done, n_root, qk_ready, s_done, exped,
         masked, av_done, at_ready, o_done, added, step_sem) = (
            sem(n) for n in ("loaded", "folded", "xb_ready", "q_done", "k_done", "v_done", "sq_ready", "v_ready",
                             "n_done", "n_root", "qk_ready", "s_done", "exped", "masked", "av_done", "at_ready",
                             "o_done", "added", "step"))
        LOADS = 12
        block = ctx.enter_context(nc.Block())

        @block.sync
        def _(sp):
            for n in w:
                sp.dma_start(w[n][:, :, :], a[n + "1"]).then_inc(loaded, 16)
            for n in bias:
                sp.dma_start(bias[n][:, :], a[n + "1"]).then_inc(loaded, 16)
            sp.dma_start(bv[:, :], a["bv1"].to_broadcast([P, D])).then_inc(loaded, 16)

        @block.gpsimd
        def _(pool):
            pool.wait_ge(loaded, 16 * LOADS)
            with pool.Fori(0, B) as b:
                pool.wait_ge(v_done, b + 1)
                pool.tensor_copy(xb[:, :, :], g.xt[:, :, bass.ts(b, S)]).then_inc(xb_ready, 1)
                for h in range(H1):
                    pool.wait_ge(exped, H1 * b + h + 3)
                    diagonal = pt[h % RING][:, 0:3:2, :]
                    pool.tensor_tensor(diagonal, diagonal, bc(g.const("causal"), 1, [P, 2, P]), ALU.mult)\
                        .then_inc(masked, 1)

        @block.tensor
        def _(pe):
            pe.wait_ge(folded, 1)
            pe.sem_inc(v_done, 1)
            pe.sem_inc(n_done, 1)
            with pe.Fori(0, B) as b:
                pe.wait_ge(xb_ready, b + 1)
                pe.wait_ge(at_ready, b + 1)
                for x, y, done in (("wq", q_ps, q_done), ("wk", k_ps, k_done)):
                    for m in range(C):
                        for c in range(C):
                            mm = pe.matmul(y[:, m, :], w[x][:, c, m * P:(m + 1) * P], xb[:, c, :],
                                           start=c == 0, stop=c == C - 1)
                    mm.then_inc(done, 1)
                pe.wait_ge(added, b + 1)
                for k in range(2):
                    for c in range(C):
                        mm = pe.matmul(v_ps[:, k, :], xb[:, c, k * P:(k + 1) * P], w["wv"][:, c, :],
                                       start=c == 0, stop=c == C - 1)
                mm.then_inc(v_done, 1)
                pe.wait_ge(v_ready, b + 1)
                for n, x in enumerate((sq, sk)):
                    pe.wait_ge(sq_ready, 2 * b + n + 1)
                    for c in range(C):
                        mm = pe.matmul(n_ps[:, n, :], g.const("ones"), x[:, c, :], start=c == 0, stop=c == C - 1)
                mm.then_inc(n_done, 1)

                def score(h):
                    c, j = h // 4, h % 4
                    pe.wait_ge(exped, H1 * b + h + 1)
                    pe.matmul(s_ps[h % 2][:, 0:2, :], kp[j][:, c, 0:P], q_sb[:, c, :], start=True, stop=True)
                    pe.matmul(s_ps[h % 2][:, 2, :], kp[j][:, c, P:S], q_sb[:, c, P:S], start=True, stop=True)\
                      .then_inc(s_done, 1)

                def value(h):
                    c, j = h // 4, h % 4
                    r = slice(32 * j, 32 * j + 32)
                    x = pt[h % RING]
                    pe.wait_ge(masked, H1 * b + h + 1)
                    for y, w0, w1 in ((q_ps, v_sb[:, 0, h * HD1:(h + 1) * HD1], v_sb[:, 1, h * HD1:(h + 1) * HD1]),
                                      (k_ps, g.const("ones")[:, 0:32], g.const("ones")[:, 0:32])):
                        pe.matmul(y[r, c, :], w0, x[:, 0:2, :], start=True, stop=False)
                        mm = pe.matmul(y[r, c, P:S], w1, x[:, 2, :], start=False, stop=True)
                    mm.then_inc(av_done, 1)

                pe.wait_ge(qk_ready, b + 1)
                for h in range(H1 + LAG):
                    if h < H1:
                        score(h)
                    if h >= LAG:
                        value(h - LAG)
                pe.wait_ge(at_ready, b + 2)
                for m in range(C):
                    for c in range(C):
                        mm = pe.matmul(o_ps[:, m, :], w["wo"][:, c, m * P:(m + 1) * P], at[:, c, :],
                                       start=c == 0, stop=c == C - 1)
                mm.then_inc(o_done, 1)

        @block.scalar
        def _(act):
            act.wait_ge(folded, 1)
            act.sem_inc(exped, 2)
            with act.Fori(0, B) as b:
                for y, x, s2, bn, done, k in ((q_ps, q_sb, sq, "bq", q_done, 0), (k_ps, k_sb, sk, "bk", k_done, 1)):
                    act.wait_ge(done, b + 1)
                    act.wait_ge(n_done, b + 1)
                    for m in range(C):
                        act.activation(s2[:, m, :], y[:, m, :], ACT.Square, bias=bias[bn][:, m:m + 1])
                        last = act.activation(x[:, m, :], y[:, m, :], ACT.Identity, bias=bias[bn][:, m:m + 1])
                    last.then_inc(sq_ready, 1)
                act.wait_ge(n_done, b + 2)
                act.activation(nrm[:, :, :], n_ps, ACT.Sqrt).then_inc(n_root, 1)
                for h in range(H1):
                    act.wait_ge(s_done, H1 * b + h + 1)
                    act.wait_ge(av_done, H1 * b + h + 1)
                    act.activation(pt[h % RING][:, :, :], s_ps[h % 2][:, :, :], ACT.Exp).then_inc(exped, 1)

        @block.vector
        def _(dve):
            dve.sem_inc(av_done, RING)
            dve.sem_inc(at_ready, 1)
            dve.sem_inc(added, 1)
            dve.wait_ge(loaded, 16 * LOADS)
            cos, sin = (bc(g.const(n), 1, [P, C, D]) for n in ("cos", "sin"))
            fold = 3
            base = 2 * fold
            step = Chain(dve, step_sem)
            for x in ("q", "k"):
                wx, wr, bx, br = w["w" + x][:, :, :], w["w" + x + "r"][:, :, :], bias["b" + x][:, :], bias["b" + x + "r"][:, :]
                dve.tensor_tensor(wx, wx, cos, ALU.mult)
                dve.tensor_tensor(bx, bx, g.const("cosc"), ALU.mult)
                dve.tensor_tensor(br, br, g.const("sinc"), ALU.mult)
                step(dve.tensor_tensor(wr, wr, sin, ALU.mult))
                dve.tensor_tensor(wx, wx, wr, ALU.add)
                step(dve.tensor_tensor(bx, bx, br, ALU.add))
            dve.sem_inc(folded, 1)
            base = step.n
            steps = 5
            with dve.Fori(0, B) as b:
                step = Chain(dve, step_sem, b * steps + base)
                dve.wait_ge(v_done, b + 2)
                dve.tensor_tensor(v_sb[:, :, :], v_ps[:, :, :], bc(bv[:, :], 1, [P, 2, D]), ALU.add).then_inc(v_ready, 1)
                dve.wait_ge(n_root, b + 1)
                step(dve.tensor_scalar(nrm[:, :, :], nrm[:, :, :], 1e-12, None, ALU.max))
                step(dve.reciprocal(nrm[:, :, :], nrm[:, :, :]))
                dve.tensor_tensor(q_sb[:, :, :], q_sb[:, :, :], bc(nrm[:, 0, :], 1, [P, C, S]), ALU.mult)
                for j in range(4):
                    last = dve.scalar_tensor_tensor(kp[j][:, :, :], k_sb[:, :, :], g.const("head4")[:, j:j + 1],
                                                    bc(nrm[:, 1, :], 1, [P, C, S]), ALU.mult, ALU.mult)
                step(last)
                dve.sem_inc(qk_ready, 1)
                dve.wait_ge(av_done, H1 * b + H1 + RING)
                step(dve.reciprocal(rec[:, :, :], k_ps[:, :, :]))
                step(dve.tensor_tensor(at[:, :, :], q_ps[:, :, :], rec[:, :, :], ALU.mult))
                dve.sem_inc(at_ready, 1)
                assert step.n == steps
                dve.wait_ge(o_done, b + 1)
                for m in range(C):
                    x = g.xt[:, m, bass.ts(b, S)]
                    last = dve.scalar_tensor_tensor(x, o_ps[:, m, :], bias["bo"][:, m:m + 1], x, ALU.add, ALU.add)
                last.then_inc(added, 1)


def cross_attention(nc, g, a):
    with ExitStack() as ctx:
        def sb(name, shape, dt=F32):
            return ctx.enter_context(nc.sbuf_tensor("y_" + name, shape, dt))

        def sem(name):
            return ctx.enter_context(nc.semaphore("y_" + name))

        def ps(name, shape):
            return ctx.enter_context(nc.psum_tensor("y_" + name, shape, F32))

        wq, wk, wv = (sb(n, [P, C, D]) for n in ("wq", "wk", "wv"))
        cb = sb("cb", [P, C, S])
        q_sb, k_sb = sb("q", [P, C, S]), sb("k", [P, C, S])
        sq, sk = sb("sq", [P, C, S]), sb("sk", [P, C, S])
        kp = [sb(f"kp{j}", [P, C, S]) for j in range(8)]
        vp = [sb(f"vp{j}", [P, 2, HX // 2, 2, HDX]) for j in range(2)]
        pt = [sb(f"pt{i}", [P, 2, S]) for i in range(RING)]
        at = sb("at", [P, C, S])
        q_ps, k_ps = ps("q_ps", [P, C, S]), ps("k_ps", [P, C, S])
        v_ps = ps("v_ps", [P, 2, D])
        s_ps = ps("s_ps", [P, 2, 2, S])
        nq_ps = v_ps[:, :, :].rearrange("p a (b s) -> p (a b) s", b=2)
        nk_ps = s_ps[:, :, :, :].rearrange("p a b s -> p (a b) s")
        o_ps = nq_ps
        (loaded, zeroed, cb_ready, q_done, k_done, v_done, sq_ready, v_ready, n_done, n_root, qk_ready, s_done, exped,
         av_done, at_ready, o_done, added, step_sem) = (
            sem(n) for n in ("loaded", "zeroed", "cb_ready", "q_done", "k_done", "v_done", "sq_ready", "v_ready",
                             "n_done", "n_root", "qk_ready", "s_done", "exped", "av_done", "at_ready",
                             "o_done", "added", "step"))
        eps = g.const("eps")[:, 1:2]
        block = ctx.enter_context(nc.Block())

        @block.sync
        def _(sp):
            for dst, src in ((wq[:, :, :], a["wqx"]), (wk[:, :, :], a["wkx"]), (wv[:, :, :], a["wvx"]), (g.aux[:, :, :], a["ct"])):
                sp.dma_start(dst, src).then_inc(loaded, 16)

        @block.gpsimd
        def _(pool):
            for j in range(2):
                pool.memset(vp[j][:, :, :, :, :], 0.0).then_inc(zeroed, 1)
            pool.wait_ge(loaded, 64)
            with pool.Fori(0, B) as b:
                pool.wait_ge(v_done, b + 1)
                pool.tensor_copy(cb[:, :, :], g.aux[:, :, bass.ts(b, S)]).then_inc(cb_ready, 1)

        @block.tensor
        def _(pe):
            pe.wait_ge(loaded, 64)
            pe.sem_inc(v_done, 1)
            with pe.Fori(0, B) as b:
                pe.wait_ge(at_ready, b + 1)
                for m in range(C):
                    for c in range(C):
                        mm = pe.matmul(q_ps[:, m, :], wq[:, c, m * P:(m + 1) * P], g.xt[:, c, bass.ts(b, S)],
                                       start=c == 0, stop=c == C - 1)
                mm.then_inc(q_done, 1)
                pe.wait_ge(cb_ready, b + 1)
                for m in range(C):
                    for c in range(C):
                        mm = pe.matmul(k_ps[:, m, :], wk[:, c, m * P:(m + 1) * P], cb[:, c, :],
                                       start=c == 0, stop=c == C - 1)
                mm.then_inc(k_done, 1)
                pe.wait_ge(added, b + 1)
                for k in range(2):
                    for c in range(C):
                        mm = pe.matmul(v_ps[:, k, :], cb[:, c, k * P:(k + 1) * P], wv[:, c, :],
                                       start=c == 0, stop=c == C - 1)
                mm.then_inc(v_done, 1)
                pe.wait_ge(v_ready, b + 1)
                pe.wait_ge(exped, HX * b + 2)
                for n, (x, y) in enumerate(((sq, nq_ps), (sk, nk_ps))):
                    pe.wait_ge(sq_ready, 2 * b + n + 1)
                    for c in range(C):
                        mm = pe.matmul(y[:, c, :], g.const("blk16"), x[:, c, :], start=True, stop=True)
                    mm.then_inc(n_done, 1)

                def score(h):
                    c, j = h // 8, h % 8
                    pe.wait_ge(exped, HX * b + h + 1)
                    for k in range(2):
                        mm = pe.matmul(s_ps[:, h % 2, k, :], kp[j][:, c, k * P:(k + 1) * P], q_sb[:, c, :],
                                       start=True, stop=True)
                    mm.then_inc(s_done, 1)

                def value(h):
                    pair, e = h // 2, h % 2
                    c, j = pair // 4, pair % 4
                    r = slice(32 * j, 32 * j + 32)
                    pe.wait_ge(exped, HX * b + h + 3)
                    for y, wt in ((q_ps, [vp[e][:, k, pair, :, :] for k in range(2)]),
                                  (k_ps, [g.const("den16")[:, 32 * e:32 * e + 32]] * 2)):
                        for k in range(2):
                            mm = pe.matmul(y[r, c, :], wt[k], pt[h % RING][:, k, :],
                                           start=e == 0 and k == 0, stop=e == 1 and k == 1, skip_group_check=True)
                    mm.then_inc(av_done, 1)

                pe.wait_ge(qk_ready, b + 1)
                for h in range(HX + LAG):
                    if h < HX:
                        score(h)
                    if h >= LAG:
                        value(h - LAG)
                pe.wait_ge(at_ready, b + 2)
                for m in range(C):
                    mm = pe.matmul(o_ps[:, m, :], g.const("perm"), at[:, m, :], start=True, stop=True)
                mm.then_inc(o_done, 1)

        @block.scalar
        def _(act):
            act.sem_inc(exped, 2)
            with act.Fori(0, B) as b:
                for y, x, s2, done in ((q_ps, q_sb, sq, q_done), (k_ps, k_sb, sk, k_done)):
                    act.wait_ge(done, b + 1)
                    act.activation(s2[:, :, :], y[:, :, :], ACT.Square)
                    act.activation(x[:, :, :], y[:, :, :], ACT.Copy).then_inc(sq_ready, 1)
                for n, (s2, y) in enumerate(((sq, nq_ps), (sk, nk_ps))):
                    act.wait_ge(n_done, 2 * b + n + 1)
                    act.activation(s2[:, :, :], y, ACT.Sqrt, bias=eps).then_inc(n_root, 1)
                for h in range(HX):
                    act.wait_ge(s_done, HX * b + h + 1)
                    act.wait_ge(av_done, HX * b + h + 1)
                    act.activation(pt[h % RING][:, :, :], s_ps[:, h % 2, :, :], ACT.Exp, scale=HDX ** -0.5)\
                       .then_inc(exped, 1)

        @block.vector
        def _(dve):
            dve.sem_inc(av_done, RING)
            dve.sem_inc(at_ready, 1)
            dve.sem_inc(added, 1)
            dve.wait_ge(zeroed, 2)
            steps = 7
            with dve.Fori(0, B) as b:
                step = Chain(dve, step_sem, b * steps)
                dve.wait_ge(v_done, b + 2)
                v = v_ps[:, :, :].rearrange("p k (n e d) -> p k n e d", e=2, d=HDX)
                for e in range(2):
                    last = dve.tensor_copy(vp[e][:, :, :, e, :], v[:, :, :, e, :])
                last.then_inc(v_ready, 1)
                for n, (x, s2) in enumerate(((q_sb, sq), (k_sb, sk))):
                    dve.wait_ge(n_root, 2 * b + n + 1)
                    step(dve.reciprocal(s2[:, :, :], s2[:, :, :]))
                    step(dve.tensor_tensor(x[:, :, :], x[:, :, :], s2[:, :, :], ALU.mult))
                for j in range(8):
                    last = dve.tensor_scalar(kp[j][:, :, :], k_sb[:, :, :], g.const("head8")[:, j:j + 1], None, ALU.mult)
                step(last)
                dve.sem_inc(qk_ready, 1)
                dve.wait_ge(av_done, HX * b + HX + RING)
                step(dve.reciprocal(sq[:, :, :], k_ps[:, :, :]))
                step(dve.tensor_tensor(at[:, :, :], q_ps[:, :, :], sq[:, :, :], ALU.mult))
                dve.sem_inc(at_ready, 1)
                assert step.n == steps
                dve.wait_ge(o_done, b + 1)
                x = g.xt[:, :, bass.ts(b, S)]
                dve.tensor_tensor(x, o_ps, x, ALU.add).then_inc(added, 1)


def feed_forward(nc, g, a):
    N_GU = 2 * I_FFN
    PIECE = 2816
    N_PIECES_GU, N_PIECES = C * N_GU // PIECE, (C * N_GU + G_F * D) // PIECE
    assert C * N_GU % PIECE == 0 and G_F * D % PIECE == 0
    with ExitStack() as ctx:
        def sb(name, shape, dt=F32):
            return ctx.enter_context(nc.sbuf_tensor("f_" + name, shape, dt))

        def sem(name):
            return ctx.enter_context(nc.semaphore("f_" + name))

        def ps(name, shape):
            return ctx.enter_context(nc.psum_tensor("f_" + name, shape, F32))

        w_gu, w_d = sb("w_gu", [P, C, N_GU]), sb("w_d", [P, G_F, D])
        raw = [sb(f"raw{i}", [P, PIECE // 4], I32) for i in range(2)]
        tmp = sb("tmp", [P, PIECE // 4], I32)
        sc = [sb(f"sc{i}", [P, PIECE], F16) for i in range(2)]
        silu = [sb(f"silu{i}", [P, TT]) for i in range(2)]
        h = [sb(f"h{i}", [P, TT]) for i in range(2)]
        gate_ps = [ps(f"gate{i}", [P, TT]) for i in range(2)]
        up_ps = [ps(f"up{i}", [P, TT]) for i in range(2)]
        y_ps = ps("y", [P, C, TT])
        landed = [sem(f"landed{i}") for i in range(2)]
        piece_ready, gu_done, silu_done, h_ready, h_used, y_copied, step_sem = (
            sem(n) for n in ("piece_ready", "gu_done", "silu_done", "h_ready", "h_used", "y_copied", "step"))
        block = ctx.enter_context(nc.Block())

        @block.sync
        def _(sp):
            for n in range(N_PIECES):
                if n >= 2:
                    sp.wait_ge(piece_ready, n - 1)
                cols = slice(n * PIECE // 4, (n + 1) * PIECE // 4)
                for half in range(2):
                    sp.dma_start(raw[n % 2][64 * half:64 * half + 64, :], a["ffn"][:, cols]).then_inc(landed[n % 2], 16)
                sp.dma_start(sc[n % 2][:, :], a["ffn_s"][:, n * PIECE:(n + 1) * PIECE].to_broadcast([P, PIECE]))\
                  .then_inc(landed[n % 2], 16)

        @block.tensor
        def _(pe):
            pe.wait_ge(piece_ready, N_PIECES)
            with pe.Fori(0, NT) as t:
                for n in range(G_F + 1):
                    if n < G_F:
                        pe.wait_ge(h_ready, t * G_F + max(n, 1) + 1)
                        for y, off in ((gate_ps[n % 2], 0), (up_ps[n % 2], I_FFN)):
                            for c in range(C):
                                mm = pe.matmul(y[:, :], w_gu[:, c, off + n * P:off + (n + 1) * P],
                                               g.xt[:, c, bass.ts(t, TT)], start=c == 0, stop=c == C - 1)
                        mm.then_inc(gu_done, 1)
                    if n >= 1:
                        m = n - 1
                        pe.wait_ge(h_ready, t * G_F + m + 3)
                        if m == 0:
                            pe.wait_ge(y_copied, t + 1)
                        for k in range(C):
                            mm = pe.matmul(y_ps[:, k, :], w_d[:, m, k * P:(k + 1) * P], h[m % 2][:, :],
                                           start=m == 0, stop=m == G_F - 1)
                        mm.then_inc(h_used, 1)

        @block.scalar
        def _(act):
            act.sem_inc(y_copied, 1)
            with act.Fori(0, NT) as t:
                for n in range(G_F):
                    k = n % 2
                    act.wait_ge(gu_done, t * G_F + n + 1)
                    act.wait_ge(h_ready, t * G_F + max(n, 1) + 1)
                    act.activation(silu[k][:, :], gate_ps[k][:, :], ACT.Silu).then_inc(silu_done, 1)
                act.wait_ge(h_used, t * G_F + G_F + 2)
                act.activation(g.aux[:, :, bass.ts(t, TT)], y_ps[:, :, :], ACT.Copy).then_inc(y_copied, 1)

        @block.vector
        def _(dve):
            step = Chain(dve, step_sem)
            flat_gu = w_gu[:, :, :].rearrange("p c n -> p (c n)")
            flat_d = w_d[:, :, :].rearrange("p c n -> p (c n)")
            for n in range(N_PIECES):
                dve.wait_ge(landed[n % 2], 48 * (n // 2 + 1))
                decode_fp4(dve, step, g, raw[n % 2][:, :], tmp[:, :])
                m = n if n < N_PIECES_GU else n - N_PIECES_GU
                dst = (flat_gu if n < N_PIECES_GU else flat_d)[:, m * PIECE:(m + 1) * PIECE]
                dve.scalar_tensor_tensor(dst, raw[n % 2][:, :].bitcast(F8), FP8_GAIN, sc[n % 2][:, :],
                                         ALU.mult, ALU.mult).then_inc(piece_ready, 1)
            dve.sem_inc(h_ready, 2)
            dve.sem_inc(h_used, 2)
            with dve.Fori(0, NT) as t:
                for n in range(G_F):
                    k = n % 2
                    dve.wait_ge(silu_done, t * G_F + n + 1)
                    dve.wait_ge(h_used, t * G_F + max(n, 1) + 1)
                    dve.tensor_tensor(h[k][:, :], silu[k][:, :], up_ps[k][:, :], ALU.mult).then_inc(h_ready, 1)


def rms_residual(nc, g, a):
    with ExitStack() as ctx:
        def sb(name, shape, dt=F32):
            return [ctx.enter_context(nc.sbuf_tensor(f"z_{name}{i}", shape, dt)) for i in range(2)]

        def sem(name):
            return ctx.enter_context(nc.semaphore("z_" + name))

        squares, sd, rs = sb("squares", [P, C, TT]), sb("sd", [P, TT]), sb("rs", [P, TT])
        ms_ps = [ctx.enter_context(nc.psum_tensor(f"z_ms{i}", [P, TT], F32)) for i in range(2)]
        squared, summed, rooted, step_sem = sem("squared"), sem("summed"), sem("rooted"), sem("step")
        eps = g.const("eps")[:, 1:2]
        block = ctx.enter_context(nc.Block())

        def tile(x, t):
            return x[:, :, t * TT:(t + 1) * TT]

        @block.tensor
        def _(pe):
            for t in range(NT):
                pe.wait_ge(squared, t + 1)
                if t >= 2:
                    pe.wait_ge(rooted, t - 1)
                for c in range(C):
                    mm = pe.matmul(ms_ps[t % 2][:, :], g.const("mean"), squares[t % 2][:, c, :],
                                   start=c == 0, stop=c == C - 1)
                mm.then_inc(summed, 1)

        @block.scalar
        def _(act):
            def square(t):
                if t >= 2:
                    act.wait_ge(summed, t - 1)
                act.activation(squares[t % 2][:, :, :], tile(g.aux, t), ACT.Square).then_inc(squared, 1)

            square(0)
            for t in range(NT):
                if t + 1 < NT:
                    square(t + 1)
                act.wait_ge(summed, t + 1)
                if t >= 2:
                    act.wait_ge(step_sem, 3 * (t - 2) + 1)
                act.activation(sd[t % 2][:, :], ms_ps[t % 2][:, :], ACT.Sqrt, bias=eps).then_inc(rooted, 1)

        @block.vector
        def _(dve):
            step = Chain(dve, step_sem)
            for t in range(NT):
                dve.wait_ge(rooted, t + 1)
                step(dve.reciprocal(rs[t % 2][:, :], sd[t % 2][:, :]))
                step(dve.tensor_tensor(tile(g.aux, t), tile(g.aux, t), bc(rs[t % 2][:, :], 1, [P, C, TT]), ALU.mult))
                step(dve.tensor_tensor(tile(g.aux, t), tile(g.aux, t), tile(g.xt, t), ALU.add))


def decoder(nc, a, out, stop=99):
    with ExitStack() as ctx:
        g = Shared()
        g.xt = ctx.enter_context(nc.sbuf_tensor("residual", [P, C, T], F32))
        g.consts = ctx.enter_context(nc.sbuf_tensor("const_tables", [P, N_CONST], F32))
        g.shift = ctx.enter_context(nc.sbuf_tensor("fp4_shifts", [P, 4], I32))
        g.const = lambda name: g.consts[:, COL[name][0]:COL[name][1]]
        g.ln_sems = [ctx.enter_context(nc.semaphore("ln_" + n)) for n in
                     ("mean_ready", "centred_ready", "squares_ready", "var_ready", "sd_ready", "rs_ready", "normed")]
        g.stored = ctx.enter_context(nc.semaphore("stored"))
        g.stored_base = 0
        g.combine_dram = nc.dram_tensor("combine", [E_ROUTED + 1, T], F32, kind="Internal").ap()
        with ExitStack() as inner:
            g.keys = inner.enter_context(nc.sbuf_tensor("keys", [P, C, B, 4 * SLOTS], F32))
            g.values = inner.enter_context(nc.sbuf_tensor("values", [P, B, H0 // 2, 64], F32))
            sparse_select(nc, g, a)
            sparse_attention(nc, g, a)
        g.aux = ctx.enter_context(nc.sbuf_tensor("aux", [P, C, T], F32))
        plan = [lambda: layer_norm(nc, g, g.xt, g.xt, 0), lambda: wkv(nc, g, a),
                lambda: layer_norm(nc, g, g.xt, g.xt, 1), lambda: route(nc, g, a), lambda: experts(nc, g, a),
                lambda: layer_norm(nc, g, g.aux, g.xt, 2), lambda: causal_attention(nc, g, a),
                lambda: layer_norm(nc, g, g.xt, g.xt, 3), lambda: cross_attention(nc, g, a),
                lambda: layer_norm(nc, g, g.xt, g.xt, 4), lambda: feed_forward(nc, g, a), lambda: rms_residual(nc, g, a),
                lambda: layer_norm(nc, g, g.aux, g.xt, 5, out)]
        for k, phase in enumerate(plan):
            if k >= stop:
                break
            phase()
        if stop < len(plan):
            with nc.Block() as block:
                @block.sync
                def _(sp):
                    sp.dma_start(out, (g.aux if stop in (5, 12) else g.xt)[:, :, :]).then_inc(g.stored, 16)
                    sp.wait_ge(g.stored, 16)


def lay_out(i):
    order = feature_order()
    i = {k: np.asarray(v) for k, v in i.items()}

    def chunks(w):
        return w.reshape(w.shape[0] // P, P, *w.shape[1:]).swapaxes(0, 1)

    def residual(w):
        return chunks(w)[order]

    def reorder(w, n=P):
        return w.reshape(*w.shape[:-1], w.shape[-1] // P, P)[..., order].reshape(w.shape)

    def nibbles(packed):
        *lead, rows, n = packed.shape
        b = np.ascontiguousarray(packed).view(np.uint8).reshape(-1, rows // 16, 16, n, 4)
        b = np.ascontiguousarray(b.transpose(0, 2, 4, 1, 3)).view(np.int32)
        return b.reshape(*lead, 64, rows // 16, n // 4)

    x = i["x"].reshape(T, D)
    o = {"consts": constants(), "xt": residual(np.ascontiguousarray(x.T)),
         "ct": residual(np.ascontiguousarray(i["ctx_2048"].reshape(T, D).T)),
         "xtok": reorder(x).reshape(T // P, P, D).swapaxes(0, 1)}
    o["wi0"] = residual(i["L0_attn_Wi"])[:, :, 0]
    o["bi0"] = i["L0_attn_bi"].reshape(1, 1)
    for n in "qkv":
        o[f"w{n}0"] = residual(i[f"L0_attn_W{n}"])
    for n in "qk":
        o[f"b{n}0"] = chunks(i[f"L0_attn_b{n}"])
    o["bv0"] = i["L0_attn_bv"].reshape(1, D)
    o["wo0"] = chunks(reorder(i["L0_attn_Wo"]))
    o["bo0"] = residual(i["L0_attn_bo"])
    o["decay"], o["first"] = residual(i["L0_xattn_time_decay"]), residual(i["L0_xattn_time_first"])
    o["gate"] = residual(i["L0_ffn_gate_w"].T)
    o["one_row"] = np.ones((1, T), np.float32)

    def stack(name):
        return np.concatenate([i[f"L0_ffn_{name}"], i[f"L0_ffn_shared_{name}"][None]])

    o["gu"] = nibbles(reorder(stack("gate_up_packed")))
    o["d"] = nibbles(reorder(stack("down_packed")))
    o["gu_s"] = reorder(stack("gate_up_scales")).reshape(E_ROUTED + 1, -1)
    o["d_s"] = reorder(stack("down_scales")).reshape(E_ROUTED + 1, -1)
    turn = np.concatenate([np.arange(1, D, 2), np.arange(0, D, 2)])
    for k, n in enumerate("qkv"):
        w, b = i["L1_attn_Wqkv"][k * D:(k + 1) * D], i["L1_attn_bqkv"][k * D:(k + 1) * D]
        o[f"w{n}1"] = residual(w.T)
        if n == "v":
            o["bv1"] = b.reshape(1, D)
        else:
            o[f"b{n}1"] = chunks(b)
            o[f"w{n}r1"], o[f"b{n}r1"] = residual(w[turn].T), chunks(b[turn])
    o["wo1"] = chunks(reorder(i["L1_attn_Wout"].T))
    o["bo1"] = residual(i["L1_attn_bout"])
    kv = np.concatenate([i["L1_xattn_Wk"], i["L1_xattn_Wv"]])
    o["wqx"], o["wkx"], o["wvx"] = (residual(w.T) for w in (i["L1_xattn_Wq"], kv[0::2], kv[1::2]))
    gu = nibbles(reorder(i["L1_ffn_gate_up_packed"].T)).reshape(64, -1)
    d = nibbles(reorder(i["L1_ffn_down_packed"].T)).reshape(64, -1)
    o["ffn"] = np.concatenate([gu, d], axis=1)
    o["ffn_s"] = np.concatenate([reorder(i["L1_ffn_gate_up_scales"]).reshape(1, -1),
                                 reorder(i["L1_ffn_down_scales"]).reshape(1, -1)], axis=1)
    shift = np.zeros((P, 4), np.int64)
    shift[:64, 0] = 4
    shift[:, 1], shift[:, 2], shift[:, 3] = 2, 0x1C1C1C1C, 0x80808080 - (1 << 32)
    o["shift"] = shift.astype(np.int32)
    return {k: np.ascontiguousarray(v) for k, v in o.items()}


def kernel(**inputs):
    import concourse.bacc as _bacc
    from concourse import mybir as _mybir
    from concourse.bass_utils import run_bass_kernel_spmd as _run

    nc = _bacc.Bacc("TRN2", target_bir_lowering=False, num_devices=1)
    arrays = lay_out(inputs)
    args = {n: nc.dram_tensor(n, v.shape, _mybir.dt.from_np(v.dtype), kind="ExternalInput").ap()
            for n, v in arrays.items()}
    out = nc.dram_tensor("out", (P, C, T), F32, kind="ExternalOutput").ap()
    decoder(nc, args, out)
    r = _run(nc, [arrays], core_ids=[0])
    got = np.asarray(r.results[0]["out"])
    natural = np.empty_like(got)
    natural[feature_order()] = got
    return np.ascontiguousarray(natural.swapaxes(0, 1).reshape(D, T).T).reshape(B, S, D)
```

```python
from contextlib import ExitStack

import numpy as np

import concourse.bass as bass
from concourse import mybir

F32 = mybir.dt.float32
F32R = mybir.dt.float32r
F16 = mybir.dt.float16
F8 = mybir.dt.float8e4
I32 = mybir.dt.int32
ALU = mybir.AluOpType
ACT = mybir.ActivationFunctionType
AX = mybir.AxisListType

P = 128
B, S, D = 8, 256, 512
T = B * S
C = D // P
TT = 512
NT = T // TT
LN_EPS = 1e-5

H0, HD0 = 16, 32
KEEP = min(max(1, int(S * 0.2)), S - 1)
MIN_TOKENS = 32
SLOTS = 64
assert max(KEEP, MIN_TOKENS) <= SLOTS

E_ROUTED, TOP_K, I_MOE, GS = 16, 4, 384, 128
G_D, G_I = D // GS, I_MOE // GS
I_FFN = 1408
G_F = I_FFN // GS
H1, HD1 = 16, 32
HX, HDX = 32, 16

_WIDTHS = [("ident", P), ("ones", P), ("mean", P), ("tri", 2 * S), ("slot", P), ("causal", P),
           ("head4", 4), ("head8", 8), ("blk16", P), ("perm", P), ("den16", 64), ("expert_lt", 256),
           ("cosc", 4), ("sinc", 4), ("eps", 3)]
COL = {}
_at = 0
for _n, _w in _WIDTHS:
    COL[_n] = (_at, _at + _w)
    _at += _w
N_CONST = _at


def feature_order():
    p = np.arange(P)
    return 2 * (p % 64) + p // 64


def constants():
    c = np.zeros((P, N_CONST), np.float32)

    def put(name, value):
        a, b = COL[name]
        c[:, a:b] = value

    p = np.arange(P)
    order = feature_order()
    put("ident", np.eye(P))
    put("ones", 1.0)
    put("mean", 1.0 / D)
    j = np.arange(S)
    put("tri", np.concatenate([(j[None, :] < (q * P + p)[:, None]) for q in range(2)], axis=1))
    put("slot", np.tile(np.arange(SLOTS), P // SLOTS)[None, :])
    put("causal", p[None, :] >= p[:, None])
    put("head4", (p[:, None] // 32 == np.arange(4)[None, :]) * (D ** -0.5))
    put("head8", p[:, None] // 16 == np.arange(8)[None, :])
    put("blk16", (p[:, None] // 16 == p[None, :] // 16) / 16.0)
    put("perm", p[:, None] == order[None, :])
    put("den16", np.concatenate([np.arange(32) < 16, np.arange(32) >= 16])[None, :])
    e = np.arange(E_ROUTED)
    put("expert_lt", (e[None, :] < e[:, None]).reshape(1, 256))
    freq = (np.float32(10000.0) ** (-(np.arange(0, D, 2, dtype=np.float32) / np.float32(D)))).astype(np.float32)
    angle = (np.float32(S) * np.repeat(freq, 2)).astype(np.float32)
    cos, sin = np.cos(angle), np.sin(angle)
    sin = np.where(np.arange(D) < D // 2, -sin, sin)
    put("cosc", cos.reshape(4, P).T)
    put("sinc", sin.reshape(4, P).T)
    put("eps", np.array([[LN_EPS, 1e-6, 0.0]]))
    return c, np.stack([cos, sin]).astype(np.float32).reshape(1, 2 * D)


class Chain:

    def __init__(self, eng, sem, base=0):
        self.eng, self.sem, self.base, self.n = eng, sem, base, 0

    def __call__(self, ins):
        self.n += 1
        ins.then_inc(self.sem, 1)
        self.eng.wait_ge(self.sem, self.base + self.n)


class Shared:
    pass


def bc(ap, axis, shape):
    return ap.unsqueeze(axis).to_broadcast(shape)


def layer_norm(nc, g, src, dst, layer, out_dram=None):
    with ExitStack() as ctx:
        def sb(name, shape, dt=F32):
            return ctx.enter_context(nc.sbuf_tensor(f"{name}_n{layer}", shape, dt))

        mean_ps = [ctx.enter_context(nc.psum_tensor(f"mean{i}_n{layer}", [P, TT], F32)) for i in range(2)]
        var_ps = [ctx.enter_context(nc.psum_tensor(f"var{i}_n{layer}", [P, TT], F32)) for i in range(2)]
        centred = [sb(f"centred{i}", [P, C, TT]) for i in range(2)]
        squares = [sb(f"squares{i}", [P, C, TT]) for i in range(2)]
        rs = [sb(f"rs{i}", [P, TT]) for i in range(2)]
        base = NT * layer
        mean_ready, centred_ready, squares_ready, var_ready, ln_ready, rs_ready, normed = g.ln_sems
        eps = g.const("eps")[:, 0:1]

        def tile(x, t):
            return x[:, :, t * TT:(t + 1) * TT]

        block = ctx.enter_context(nc.Block())

        @block.tensor
        def _(pe):
            def mean(t):
                if t >= 2:
                    pe.wait_ge(centred_ready, base + t - 1)
                for c in range(C):
                    mm = pe.matmul(mean_ps[t % 2][:, :], g.const("mean"), tile(src, t)[:, c, :],
                                   start=c == 0, stop=c == C - 1)
                mm.then_inc(mean_ready, 1)

            def var(t):
                pe.wait_ge(squares_ready, base + t + 1)
                if t >= 2:
                    pe.wait_ge(ln_ready, base + t - 1)
                for c in range(C):
                    mm = pe.matmul(var_ps[t % 2][:, :], g.const("mean"), squares[t % 2][:, c, :],
                                   start=c == 0, stop=c == C - 1)
                mm.then_inc(var_ready, 1)

            mean(0)
            for t in range(NT):
                if t + 1 < NT:
                    mean(t + 1)
                var(t)

        @block.vector
        def _(dve):
            def centre(t):
                dve.wait_ge(mean_ready, base + t + 1)
                if t >= 2:
                    dve.wait_ge(normed, base + t - 1)
                dve.tensor_tensor(centred[t % 2][:, :, :], tile(src, t), bc(mean_ps[t % 2][:, :], 1, [P, C, TT]),
                                  ALU.subtract).then_inc(centred_ready, 1)

            centre(0)
            for t in range(NT):
                if t + 1 < NT:
                    centre(t + 1)
                dve.wait_ge(rs_ready, base + t + 1)
                dve.tensor_tensor(tile(dst, t), centred[t % 2][:, :, :], bc(rs[t % 2][:, :], 1, [P, C, TT]),
                                  ALU.mult).then_inc(normed, 1)

        @block.scalar
        def _(act):
            def square(t):
                act.wait_ge(centred_ready, base + t + 1)
                if t >= 2:
                    act.wait_ge(var_ready, base + t - 1)
                act.activation(squares[t % 2][:, :, :], centred[t % 2][:, :, :], ACT.Square).then_inc(squares_ready, 1)

            square(0)
            for t in range(NT):
                if t + 1 < NT:
                    square(t + 1)
                act.wait_ge(var_ready, base + t + 1)
                if t >= 2:
                    act.wait_ge(normed, base + t - 1)
                act.activation(rs[t % 2][:, :], var_ps[t % 2][:, :], ACT.Ln, bias=eps).then_inc(ln_ready, 1)
                act.wait_ge(ln_ready, base + t + 1)
                act.activation(rs[t % 2][:, :], rs[t % 2][:, :], ACT.Exp, scale=-0.5).then_inc(rs_ready, 1)

        @block.sync
        def _(sp):
            sp.wait_ge(normed, base + NT)
            if out_dram is not None:
                sp.dma_start(out_dram, dst[:, :, :]).then_inc(g.stored, 16)
                sp.wait_ge(g.stored, g.stored_base + 16)


def sparse_select(nc, g, a):
    with ExitStack() as ctx:
        def sb(name, shape, dt=F32):
            return ctx.enter_context(nc.sbuf_tensor("s_" + name, shape, dt))

        def sem(name):
            return ctx.enter_context(nc.semaphore("s_" + name))

        wi = sb("wi", [P, C])
        wib = sb("wib", [P, C, P])
        bi = sb("bi", [P, 1])
        wk = sb("wk", [P, C, D])
        wv = sb("wv", [P, C, D])
        bk = sb("bk", [P, C])
        bv = sb("bv", [1, D])
        imp = sb("imp", [P, B, S])
        ge = sb("ge", [P, B, 2, S])
        gt = sb("gt", [P, B, 2, S])
        own = sb("own", [P, 2 * B])
        small = sb("small", [P, 4, 2 * B])
        sel = sb("sel", [P, 2 * B, P])
        xtok = [sb(f"xtok{i}", [P, 2, D]) for i in range(2)]
        xsel = sb("xsel", [P, C, B, P])
        valid = sb("valid", [P, B, P])
        imp_ps = ctx.enter_context(nc.psum_tensor("s_imp_ps", [P, T], F32))
        row_ps = [ctx.enter_context(nc.psum_tensor(f"s_row{i}", [P, 512], F32)) for i in range(2)]
        xsel_ps = [ctx.enter_context(nc.psum_tensor(f"s_xs{i}", [P, 512], F32)) for i in range(2)]

        loaded, weights, wib_ready = sem("loaded"), sem("weights"), sem("wib_ready")
        imp_done, imp_copied, dve_step, sel_ready = sem("imp_done"), sem("imp_copied"), sem("dve_step"), sem("sel_ready")
        zeroed = sem("zeroed")
        tok_loaded = [sem(f"tok_loaded{i}") for i in range(2)]
        gathered, xsel_copied = sem("gathered"), sem("xsel_copied")
        row_done, row_used = sem("row_done"), sem("row_used")

        block = ctx.enter_context(nc.Block())

        @block.sync
        def _(sp):
            sp.dma_start(g.consts[:, :], a["consts"]).then_inc(loaded, 16)
            sp.dma_start(g.shift[:, :], a["shift"]).then_inc(loaded, 16)
            sp.dma_start(wi[:, :], a["wi0"]).then_inc(loaded, 16)
            sp.dma_start(bi[:, :], a["bi0"].to_broadcast([P, 1])).then_inc(loaded, 16)
            for t in range(NT):
                sp.dma_start(g.xt[:, :, t * TT:(t + 1) * TT], a["xt"][:, :, t * TT:(t + 1) * TT]).then_inc(loaded, 16)
            for dst, src in ((wk[:, :, :], a["wk0"]), (wv[:, :, :], a["wv0"]), (bk[:, :], a["bk0"]), (bv[:, :], a["bv0"])):
                sp.dma_start(dst, src).then_inc(weights, 16)
            with sp.Fori(0, B // 2) as i:
                for u in range(2):
                    sp.wait_ge(gathered, 2 * i + u + 1)
                    sp.dma_start(xtok[u][:, :, :], a["xtok"][:, bass.ds(4 * i + 2 * u, 2), :]).then_inc(tok_loaded[u], 16)

        @block.gpsimd
        def _(pool):
            pool.memset(g.keys[:, :, :, :], 0.0).then_inc(zeroed, 1)
            pool.memset(g.values[:, :, :, :], 0.0).then_inc(zeroed, 1)

        @block.scalar
        def _(act):
            for t in range(NT):
                act.wait_ge(imp_done, t + 1)
                act.activation(imp[:, 2 * t:2 * t + 2, :], imp_ps[:, t * TT:(t + 1) * TT].rearrange("p (b s) -> p b s", b=2),
                               ACT.Identity, bias=bi[:, :]).then_inc(imp_copied, 1)
            with act.Fori(0, B // 2) as i:
                for u in range(2):
                    act.wait_ge(gathered, 2 * i + u + 3)
                    act.activation(xsel[:, :, bass.ds(2 * i + u, 1), :],
                                   xsel_ps[u][:, :].rearrange("p (c o s) -> p c o s", c=C, o=1),
                                   ACT.Copy).then_inc(xsel_copied, 1)

        @block.vector
        def _(dve):
            step = Chain(dve, dve_step)
            dve.wait_ge(loaded, 16 * (4 + NT))
            dve.tensor_copy(wib[:, :, :], bc(wi[:, :], 2, [P, C, P])).then_inc(wib_ready, 1)
            dve.wait_ge(imp_copied, NT)
            step(dve.tensor_tensor(sel[:, :, :], imp[:, :, :].rearrange("p b (q i) -> p (b q) i", q=2),
                                   bc(g.const("ident"), 1, [P, 2 * B, P]), ALU.mult))
            step(dve.tensor_reduce(own[:, :], sel[:, :, :], AX.X, ALU.add))
            own_v = own[:, :].rearrange("p (b q) -> p b q", q=2)
            for q in range(2):
                mine = bc(own_v[:, :, q], 2, [P, B, S])
                dve.tensor_tensor(ge[:, :, q, :], imp[:, :, :], mine, ALU.is_ge)
                last = dve.tensor_tensor(gt[:, :, q, :], imp[:, :, :], mine, ALU.is_gt)
            step(last)
            n_ge, n_gt, ties, keep = (small[:, k, :] for k in range(4))
            dve.tensor_reduce(n_ge, ge[:, :, :, :].rearrange("p b q j -> p (b q) j"), AX.X, ALU.add)
            step(dve.tensor_reduce(n_gt, gt[:, :, :, :].rearrange("p b q j -> p (b q) j"), AX.X, ALU.add))
            step(dve.tensor_tensor(ge[:, :, :, :], ge[:, :, :, :], gt[:, :, :, :], ALU.subtract))
            step(dve.tensor_tensor(ge[:, :, :, :].rearrange("p b q j -> p b (q j)"),
                                   ge[:, :, :, :].rearrange("p b q j -> p b (q j)"),
                                   bc(g.const("tri"), 1, [P, B, 2 * S]), ALU.mult))
            step(dve.tensor_reduce(ties, ge[:, :, :, :].rearrange("p b q j -> p (b q) j"), AX.X, ALU.add))
            step(dve.tensor_tensor(ties, ties, n_gt, ALU.add))
            dve.tensor_scalar(n_ge, n_ge, float(KEEP) + 0.5, None, ALU.is_lt)
            step(dve.tensor_scalar(keep, ties, float(MIN_TOKENS) - 0.5, None, ALU.is_lt))
            step(dve.tensor_tensor(keep, keep, n_ge, ALU.max))
            step(dve.tensor_tensor(sel[:, :, :], bc(g.const("slot"), 1, [P, 2 * B, P]), bc(ties, 2, [P, 2 * B, P]),
                                   ALU.is_equal))
            dve.tensor_tensor(sel[:, :, :], sel[:, :, :], bc(keep, 2, [P, 2 * B, P]), ALU.mult).then_inc(sel_ready, 1)
            for n in range(2):
                dve.wait_ge(row_done, n + 1)
                dve.tensor_copy(valid[:, 4 * n:4 * n + 4, :], row_ps[n][:, :].rearrange("p (b s) -> p b s", b=4))\
                   .then_inc(row_used, 1)
            dve.wait_ge(row_used, 2)
            dve.wait_ge(weights, 64)
            dve.wait_ge(zeroed, 2)
            for m in range(C):
                dve.wait_ge(row_done, 3 + m)
                ps = row_ps[m % 2][:, :].rearrange("p (b s) -> p b s", b=B)
                for j in range(4):
                    r = slice(32 * j, 32 * j + 32)
                    last = dve.scalar_tensor_tensor(g.keys[r, m, :, j * SLOTS:(j + 1) * SLOTS], valid[r, :, 0:SLOTS],
                                                    bk[r, m:m + 1], ps[r, :, :], ALU.mult, ALU.add)
                last.then_inc(row_used, 1)
            for b in range(B):
                dve.wait_ge(row_done, 3 + C + b)
                ps = row_ps[b % 2][:, :].rearrange("p (n two d) -> p n two d", two=2, d=HD0)
                for u in range(2):
                    r = slice(64 * u, 64 * u + 64)
                    last = dve.tensor_copy(g.values[r, b, :, 32 * u:32 * u + 32], ps[r, :, u, :])
                last.then_inc(row_used, 1)

        @block.tensor
        def _(pe):
            pe.wait_ge(wib_ready, 1)
            for t in range(NT):
                for c in range(C):
                    mm = pe.matmul(imp_ps[:, t * TT:(t + 1) * TT], wib[:, c, :], g.xt[:, c, t * TT:(t + 1) * TT],
                                   start=c == 0, stop=c == C - 1)
                mm.then_inc(imp_done, 1)
            pe.wait_ge(sel_ready, 1)
            sel_v = sel[:, :, :].rearrange("p (b q) s -> p b q s", q=2)
            for n in range(2):
                for q in range(2):
                    mm = pe.matmul(row_ps[n][:, :], g.const("ones"), sel_v[:, 4 * n:4 * n + 4, q, :],
                                   start=q == 0, stop=q == 1)
                mm.then_inc(row_done, 1)
            pe.sem_inc(gathered, 2)
            pe.sem_inc(xsel_copied, 2)
            with pe.Fori(0, B // 2) as i:
                for u in range(2):
                    pe.wait_ge(tok_loaded[u], 16 * i + 16)
                    pe.wait_ge(xsel_copied, 2 * i + u + 1)
                    for c in range(C):
                        for q in range(2):
                            mm = pe.matmul(xsel_ps[u][:, c * P:(c + 1) * P], xtok[u][:, q, c * P:(c + 1) * P],
                                           sel[:, bass.ds(4 * i + 2 * u + q, 1), :], start=q == 0, stop=q == 1)
                    mm.then_inc(gathered, 1)
            pe.wait_ge(xsel_copied, B + 2)
            pe.wait_ge(weights, 64)
            for m in range(C):
                pe.wait_ge(row_used, m + 1)
                for c in range(C):
                    mm = pe.matmul(row_ps[m % 2][:, :], wk[:, c, m * P:(m + 1) * P], xsel[:, c, :, 0:SLOTS],
                                   start=c == 0, stop=c == C - 1)
                mm.then_inc(row_done, 1)
            for b in range(B):
                pe.wait_ge(row_used, C + b + 1)
                for c in range(C):
                    pe.matmul(row_ps[b % 2][:, :], xsel[:, c, b, :], wv[:, c, :], start=c == 0, stop=False)
                pe.matmul(row_ps[b % 2][:, :], valid[0:1, b, :], bv[:, :], start=False, stop=True).then_inc(row_done, 1)


def sparse_attention(nc, g, a):
    scale = HD0 ** -0.5
    with ExitStack() as ctx:
        def sb(name, shape, dt=F32):
            return ctx.enter_context(nc.sbuf_tensor("a0_" + name, shape, dt))

        def sem(name):
            return ctx.enter_context(nc.semaphore("a0_" + name))

        def ps(name, shape):
            return ctx.enter_context(nc.psum_tensor("a0_" + name, shape, F32))

        wq = sb("wq", [P, C, D])
        wo = sb("wo", [P, C, D])
        bq = sb("bq", [P, C])
        bo = sb("bo", [P, C])
        q_sb = sb("q", [P, C, S])
        v_sb = sb("v", [P, H0 // 2, 64])
        e_sb = [sb(f"e{i}", [P, H0, SLOTS]) for i in range(2)]
        mx = [sb(f"mx{i}", [P, H0]) for i in range(2)]
        e0 = [sb(f"e0{i}", [P, H0]) for i in range(2)]
        den = [sb(f"den{i}", [P, H0]) for i in range(2)]
        pt = sb("pt", [P, H0 // 2, S])
        at = sb("at", [P, C, S])
        head_ps = ps("head", [P, C, S])
        s_ps = [ps(f"s{i}", [P, H0, SLOTS]) for i in range(2)]
        pt_ps = ps("pt_ps", [P, H0 // 2, P])
        o_ps = s_ps[0][:, :, :].rearrange("p h s -> p (h s)").rearrange("p (c q) -> p c q", c=C)

        weights = sem("weights")
        q_done, q_copied, s_done, shifted, exped, p_ready = (sem(n) for n in ("q_done", "q_copied", "s_done", "shifted", "exped", "p_ready"))
        t_done, t_copied, v_copied, av_done, av_copied, o_done, added, step_sem = (
            sem(n) for n in ("t_done", "t_copied", "v_copied", "av_done", "av_copied", "o_done", "added", "step"))

        block = ctx.enter_context(nc.Block())

        @block.sync
        def _(sp):
            for dst, src in ((wq[:, :, :], a["wq0"]), (wo[:, :, :], a["wo0"]), (bq[:, :], a["bq0"]), (bo[:, :], a["bo0"])):
                sp.dma_start(dst, src).then_inc(weights, 16)

        @block.gpsimd
        def _(pool):
            with pool.Fori(0, B) as b:
                pool.wait_ge(av_done, b + 1)
                pool.tensor_copy(v_sb[:, :, :].rearrange("p n d -> p (n d)"),
                                 g.values[:, bass.ds(b, 1), :, :].rearrange("p b n d -> p (b n d)"))\
                    .then_inc(v_copied, 1)

        @block.tensor
        def _(pe):
            pe.wait_ge(weights, 64)
            pe.sem_inc(av_done, 1)
            with pe.Fori(0, B) as b:
                pe.wait_ge(av_copied, b + 1)
                for m in range(C):
                    for c in range(C):
                        mm = pe.matmul(head_ps[:, m, :], wq[:, c, m * P:(m + 1) * P], g.xt[:, c, bass.ts(b, S)],
                                       start=c == 0, stop=c == C - 1)
                mm.then_inc(q_done, 1)
                pe.wait_ge(q_copied, b + 1)
                pe.wait_ge(added, b + 1)
                for q in range(2):
                    for c in range(C):
                        mm = pe.matmul(s_ps[q][:, 4 * c:4 * c + 4, :], q_sb[:, c, q * P:(q + 1) * P],
                                       g.keys[:, c, bass.ds(b, 1), :], start=True, stop=True)
                    mm.then_inc(s_done, 1)
                for q in range(2):
                    pe.wait_ge(p_ready, 2 * b + q + 1)
                    pe.wait_ge(t_copied, 2 * b + q + 1)
                    for n in range(H0 // 2):
                        mm = pe.transpose(pt_ps[:, n, :], e_sb[q][:, 2 * n:2 * n + 2, :].rearrange("p h s -> p (h s)"),
                                          g.const("ident"))
                    mm.then_inc(t_done, 1)
                pe.wait_ge(t_copied, 2 * b + 3)
                pe.wait_ge(v_copied, b + 1)
                for n in range(H0 // 2):
                    r = 64 * (n % 2)
                    mm = pe.matmul(head_ps[r:r + 64, n // 2, :], v_sb[:, n, :], pt[:, n, :], start=True, stop=True)
                mm.then_inc(av_done, 1)
                pe.wait_ge(av_copied, b + 2)
                for m in range(C):
                    for c in range(C):
                        mm = pe.matmul(o_ps[:, m, :], wo[:, c, m * P:(m + 1) * P], at[:, c, :],
                                       start=c == 0, stop=c == C - 1)
                mm.then_inc(o_done, 1)

        @block.scalar
        def _(act):
            act.wait_ge(weights, 64)
            act.sem_inc(av_copied, 1)
            act.sem_inc(t_copied, 1)
            with act.Fori(0, B) as b:
                act.wait_ge(q_done, b + 1)
                for m in range(C):
                    last = act.activation(q_sb[:, m, :], head_ps[:, m, :], ACT.Identity, bias=bq[:, m:m + 1])
                last.then_inc(q_copied, 1)
                for q in range(2):
                    act.wait_ge(shifted, 2 * b + q + 1)
                    act.activation(e0[q][:, :], mx[q][:, :], ACT.Exp, scale=-scale)
                    act.activation(e_sb[q][:, :, :], e_sb[q][:, :, :], ACT.Exp, scale=scale).then_inc(exped, 1)
                for q in range(2):
                    act.wait_ge(t_done, 2 * b + q + 1)
                    act.activation(pt[:, :, q * P:(q + 1) * P], pt_ps[:, :, :], ACT.Copy).then_inc(t_copied, 1)
                act.wait_ge(av_done, b + 2)
                act.activation(at[:, :, :], head_ps[:, :, :], ACT.Copy).then_inc(av_copied, 1)

        @block.vector
        def _(dve):
            dve.wait_ge(weights, 64)
            dve.sem_inc(added, 1)
            steps = 2 * 2 + 2 * 3
            with dve.Fori(0, B) as b:
                step = Chain(dve, step_sem, b * steps)
                for q in range(2):
                    dve.wait_ge(s_done, 2 * b + q + 1)
                    step(dve.tensor_reduce(mx[q][:, :], s_ps[q][:, :, :], AX.X, ALU.max))
                    step(dve.tensor_scalar(mx[q][:, :], mx[q][:, :], 0.0, None, ALU.max))
                    dve.tensor_tensor(e_sb[q][:, :, :], s_ps[q][:, :, :], bc(mx[q][:, :], 2, [P, H0, SLOTS]),
                                      ALU.subtract).then_inc(shifted, 1)
                for q in range(2):
                    dve.wait_ge(exped, 2 * b + q + 1)
                    step(dve.tensor_reduce(den[q][:, :], e_sb[q][:, :, :], AX.X, ALU.add))
                    step(dve.scalar_tensor_tensor(den[q][:, :], e0[q][:, :], float(S - SLOTS), den[q][:, :],
                                                  ALU.mult, ALU.add))
                    step(dve.reciprocal(den[q][:, :], den[q][:, :]))
                    dve.tensor_tensor(e_sb[q][:, :, :], e_sb[q][:, :, :], bc(den[q][:, :], 2, [P, H0, SLOTS]),
                                      ALU.mult).then_inc(p_ready, 1)
                assert step.n == steps
                dve.wait_ge(o_done, b + 1)
                for m in range(C):
                    x = g.xt[:, m, bass.ts(b, S)]
                    last = dve.scalar_tensor_tensor(x, o_ps[:, m, :], bo[:, m:m + 1], x, ALU.add, ALU.add)
                last.then_inc(added, 1)


def wkv(nc, g, a):
    FAR = -1e38
    BP = 4
    PIECES = C * (B // BP)
    with ExitStack() as ctx:
        def sb(name, shape, dt=F32):
            return ctx.enter_context(nc.sbuf_tensor("w_" + name, shape, dt))

        def sem(name):
            return ctx.enter_context(nc.semaphore("w_" + name))

        decay = sb("decay", [P, C])
        first = sb("first", [P, C])
        w_dec = sb("w_dec", [P, C])
        w_row = sb("w_row", [P, C, BP, S])
        names = ("pp", "prev", "eb", "kb", "kv", "aa", "bb", "e1", "e2", "num")
        buf = {n: [sb(f"{n}{i}", [P, BP, S]) for i in range(2)] for n in names}

        loaded, w_ready, row_ready = sem("loaded"), sem("w_ready"), sem("row_ready")
        den_ready, logged, inverted = sem("den_ready"), sem("logged"), sem("inverted")
        pp_done, prev_ready, diffs, exps_a, kv_ready, scanned, yexp, done, step_sem, kb_sub, e2v = (
            sem(n) for n in ("pp_done", "prev_ready", "diffs", "exps_a", "kv_ready", "scanned", "yexp", "done", "step",
                             "kb_sub", "e2v"))

        def piece(n):
            c, h = n // (B // BP), n % (B // BP)
            sl = slice(h * BP * S, (h + 1) * BP * S)
            k = g.xt[:, c, sl].rearrange("p (b s) -> p b s", b=BP)
            v = g.aux[:, c, sl].rearrange("p (b s) -> p b s", b=BP)
            return c, k, v

        def flat(x):
            return x[:, :, :].rearrange("p b s -> p (b s)")

        block = ctx.enter_context(nc.Block())

        @block.sync
        def _(sp):
            sp.dma_start(decay[:, :], a["decay"]).then_inc(loaded, 16)
            sp.dma_start(first[:, :], a["first"]).then_inc(loaded, 16)
            sp.dma_start(g.aux[:, :, :], a["ct"]).then_inc(loaded, 16)

        @block.scalar
        def _(act):
            act.wait_ge(loaded, 48)
            act.activation(w_dec[:, :], decay[:, :], ACT.Exp).then_inc(w_ready, 1)

            def early_prev(n):
                i = n % 2
                act.wait_ge(pp_done, n + 1)
                if n >= 2:
                    act.wait_ge(diffs, n - 1)
                act.activation(buf["prev"][i][:, :, 1:S], buf["pp"][i][:, :, 0:S - 1], ACT.Copy).then_inc(prev_ready, 1)

            def early(n):
                i = n % 2
                c, k, v = piece(n)
                if n == 0:
                    early_prev(n)
                act.wait_ge(diffs, n + 1)
                act.activation(buf["eb"][i][:, :, :], buf["eb"][i][:, :, :], ACT.Exp, bias=w_dec[:, c:c + 1])
                act.wait_ge(kb_sub, n + 1)
                act.activation(buf["kb"][i][:, :, :], buf["kb"][i][:, :, :], ACT.Exp).then_inc(exps_a, 1)
                act.activation(buf["e2"][i][:, :, :], buf["e2"][i][:, :, :], ACT.Exp)
                act.activation(buf["e1"][i][:, :, :], buf["e1"][i][:, :, :], ACT.Exp, scale=-1.0).then_inc(yexp, 1)

            def invert(n):
                x = buf["kv"][n % 2][:, :, :]
                act.wait_ge(den_ready, n + 1)
                act.activation(x, x, ACT.Ln).then_inc(logged, 1)
                act.wait_ge(logged, n + 1)
                act.activation(x, x, ACT.Exp, scale=-1.0).then_inc(inverted, 1)

            early(0)
            for n in range(PIECES):
                if n + 1 < PIECES:
                    early_prev(n + 1)
                invert(n)
                if n + 1 < PIECES:
                    early(n + 1)

        @block.gpsimd
        def _(pool):
            for i in range(2):
                pool.memset(buf["prev"][i][:, :, 0:1], FAR).then_inc(prev_ready, 1)
            pool.memset(w_row[:, :, :, :], 0.0).then_inc(row_ready, 1)
            for n in range(PIECES):
                i = n % 2
                c, k, v = piece(n)
                pool.wait_ge(pp_done, n + 1)
                if n >= 2:
                    pool.wait_ge(done, n - 1)
                pool.tensor_tensor(buf["kb"][i][:, :, :], k, buf["pp"][i][:, :, :], ALU.subtract).then_inc(kb_sub, 1)
                pool.wait_ge(exps_a, n + 1)
                pool.tensor_tensor(buf["kv"][i][:, :, :], buf["kb"][i][:, :, :], v, ALU.mult).then_inc(kv_ready, 1)
                pool.wait_ge(yexp, n + 1)
                pool.tensor_tensor(buf["num"][i][:, :, :], buf["e2"][i][:, :, :], v, ALU.mult).then_inc(e2v, 1)

        @block.vector
        def _(dve):
            step = Chain(dve, step_sem)
            dve.wait_ge(w_ready, 1)
            step(dve.tensor_scalar(w_dec[:, :], w_dec[:, :], -1.0, None, ALU.mult))
            dve.wait_ge(row_ready, 1)
            for c in range(C):
                last = dve.tensor_scalar(w_row[:, c, :, :], w_row[:, c, :, :], w_dec[:, c:c + 1], None, ALU.add)
            step(last)
            step(dve.memset(w_row[:, :, :, 0:1], 3 * FAR))
            dve.wait_ge(prev_ready, 2)

            def front(n):
                i = n % 2
                c, k, v = piece(n)
                if n >= 2:
                    dve.wait_ge(kb_sub, n - 1)
                    dve.wait_ge(prev_ready, 2 + n - 1)
                    dve.wait_ge(diffs, n - 1)
                dve.tensor_tensor_scan(flat(buf["pp"][i]), w_row[:, c, :, :].rearrange("p b s -> p (b s)"),
                                       k.rearrange("p b s -> p (b s)"), FAR, ALU.add, ALU.max).then_inc(pp_done, 1)

            def middle(n):
                i = n % 2
                c, k, v = piece(n)
                dve.wait_ge(prev_ready, 2 + n + 1)
                dve.wait_ge(pp_done, n + 1)
                if n >= 2:
                    dve.wait_ge(done, n - 1)
                prev = buf["prev"][i][:, :, :]
                step(dve.scalar_tensor_tensor(flat(buf["e1"][i]), k.rearrange("p b s -> p (b s)"), first[:, c:c + 1],
                                              flat(buf["prev"][i]), ALU.add, ALU.subtract))
                step(dve.tensor_scalar(flat(buf["e2"][i]), flat(buf["e1"][i]), 0.0, None, ALU.min))
                dve.tensor_scalar(flat(buf["e1"][i]), flat(buf["e1"][i]), 0.0, None, ALU.max)
                dve.tensor_tensor(buf["eb"][i][:, :, :], prev, buf["pp"][i][:, :, :], ALU.subtract).then_inc(diffs, 1)

            def scans(n):
                i = n % 2
                dve.wait_ge(exps_a, n + 1)
                dve.tensor_tensor_scan(flat(buf["bb"][i]), flat(buf["eb"][i]), flat(buf["kb"][i]), 0.0, ALU.mult, ALU.add)
                dve.wait_ge(kv_ready, n + 1)
                step(dve.tensor_tensor_scan(flat(buf["aa"][i]), flat(buf["eb"][i]), flat(buf["kv"][i]), 0.0,
                                            ALU.mult, ALU.add))

            def back(n):
                i = n % 2
                c, k, v = piece(n)
                e1, e2, aa, bb, num = (buf[x][i] for x in ("e1", "e2", "aa", "bb", "num"))
                dve.wait_ge(yexp, n + 1)
                t1, t2 = buf["kb"][i], buf["kv"][i]
                dve.tensor_tensor(t1[:, :, 1:S], e1[:, :, 1:S], aa[:, :, 0:S - 1], ALU.mult)
                dve.tensor_tensor(t2[:, :, 1:S], e1[:, :, 1:S], bb[:, :, 0:S - 1], ALU.mult)
                dve.memset(t1[:, :, 0:1], 0.0)
                step(dve.memset(t2[:, :, 0:1], 0.0))
                dve.wait_ge(e2v, n + 1)
                dve.tensor_tensor(t1[:, :, :], t1[:, :, :], num[:, :, :], ALU.add)
                dve.tensor_tensor(t2[:, :, :], t2[:, :, :], e2[:, :, :], ALU.add).then_inc(den_ready, 1)

            def finish(n):
                i = n % 2
                c, k, v = piece(n)
                t1, t2 = buf["kb"][i], buf["kv"][i]
                dve.wait_ge(inverted, n + 1)
                dve.wait_ge(den_ready, n + 1)
                step(dve.tensor_tensor(flat(t1), flat(t1), flat(t2), ALU.mult))
                dve.tensor_tensor(k, k, t1[:, :, :], ALU.add).then_inc(done, 1)

            front(0)
            middle(0)
            for n in range(PIECES):
                if n + 1 < PIECES:
                    front(n + 1)
                scans(n)
                if n >= 1:
                    finish(n - 1)
                if n + 1 < PIECES:
                    middle(n + 1)
                back(n)
            finish(PIECES - 1)


def route(nc, g, a):
    NTOK = T // P
    E = E_ROUTED
    with ExitStack() as ctx:
        def sb(name, shape, dt=F32):
            return ctx.enter_context(nc.sbuf_tensor("r_" + name, shape, dt))

        def sem(name):
            return ctx.enter_context(nc.semaphore("r_" + name))

        wg = sb("wg", [P, C, E])
        lt = sb("lt", [E, T])
        p = sb("p", [P, NTOK, E])
        big = [sb(f"big{i}", [P, NTOK, E, E]) for i in range(2)]
        m = sb("m", [P, NTOK])
        rank = sb("rank", [P, NTOK, E])
        ct = sb("ct", [E, T])
        logit_ps = ctx.enter_context(nc.psum_tensor("r_logit", [E, T], F32))
        tok_ps = ctx.enter_context(nc.psum_tensor("r_tok", [P, NTOK, E], F32))
        loaded, logits, copied, turned, shifted, exped, ready, back, ct_ready, stored, step_sem = (
            sem(n) for n in ("loaded", "logits", "copied", "turned", "shifted", "exped", "ready", "back", "ct_ready",
                             "stored", "step"))
        block = ctx.enter_context(nc.Block())

        @block.sync
        def _(sp):
            sp.dma_start(wg[:, :, :], a["gate"]).then_inc(loaded, 16)
            sp.dma_start(g.combine_dram[E:E + 1, :], a["one_row"]).then_inc(stored, 16)
            sp.wait_ge(ct_ready, NT)
            sp.dma_start(g.combine_dram[0:E, :], ct[:, :]).then_inc(stored, 16)
            sp.wait_ge(stored, 32)

        @block.tensor
        def _(pe):
            pe.wait_ge(loaded, 16)
            for t in range(NT):
                for c in range(C):
                    mm = pe.matmul(logit_ps[:, t * TT:(t + 1) * TT], wg[:, c, :], g.xt[:, c, t * TT:(t + 1) * TT],
                                   start=c == 0, stop=c == C - 1)
                mm.then_inc(logits, 1)
            pe.wait_ge(copied, NT)
            for n in range(NTOK):
                mm = pe.transpose(tok_ps[:, n, :], lt[:, n * P:(n + 1) * P], g.const("ident")[0:E, 0:E])
            mm.then_inc(turned, 1)
            pe.wait_ge(ready, 1)
            for n in range(NTOK):
                mm = pe.transpose(logit_ps[:, n * P:(n + 1) * P], p[:, n, :], g.const("ident"))
                if n % 4 == 3:
                    mm.then_inc(back, 1)

        @block.scalar
        def _(act):
            for t in range(NT):
                act.wait_ge(logits, t + 1)
                act.activation(lt[:, t * TT:(t + 1) * TT], logit_ps[:, t * TT:(t + 1) * TT], ACT.Copy).then_inc(copied, 1)
            act.wait_ge(shifted, 1)
            act.activation(p[:, :, :], p[:, :, :], ACT.Exp).then_inc(exped, 1)
            for t in range(NT):
                act.wait_ge(back, t + 1)
                act.activation(ct[:, t * TT:(t + 1) * TT], logit_ps[:, t * TT:(t + 1) * TT], ACT.Copy).then_inc(ct_ready, 1)

        @block.vector
        def _(dve):
            step = Chain(dve, step_sem)
            full, small = [P, NTOK, E, E], [P, NTOK, E]
            dve.wait_ge(turned, 1)
            step(dve.tensor_reduce(m[:, :], tok_ps[:, :, :], AX.X, ALU.max))
            dve.tensor_tensor(p[:, :, :], tok_ps[:, :, :], bc(m[:, :], 2, small), ALU.subtract).then_inc(shifted, 1)
            dve.wait_ge(exped, 1)
            step(dve.tensor_reduce(m[:, :], p[:, :, :], AX.X, ALU.add))
            step(dve.reciprocal(m[:, :], m[:, :]))
            step(dve.tensor_tensor(p[:, :, :], p[:, :, :], bc(m[:, :], 2, small), ALU.mult))
            other, mine = bc(p[:, :, :], 2, full), bc(p[:, :, :], 3, full)
            dve.tensor_tensor(big[0][:, :, :, :], other, mine, ALU.is_gt)
            step(dve.tensor_tensor(big[1][:, :, :, :], other, mine, ALU.is_equal))
            step(dve.tensor_tensor(big[1][:, :, :, :].rearrange("p n e f -> p n (e f)"),
                                   big[1][:, :, :, :].rearrange("p n e f -> p n (e f)"),
                                   bc(g.const("expert_lt"), 1, [P, NTOK, E * E]), ALU.mult))
            step(dve.tensor_tensor(big[0][:, :, :, :], big[0][:, :, :, :], big[1][:, :, :, :], ALU.add))
            step(dve.tensor_reduce(rank[:, :, :], big[0][:, :, :, :], AX.X, ALU.add))
            step(dve.tensor_scalar(rank[:, :, :], rank[:, :, :], TOP_K - 0.5, None, ALU.is_lt))
            step(dve.tensor_tensor(p[:, :, :], p[:, :, :], rank[:, :, :], ALU.mult))
            step(dve.tensor_reduce(m[:, :], p[:, :, :], AX.X, ALU.add))
            step(dve.reciprocal(m[:, :], m[:, :]))
            dve.tensor_tensor(p[:, :, :], p[:, :, :], bc(m[:, :], 2, small), ALU.mult).then_inc(ready, 1)


def decode_fp4(dve, step, g, raw, tmp):
    step(dve.tensor_scalar(raw, raw, g.shift[:, 0:1], None, ALU.logical_shift_left))
    step(dve.tensor_scalar(tmp, raw, g.shift[:, 1:2], g.shift[:, 2:3], ALU.logical_shift_right, ALU.bitwise_and))
    step(dve.scalar_tensor_tensor(raw, raw, g.shift[:, 3:4], tmp, ALU.bitwise_and, ALU.bitwise_or))


FP8_GAIN = 64.0


def experts(nc, g, a):
    N_GU, N_D = 2 * I_MOE, D
    NO = 2 * G_I
    PER = NT * G_I
    T_RING, G_RING, Y_RING = 4, 6, 2
    DOWN_AT = {2: (0,), 3: (1,), 4: (2,), 5: (3,)}
    Y_CREDIT = 5
    with ExitStack() as ctx:
        def sb(name, shape, dt=F32):
            return ctx.enter_context(nc.sbuf_tensor(f"x_{name}", shape, dt))

        def sem(name):
            return ctx.enter_context(nc.semaphore("x_" + name))

        x_hi, x_lo = sb("x_hi", [P, C, T], F32R), sb("x_lo", [P, C, T], F32R)
        raw_gu, raw_d = sb("raw_gu", [P, G_D, N_GU // 4], I32), sb("raw_d", [P, G_I, N_D // 4], I32)
        tmp = sb("tmp", [P, G_D, N_GU // 4], I32)
        mark, mark_act = sb("mark", [P, 1], I32), sb("mark_act", [P, 1])
        w_gu = [sb(f"w_gu{u}", [P, G_D, N_GU], F32R) for u in range(2)]
        s_gu = sb("s_gu", [P, E_ROUTED + 1, NO, G_D])
        s_gu_now = sb("s_gu_now", [P, 2, NO, G_D])
        w_d = sb("w_d", [P, G_I, N_D])
        d_hi, d_lo = sb("d_hi", [P, G_I, N_D], F32R), sb("d_lo", [P, G_I, N_D], F32R)
        part = [[sb(f"part{k}{j}", [P, TT]) for j in range(2)] for k in range(T_RING)]
        h = [sb(f"h{i}", [P, TT]) for i in range(2)]
        h_hi = [sb(f"h_hi{i}", [P, G_I, TT], F32R) for i in range(2)]
        h_lo = [sb(f"h_lo{i}", [P, G_I, TT], F32R) for i in range(2)]
        cmb = [sb(f"cmb{i}", [P, TT]) for i in range(2)]
        group_ps = [ctx.enter_context(nc.psum_tensor(f"x_group{i}", [P, TT], F32)) for i in range(G_RING)]
        y_ps = [ctx.enter_context(nc.psum_tensor(f"x_y{i}", [P, TT], F32)) for i in range(Y_RING)]
        raw_landed, sc_landed, x_high, x_ready = sem("raw_landed"), sem("sc_landed"), sem("x_high"), sem("x_ready")
        cmb_landed = [sem(f"cmb_landed{i}") for i in range(2)]
        gu_half = sem("gu_half")
        decoded, gu_ready, wd_ready, d_high, d_ready, step_sem, scales_ready = (
            sem(n) for n in ("decoded", "gu_ready", "wd_ready", "d_high", "d_ready", "step", "scales_ready"))
        group_done, ev_act, ev_dve, summed, silu_done, weighted, h_done, h_high, h_ready, y_done, y_added = (
            sem(n) for n in ("group_done", "ev_act", "ev_dve", "summed", "silu_done", "weighted", "h_done", "h_high",
                             "h_ready", "y_done", "y_added"))
        block = ctx.enter_context(nc.Block())

        def each_tile(eng, output, product, down, between):
            def tile(tau, e, u, t, first=False):
                for o in range(NO):
                    output(tau, e, u, t, o)
                    if o:
                        if o % 2 == 0:
                            product(tau, t, o // 2 - 1)
                    elif not first:
                        product(tau - 1, (t - 1) % NT, G_I - 1)
                    if not first:
                        for c in DOWN_AT.get(o, ()):
                            down(tau - 1, (t - 1) % NT, c)
                between(e, u, t)

            tile(0, 0, 0, 0, first=True)
            with eng.Fori(0, E_ROUTED // 2) as i:
                for k in range(1, 2 * NT + 1):
                    tile(2 * NT * i + k, 2 * i + k // NT, k // NT % 2, k % NT)
            last = E_ROUTED * NT
            for k in range(1, NT):
                tile(last + k, E_ROUTED, 0, k)
            product(last + NT - 1, NT - 1, G_I - 1)
            for c in range(C):
                down(last + NT - 1, NT - 1, c)

        def nothing(*_):
            pass

        def more(e):
            return not (isinstance(e, int) and e == E_ROUTED)

        def part_of(t, o):
            return (t * NO + o) % T_RING

        @block.sync
        def _(sp):
            def raw(e):
                for half in range(2):
                    r = slice(64 * half, 64 * half + 64)
                    sp.dma_start(raw_gu[r, :, :], a["gu"][bass.ds(e, 1)].rearrange("o r g n -> (o r) g n"))\
                      .then_inc(raw_landed, 16)
                    sp.dma_start(raw_d[r, :, :], a["d"][bass.ds(e, 1)].rearrange("o r g n -> (o r) g n"))\
                      .then_inc(raw_landed, 16)

            def scales(e):
                sp.dma_start(w_d[:, :, :].rearrange("p g n -> p (g n)"),
                             a["d_s"][bass.ds(e, 1), :].to_broadcast([P, G_I * N_D])).then_inc(sc_landed, 16)

            def weights_of(tau, t):
                sp.wait_ge(weighted, G_I * tau + G_I)
                sp.dma_start(cmb[t % 2][:, :], g.combine_dram[bass.ds(tau // NT if isinstance(tau, int) else tau_e[0], 1),
                                                              t * TT:(t + 1) * TT].to_broadcast([P, TT]))\
                  .then_inc(cmb_landed[t % 2], 16)

            tau_e = [None]

            def expert(e, raw_after, scales_after):
                tau_e[0] = e
                weights_of(NT * e, 0)
                weights_of(NT * e + 1, 1)
                if scales_after:
                    sp.wait_ge(d_ready, e + 1)
                    scales(e + 1)
                weights_of(NT * e + 2, 2)
                weights_of(NT * e + 3, 3)
                if raw_after:
                    sp.wait_ge(gu_ready, e + 2)
                    sp.wait_ge(wd_ready, e + 2)
                    raw(e + 2)

            sp.dma_start(s_gu[:, :, :, :], a["gu_s"]).then_inc(scales_ready, 16)
            raw(0)
            scales(0)
            sp.wait_ge(gu_ready, 1)
            sp.wait_ge(wd_ready, 1)
            raw(1)
            with sp.Fori(0, E_ROUTED - 1) as e:
                expert(e, True, True)
            expert(E_ROUTED - 1, False, True)
            expert(E_ROUTED, False, False)

        @block.tensor
        def _(pe):
            pe.sem_inc(y_done, Y_CREDIT)

            def output(tau, e, u, t, o):
                G = NO * tau + o
                if t == 0 and o == 0:
                    pe.wait_ge(gu_ready, e + 1)
                if isinstance(e, int) and e == 0 and o == 0:
                    pe.wait_ge(x_ready, t + 1)
                elif t > 0 and o == 0:
                    pe.wait_ge(x_ready, NT)
                col = (o % 2) * I_MOE + (o // 2) * P
                for q in range(G_D):
                    pe.wait_ge(*((ev_dve, 2 * G + q + 1) if q < 2 else (ev_act, 2 * G + q - 1)))
                    out = group_ps[(o * G_D + q) % G_RING]
                    for k, x in enumerate((x_hi, x_lo)):
                        mm = pe.matmul(out[:, :], w_gu[u][:, q, col:col + P], x[:, q, t * TT:(t + 1) * TT],
                                       start=k == 0, stop=k == 1)
                    mm.then_inc(group_done, 1)

            def down(tau, t, c):
                if c == 0:
                    pe.wait_ge(h_ready, G_I * tau + G_I + 2)
                    if t == 0:
                        pe.wait_ge(d_ready, tau_expert(tau) + 1)
                pe.wait_ge(y_added, C * tau + c + 1)
                n = 0
                for k in range(G_I):
                    for w, x in ((d_hi, h_hi), (d_hi, h_lo), (d_lo, h_hi)):
                        mm = pe.matmul(y_ps[c % Y_RING][:, :], w[:, k, c * P:(c + 1) * P], x[t % 2][:, k, :],
                                       start=n == 0, stop=n == 3 * G_I - 1)
                        n += 1
                mm.then_inc(y_done, 1)

            expert_now = [0]

            def tau_expert(tau):
                return expert_now[0]

            def between(e, u, t):
                expert_now[0] = e

            each_tile(pe, output, nothing, down, between)

        @block.scalar
        def _(act):
            for t in range(NT):
                cols = slice(t * TT, (t + 1) * TT)
                act.activation(x_hi[:, :, cols], g.xt[:, :, cols], ACT.Copy).then_inc(x_high, 1)
                if t == 0:
                    convert_first = True
            act.sem_inc(ev_act, 2)

            def convert(e, u, groups):
                act.wait_ge(decoded, e + 1)
                act.activation(mark_act[:, :], raw_gu[:, 0, 0:1].bitcast(F32), ACT.Copy)
                act.activation(w_gu[u][:, groups, :], raw_gu[:, groups, :].bitcast(F8), ACT.Copy, scale=FP8_GAIN)\
                   .then_inc(gu_half, 1)

            def output(tau, e, u, t, o):
                G = NO * tau + o
                k = part_of(t, o)
                if t == 0 and o == 0:
                    act.wait_ge(scales_ready, e + 17)
                act.wait_ge(h_done, G_I * tau + o // 2 + 1)
                for j in range(2):
                    act.wait_ge(group_done, G_D * G + j + 1)
                    act.activation(part[k][j][:, :], group_ps[(o * G_D + j) % G_RING][:, :], ACT.Copy,
                                   scale=s_gu_now[:, u, o, j:j + 1]).then_inc(ev_act, 1)
                if o % 2:
                    act.wait_ge(summed, G)
                    x = part[part_of(t, o - 1)][0]
                    act.activation(x[:, :], x[:, :], ACT.Silu).then_inc(silu_done, 1)

            def product(tau, t, n):
                N = G_I * tau + n
                act.wait_ge(h_done, N + 3)
                act.wait_ge(y_done, C * tau + 1)
                act.activation(h_hi[t % 2][:, n, :], h[(t * G_I + n) % 2][:, :], ACT.Copy).then_inc(h_high, 1)

            def split_down(e):
                act.wait_ge(wd_ready, e + 1)
                act.wait_ge(y_done, NT * C * e + Y_CREDIT)
                act.activation(d_hi[:, :, :], w_d[:, :, :], ACT.Copy).then_inc(d_high, 1)

            def between(e, u, t):
                if t == 0:
                    split_down(e)
                if t >= 2 and more(e):
                    convert(e + 1, 1 - u, slice(2 * t - 4, 2 * t - 2))
                if t == 3 and more(e):
                    act.wait_ge(gu_half, 2 * e + 4)
                    act.sem_inc(gu_ready, 1)

            convert(0, 0, slice(0, G_D))
            act.wait_ge(gu_half, 1)
            act.sem_inc(gu_ready, 1)
            act.sem_inc(gu_half, 1)
            each_tile(act, output, product, nothing, between)

        @block.gpsimd
        def _(pool):
            pool.sem_inc(weighted, 2 * G_I)
            pool.sem_inc(h_ready, 2)

            def output(tau, e, u, t, o):
                G = NO * tau + o
                x = part[part_of(t, o)]
                pool.wait_ge(ev_dve, 2 * G + 6)
                pool.tensor_tensor(x[0][:, :], x[0][:, :], x[1][:, :], ALU.add).then_inc(summed, 1)
                if o % 2:
                    pool.wait_ge(silu_done, G_I * tau + o // 2 + 1)
                    if o == 1:
                        pool.wait_ge(cmb_landed[t % 2], landed_of(e, t))
                    x = part[part_of(t, o - 1)][0]
                    pool.tensor_tensor(x[:, :], x[:, :], cmb[t % 2][:, :], ALU.mult).then_inc(weighted, 1)

            def landed_of(e, t):
                return 32 * e + 16 * (t // 2) + 16

            def product(tau, t, n):
                pool.wait_ge(h_high, G_I * tau + n + 1)
                pool.tensor_tensor(h_lo[t % 2][:, n, :], h[(t * G_I + n) % 2][:, :],
                                   h_hi[t % 2][:, n, :].bitcast(F32), ALU.subtract).then_inc(h_ready, 1)

            each_tile(pool, output, product, nothing, nothing)

        @block.vector
        def _(dve):
            steps = 6

            def decode(e):
                step = Chain(dve, step_sem, e * steps)
                dve.wait_ge(raw_landed, 64 * e + 64)
                decode_fp4(dve, step, g, raw_gu[:, :, :], tmp[:, :, :])
                dve.sem_inc(decoded, 1)
                decode_fp4(dve, step, g, raw_d[:, :, :], tmp[:, 0:G_I, 0:N_D // 4])
                assert step.n == steps
                dve.wait_ge(sc_landed, 16 * e + 16)
                dve.tensor_copy(mark[:, :], raw_d[:, 0, 0:1])
                dve.scalar_tensor_tensor(w_d[:, :, :], raw_d[:, :, :].bitcast(F8), FP8_GAIN, w_d[:, :, :],
                                         ALU.mult, ALU.mult).then_inc(wd_ready, 1)

            def scales_now(e, u):
                dve.tensor_copy(s_gu_now[:, u, :, :], s_gu[:, bass.ds(e, 1), :, :].rearrange("p e o g -> p (e o) g"))\
                   .then_inc(scales_ready, 1)

            def output(tau, e, u, t, o):
                G = NO * tau + o
                k = part_of(t, o)
                if t == 0 and o == 0:
                    dve.wait_ge(scales_ready, e + 17)
                for j in range(2):
                    dve.wait_ge(group_done, G_D * G + j + 3)
                    dve.wait_ge(ev_act, 2 * G + j + 3)
                    x = part[k][j][:, :]
                    dve.scalar_tensor_tensor(x, group_ps[(o * G_D + 2 + j) % G_RING][:, :],
                                             s_gu_now[:, u, o, 2 + j:3 + j], x, ALU.mult, ALU.add).then_inc(ev_dve, 1)

            def product(tau, t, n):
                N = G_I * tau + n
                dve.wait_ge(weighted, N + 1 + 2 * G_I)
                dve.wait_ge(summed, 2 * N + 2)
                dve.wait_ge(h_ready, N + 1)
                gate, up = part[part_of(t, 2 * n)][0], part[part_of(t, 2 * n + 1)][0]
                dve.tensor_tensor(h[N_par(t, n)][:, :], gate[:, :], up[:, :], ALU.mult).then_inc(h_done, 1)

            def N_par(t, n):
                return (t * G_I + n) % 2

            def down(tau, t, c):
                dve.wait_ge(y_done, C * tau + c + 1 + Y_CREDIT)
                dve.wait_ge(y_added, C * tau + c + 1)
                x = g.xt[:, c, t * TT:(t + 1) * TT]
                dve.tensor_tensor(x, x, y_ps[c % Y_RING][:, :], ALU.add).then_inc(y_added, 1)

            def between(e, u, t):
                if t == 0:
                    dve.wait_ge(d_high, e + 1)
                    dve.tensor_tensor(d_lo[:, :, :], w_d[:, :, :], d_hi[:, :, :].bitcast(F32), ALU.subtract)\
                       .then_inc(d_ready, 1)
                if t == 1 and more(e):
                    decode(e + 1)
                if t == 3 and more(e):
                    dve.wait_ge(ev_act, scaled_of(e))
                    scales_now(e + 1, 1 - u)

            def scaled_of(e):
                return 2 * NO * NT * e + 2

            dve.wait_ge(scales_ready, 16)
            dve.sem_inc(ev_dve, 4)
            dve.sem_inc(h_done, 2)
            dve.sem_inc(y_added, Y_RING)
            decode(0)
            scales_now(0, 0)
            for t in range(NT):
                cols = slice(t * TT, (t + 1) * TT)
                dve.wait_ge(x_high, t + 1)
                dve.tensor_tensor(x_lo[:, :, cols], g.xt[:, :, cols], x_hi[:, :, cols].bitcast(F32), ALU.subtract)\
                   .then_inc(x_ready, 1)
            dve.wait_ge(x_ready, NT)
            each_tile(dve, output, product, down, between)


LAG = 2
RING = 8
X_RING = 16


def causal_attention(nc, g, a):
    with ExitStack() as ctx:
        def sb(name, shape, dt=F32):
            return ctx.enter_context(nc.sbuf_tensor("c_" + name, shape, dt))

        def sem(name):
            return ctx.enter_context(nc.semaphore("c_" + name))

        def ps(name, shape):
            return ctx.enter_context(nc.psum_tensor("c_" + name, shape, F32))

        w = {n: sb(n, [P, C, D]) for n in ("wq", "wqr", "wk", "wkr", "wv", "wo")}
        bias = {n: sb(n, [P, C]) for n in ("bq", "bqr", "bk", "bkr", "bo")}
        bv = sb("bv", [P, D])
        rope = sb("rope", [P, 2, D])
        xb = sb("xb", [P, C, S])
        q_sb, k_sb = sb("q", [P, C, S]), sb("k", [P, C, S])
        sq, sk = sb("sq", [P, C, S]), sb("sk", [P, C, S])
        nrm = sb("nrm", [P, 2, S])
        kp = [sb(f"kp{j}", [P, C, S]) for j in range(4)]
        v_sb = sb("v", [P, 2, D])
        pt = [sb(f"pt{i}", [P, 3, P]) for i in range(RING)]
        rec = sb("rec", [P, C, S])
        at = sb("at", [P, C, S])
        q_ps, k_ps = ps("q_ps", [P, C, S]), ps("k_ps", [P, C, S])
        v_ps = ps("v_ps", [P, 2, D])
        s_ps = [ps(f"s{i}", [P, 3, P]) for i in range(2)]
        n_ps = v_ps[:, 0, :].rearrange("p (n s) -> p n s", n=2)
        o_ps = v_ps[:, :, :].rearrange("p a (b s) -> p (a b) s", b=2)
        logged, inverted = sem("logged"), sem("inverted")
        (loaded, folded, xb_ready, q_done, k_done, v_done, sq_ready, v_ready, n_done, n_root, qk_ready, s_done, exped,
         masked, av_done, at_ready, o_done, added, step_sem) = (
            sem(n) for n in ("loaded", "folded", "xb_ready", "q_done", "k_done", "v_done", "sq_ready", "v_ready",
                             "n_done", "n_root", "qk_ready", "s_done", "exped", "masked", "av_done", "at_ready",
                             "o_done", "added", "step"))
        LOADS = 13
        block = ctx.enter_context(nc.Block())

        @block.sync
        def _(sp):
            for n in w:
                sp.dma_start(w[n][:, :, :], a[n + "1"]).then_inc(loaded, 16)
            for n in bias:
                sp.dma_start(bias[n][:, :], a[n + "1"]).then_inc(loaded, 16)
            sp.dma_start(bv[:, :], a["bv1"].to_broadcast([P, D])).then_inc(loaded, 16)
            sp.dma_start(rope[:, :, :].rearrange("p a n -> p (a n)"), a["rope"].to_broadcast([P, 2 * D]))\
              .then_inc(loaded, 16)

        @block.gpsimd
        def _(pool):
            pool.wait_ge(loaded, 16 * LOADS)
            with pool.Fori(0, B) as b:
                pool.wait_ge(v_done, b + 1)
                pool.tensor_copy(xb[:, :, :], g.xt[:, :, bass.ts(b, S)]).then_inc(xb_ready, 1)
                for h in range(H1):
                    pool.wait_ge(exped, H1 * b + h + 3)
                    diagonal = pt[h % RING][:, 0:3:2, :]
                    pool.tensor_tensor(diagonal, diagonal, bc(g.const("causal"), 1, [P, 2, P]), ALU.mult)\
                        .then_inc(masked, 1)

        @block.tensor
        def _(pe):
            pe.wait_ge(folded, 1)
            pe.sem_inc(v_done, 1)
            pe.sem_inc(n_done, 1)
            with pe.Fori(0, B) as b:
                pe.wait_ge(xb_ready, b + 1)
                pe.wait_ge(at_ready, b + 1)
                for x, y, done in (("wq", q_ps, q_done), ("wk", k_ps, k_done)):
                    for m in range(C):
                        for c in range(C):
                            mm = pe.matmul(y[:, m, :], w[x][:, c, m * P:(m + 1) * P], xb[:, c, :],
                                           start=c == 0, stop=c == C - 1)
                    mm.then_inc(done, 1)
                pe.wait_ge(added, b + 1)
                for k in range(2):
                    for c in range(C):
                        mm = pe.matmul(v_ps[:, k, :], xb[:, c, k * P:(k + 1) * P], w["wv"][:, c, :],
                                       start=c == 0, stop=c == C - 1)
                mm.then_inc(v_done, 1)
                pe.wait_ge(v_ready, b + 1)
                for n, x in enumerate((sq, sk)):
                    pe.wait_ge(sq_ready, 2 * b + n + 1)
                    for c in range(C):
                        mm = pe.matmul(n_ps[:, n, :], g.const("ones"), x[:, c, :], start=c == 0, stop=c == C - 1)
                mm.then_inc(n_done, 1)

                def score(h):
                    c, j = h // 4, h % 4
                    pe.wait_ge(exped, H1 * b + h + 1)
                    pe.matmul(s_ps[h % 2][:, 0:2, :], kp[j][:, c, 0:P], q_sb[:, c, :], start=True, stop=True)
                    pe.matmul(s_ps[h % 2][:, 2, :], kp[j][:, c, P:S], q_sb[:, c, P:S], start=True, stop=True)\
                      .then_inc(s_done, 1)

                def values(c):
                    pe.wait_ge(masked, H1 * b + 4 * c + 4)
                    for y in (q_ps, k_ps):
                        for k in range(2):
                            for j in range(4):
                                h = 4 * c + j
                                r = slice(32 * j, 32 * j + 32)
                                x, w = pt[h % RING], g.const("ones")[:, 0:32]
                                if y is q_ps:
                                    w = v_sb[:, k, h * HD1:(h + 1) * HD1]
                                if k == 0:
                                    pe.matmul(y[r, c, :], w, x[:, 0:2, :], start=True, stop=False,
                                              skip_group_check=True)
                                else:
                                    mm = pe.matmul(y[r, c, P:S], w, x[:, 2, :], start=False, stop=True,
                                                   skip_group_check=True)
                    mm.then_inc(av_done, 4)

                pe.wait_ge(qk_ready, b + 1)
                for h in range(H1 + LAG):
                    if h < H1:
                        score(h)
                    if h >= LAG and (h - LAG) % 4 == 3:
                        values((h - LAG) // 4)
                pe.wait_ge(at_ready, b + 2)
                for m in range(C):
                    for c in range(C):
                        mm = pe.matmul(o_ps[:, m, :], w["wo"][:, c, m * P:(m + 1) * P], at[:, c, :],
                                       start=c == 0, stop=c == C - 1)
                mm.then_inc(o_done, 1)

        @block.scalar
        def _(act):
            act.wait_ge(folded, 1)
            act.sem_inc(exped, 2)
            with act.Fori(0, B) as b:
                for y, x, s2, bn, done, k in ((q_ps, q_sb, sq, "bq", q_done, 0), (k_ps, k_sb, sk, "bk", k_done, 1)):
                    act.wait_ge(done, b + 1)
                    act.wait_ge(n_done, b + 1)
                    for m in range(C):
                        act.activation(s2[:, m, :], y[:, m, :], ACT.Square, bias=bias[bn][:, m:m + 1])
                        last = act.activation(x[:, m, :], y[:, m, :], ACT.Identity, bias=bias[bn][:, m:m + 1])
                    last.then_inc(sq_ready, 1)
                act.wait_ge(n_done, b + 2)
                act.activation(nrm[:, :, :], n_ps, ACT.Sqrt).then_inc(n_root, 1)
                for h in range(H1):
                    act.wait_ge(s_done, H1 * b + h + 1)
                    act.wait_ge(av_done, H1 * b + h + 1)
                    act.activation(pt[h % RING][:, :, :], s_ps[h % 2][:, :, :], ACT.Exp).then_inc(exped, 1)
                act.wait_ge(av_done, H1 * b + H1 + RING)
                act.activation(rec[:, :, :], k_ps[:, :, :], ACT.Ln).then_inc(logged, 1)
                act.wait_ge(logged, b + 1)
                act.activation(rec[:, :, :], rec[:, :, :], ACT.Exp, scale=-1.0).then_inc(inverted, 1)

        @block.vector
        def _(dve):
            dve.sem_inc(av_done, RING)
            dve.sem_inc(at_ready, 1)
            dve.sem_inc(added, 1)
            dve.wait_ge(loaded, 16 * LOADS)
            cos, sin = (bc(rope[:, n, :], 1, [P, C, D]) for n in range(2))
            fold = 3
            base = 2 * fold
            step = Chain(dve, step_sem)
            for x in ("q", "k"):
                wx, wr, bx, br = w["w" + x][:, :, :], w["w" + x + "r"][:, :, :], bias["b" + x][:, :], bias["b" + x + "r"][:, :]
                dve.tensor_tensor(wx, wx, cos, ALU.mult)
                dve.tensor_tensor(bx, bx, g.const("cosc"), ALU.mult)
                dve.tensor_tensor(br, br, g.const("sinc"), ALU.mult)
                step(dve.tensor_tensor(wr, wr, sin, ALU.mult))
                dve.tensor_tensor(wx, wx, wr, ALU.add)
                step(dve.tensor_tensor(bx, bx, br, ALU.add))
            dve.sem_inc(folded, 1)
            base = step.n
            steps = 4
            with dve.Fori(0, B) as b:
                step = Chain(dve, step_sem, b * steps + base)
                dve.wait_ge(v_done, b + 2)
                dve.tensor_tensor(v_sb[:, :, :], v_ps[:, :, :], bc(bv[:, :], 1, [P, 2, D]), ALU.add).then_inc(v_ready, 1)
                dve.wait_ge(n_root, b + 1)
                step(dve.tensor_scalar(nrm[:, :, :], nrm[:, :, :], 1e-12, None, ALU.max))
                step(dve.reciprocal(nrm[:, :, :], nrm[:, :, :]))
                dve.tensor_tensor(q_sb[:, :, :], q_sb[:, :, :], bc(nrm[:, 0, :], 1, [P, C, S]), ALU.mult)
                for j in range(4):
                    last = dve.scalar_tensor_tensor(kp[j][:, :, :], k_sb[:, :, :], g.const("head4")[:, j:j + 1],
                                                    bc(nrm[:, 1, :], 1, [P, C, S]), ALU.mult, ALU.mult)
                step(last)
                dve.sem_inc(qk_ready, 1)
                dve.wait_ge(inverted, b + 1)
                step(dve.tensor_tensor(at[:, :, :], q_ps[:, :, :], rec[:, :, :], ALU.mult))
                dve.sem_inc(at_ready, 1)
                assert step.n == steps
                dve.wait_ge(o_done, b + 1)
                for m in range(C):
                    x = g.xt[:, m, bass.ts(b, S)]
                    last = dve.scalar_tensor_tensor(x, o_ps[:, m, :], bias["bo"][:, m:m + 1], x, ALU.add, ALU.add)
                last.then_inc(added, 1)


def cross_attention(nc, g, a):
    with ExitStack() as ctx:
        def sb(name, shape, dt=F32):
            return ctx.enter_context(nc.sbuf_tensor("y_" + name, shape, dt))

        def sem(name):
            return ctx.enter_context(nc.semaphore("y_" + name))

        def ps(name, shape):
            return ctx.enter_context(nc.psum_tensor("y_" + name, shape, F32))

        wq, wk, wv = (sb(n, [P, C, D]) for n in ("wq", "wk", "wv"))
        cb = sb("cb", [P, C, S])
        q_sb, k_sb = sb("q", [P, C, S]), sb("k", [P, C, S])
        sq, sk = sb("sq", [P, C, S]), sb("sk", [P, C, S])
        kp = [sb(f"kp{j}", [P, C, S]) for j in range(8)]
        vp = [sb(f"vp{j}", [P, 2, HX // 2, 2, HDX]) for j in range(2)]
        pt = [sb(f"pt{i}", [P, 2, S]) for i in range(X_RING)]
        at = sb("at", [P, C, S])
        q_ps, k_ps = ps("q_ps", [P, C, S]), ps("k_ps", [P, C, S])
        v_ps = ps("v_ps", [P, 2, D])
        s_ps = ps("s_ps", [P, 2, 2, S])
        nq_ps = v_ps[:, :, :].rearrange("p a (b s) -> p (a b) s", b=2)
        nk_ps = s_ps[:, :, :, :].rearrange("p a b s -> p (a b) s")
        o_ps = nq_ps
        logged, inverted = sem("logged"), sem("inverted")
        (loaded, zeroed, cb_ready, q_done, k_done, v_done, sq_ready, v_ready, n_done, n_root, qk_ready, s_done, exped,
         av_done, at_ready, o_done, added, step_sem) = (
            sem(n) for n in ("loaded", "zeroed", "cb_ready", "q_done", "k_done", "v_done", "sq_ready", "v_ready",
                             "n_done", "n_root", "qk_ready", "s_done", "exped", "av_done", "at_ready",
                             "o_done", "added", "step"))
        eps = g.const("eps")[:, 1:2]
        block = ctx.enter_context(nc.Block())

        @block.sync
        def _(sp):
            for dst, src in ((wq[:, :, :], a["wqx"]), (wk[:, :, :], a["wkx"]), (wv[:, :, :], a["wvx"]), (g.aux[:, :, :], a["ct"])):
                sp.dma_start(dst, src).then_inc(loaded, 16)

        @block.gpsimd
        def _(pool):
            for j in range(2):
                pool.memset(vp[j][:, :, :, :, :], 0.0).then_inc(zeroed, 1)
            pool.wait_ge(loaded, 64)
            with pool.Fori(0, B) as b:
                pool.wait_ge(v_done, b + 1)
                pool.tensor_copy(cb[:, :, :], g.aux[:, :, bass.ts(b, S)]).then_inc(cb_ready, 1)

        @block.tensor
        def _(pe):
            pe.wait_ge(loaded, 64)
            pe.sem_inc(v_done, 1)
            with pe.Fori(0, B) as b:
                pe.wait_ge(at_ready, b + 1)
                for m in range(C):
                    for c in range(C):
                        mm = pe.matmul(q_ps[:, m, :], wq[:, c, m * P:(m + 1) * P], g.xt[:, c, bass.ts(b, S)],
                                       start=c == 0, stop=c == C - 1)
                mm.then_inc(q_done, 1)
                pe.wait_ge(cb_ready, b + 1)
                for m in range(C):
                    for c in range(C):
                        mm = pe.matmul(k_ps[:, m, :], wk[:, c, m * P:(m + 1) * P], cb[:, c, :],
                                       start=c == 0, stop=c == C - 1)
                mm.then_inc(k_done, 1)
                pe.wait_ge(added, b + 1)
                for k in range(2):
                    for c in range(C):
                        mm = pe.matmul(v_ps[:, k, :], cb[:, c, k * P:(k + 1) * P], wv[:, c, :],
                                       start=c == 0, stop=c == C - 1)
                mm.then_inc(v_done, 1)
                pe.wait_ge(v_ready, b + 1)
                pe.wait_ge(exped, HX * b + 2)
                for n, (x, y) in enumerate(((sq, nq_ps), (sk, nk_ps))):
                    pe.wait_ge(sq_ready, 2 * b + n + 1)
                    for c in range(C):
                        mm = pe.matmul(y[:, c, :], g.const("blk16"), x[:, c, :], start=True, stop=True)
                    mm.then_inc(n_done, 1)

                def score(h):
                    c, j = h // 8, h % 8
                    pe.wait_ge(exped, HX * b + h + 1)
                    for k in range(2):
                        mm = pe.matmul(s_ps[:, h % 2, k, :], kp[j][:, c, k * P:(k + 1) * P], q_sb[:, c, :],
                                       start=True, stop=True)
                    mm.then_inc(s_done, 1)

                def values(c):
                    pe.wait_ge(exped, HX * b + 8 * c + 8 + 2)
                    for y in (q_ps, k_ps):
                        for e in range(2):
                            for k in range(2):
                                for j in range(4):
                                    pair = 4 * c + j
                                    w = g.const("den16")[:, 32 * e:32 * e + 32]
                                    if y is q_ps:
                                        w = vp[e][:, k, pair, :, :]
                                    mm = pe.matmul(y[32 * j:32 * j + 32, c, :], w, pt[(2 * pair + e) % X_RING][:, k, :],
                                                   start=e == 0 and k == 0, stop=e == 1 and k == 1,
                                                   skip_group_check=True)
                    mm.then_inc(av_done, 8)

                pe.wait_ge(qk_ready, b + 1)
                for h in range(HX + LAG):
                    if h < HX:
                        score(h)
                    if h >= LAG and (h - LAG) % 8 == 7:
                        values((h - LAG) // 8)
                pe.wait_ge(at_ready, b + 2)
                for m in range(C):
                    mm = pe.matmul(o_ps[:, m, :], g.const("perm"), at[:, m, :], start=True, stop=True)
                mm.then_inc(o_done, 1)

        @block.scalar
        def _(act):
            act.sem_inc(exped, 2)
            with act.Fori(0, B) as b:
                for y, x, s2, done in ((q_ps, q_sb, sq, q_done), (k_ps, k_sb, sk, k_done)):
                    act.wait_ge(done, b + 1)
                    act.activation(s2[:, :, :], y[:, :, :], ACT.Square)
                    act.activation(x[:, :, :], y[:, :, :], ACT.Copy).then_inc(sq_ready, 1)
                for n, (s2, y) in enumerate(((sq, nq_ps), (sk, nk_ps))):
                    act.wait_ge(n_done, 2 * b + n + 1)
                    act.activation(s2[:, :, :], y, ACT.Ln, bias=eps).then_inc(logged, 1)
                    act.wait_ge(logged, 3 * b + n + 1)
                    act.activation(s2[:, :, :], s2[:, :, :], ACT.Exp, scale=-0.5).then_inc(n_root, 1)
                for h in range(HX):
                    act.wait_ge(s_done, HX * b + h + 1)
                    act.wait_ge(av_done, HX * b + h + 1)
                    act.activation(pt[h % X_RING][:, :, :], s_ps[:, h % 2, :, :], ACT.Exp, scale=HDX ** -0.5)\
                       .then_inc(exped, 1)
                act.wait_ge(av_done, HX * b + HX + X_RING)
                act.activation(sq[:, :, :], k_ps[:, :, :], ACT.Ln).then_inc(logged, 1)
                act.wait_ge(logged, 3 * b + 3)
                act.activation(sq[:, :, :], sq[:, :, :], ACT.Exp, scale=-1.0).then_inc(inverted, 1)

        @block.vector
        def _(dve):
            dve.sem_inc(av_done, X_RING)
            dve.sem_inc(at_ready, 1)
            dve.sem_inc(added, 1)
            dve.wait_ge(zeroed, 2)
            steps = 4
            with dve.Fori(0, B) as b:
                step = Chain(dve, step_sem, b * steps)
                dve.wait_ge(v_done, b + 2)
                v = v_ps[:, :, :].rearrange("p k (n e d) -> p k n e d", e=2, d=HDX)
                for e in range(2):
                    last = dve.tensor_copy(vp[e][:, :, :, e, :], v[:, :, :, e, :])
                last.then_inc(v_ready, 1)
                for n, (x, s2) in enumerate(((q_sb, sq), (k_sb, sk))):
                    dve.wait_ge(n_root, 2 * b + n + 1)
                    step(dve.tensor_tensor(x[:, :, :], x[:, :, :], s2[:, :, :], ALU.mult))
                for j in range(8):
                    last = dve.tensor_scalar(kp[j][:, :, :], k_sb[:, :, :], g.const("head8")[:, j:j + 1], None, ALU.mult)
                step(last)
                dve.sem_inc(qk_ready, 1)
                dve.wait_ge(inverted, b + 1)
                step(dve.tensor_tensor(at[:, :, :], q_ps[:, :, :], sq[:, :, :], ALU.mult))
                dve.sem_inc(at_ready, 1)
                assert step.n == steps
                dve.wait_ge(o_done, b + 1)
                x = g.xt[:, :, bass.ts(b, S)]
                dve.tensor_tensor(x, o_ps, x, ALU.add).then_inc(added, 1)


def feed_forward(nc, g, a):
    N_GU = 2 * I_FFN
    PIECE = 2816
    N_PIECES_GU, N_PIECES = C * N_GU // PIECE, (C * N_GU + G_F * D) // PIECE
    assert C * N_GU % PIECE == 0 and G_F * D % PIECE == 0
    with ExitStack() as ctx:
        def sb(name, shape, dt=F32):
            return ctx.enter_context(nc.sbuf_tensor("f_" + name, shape, dt))

        def sem(name):
            return ctx.enter_context(nc.semaphore("f_" + name))

        def ps(name, shape):
            return ctx.enter_context(nc.psum_tensor("f_" + name, shape, F32))

        w_gu, w_d = sb("w_gu", [P, C, N_GU]), sb("w_d", [P, G_F, D])
        raw = [sb(f"raw{i}", [P, PIECE // 4], I32) for i in range(2)]
        tmp = sb("tmp", [P, PIECE // 4], I32)
        sc = [sb(f"sc{i}", [P, PIECE], F16) for i in range(2)]
        silu = [sb(f"silu{i}", [P, TT]) for i in range(2)]
        h = [sb(f"h{i}", [P, TT]) for i in range(2)]
        gate_ps = [ps(f"gate{i}", [P, TT]) for i in range(2)]
        up_ps = [ps(f"up{i}", [P, TT]) for i in range(2)]
        y_ps = ps("y", [P, C, TT])
        landed = [sem(f"landed{i}") for i in range(2)]
        piece_ready, gu_done, silu_done, h_ready, h_used, y_copied, step_sem = (
            sem(n) for n in ("piece_ready", "gu_done", "silu_done", "h_ready", "h_used", "y_copied", "step"))
        block = ctx.enter_context(nc.Block())

        @block.sync
        def _(sp):
            for n in range(N_PIECES):
                if n >= 2:
                    sp.wait_ge(piece_ready, n - 1)
                cols = slice(n * PIECE // 4, (n + 1) * PIECE // 4)
                for half in range(2):
                    sp.dma_start(raw[n % 2][64 * half:64 * half + 64, :], a["ffn"][:, cols]).then_inc(landed[n % 2], 16)
                sp.dma_start(sc[n % 2][:, :], a["ffn_s"][:, n * PIECE:(n + 1) * PIECE].to_broadcast([P, PIECE]))\
                  .then_inc(landed[n % 2], 16)

        @block.tensor
        def _(pe):
            pe.wait_ge(piece_ready, N_PIECES)
            with pe.Fori(0, NT) as t:
                for n in range(G_F + 1):
                    if n < G_F:
                        pe.wait_ge(h_ready, t * G_F + max(n, 1) + 1)
                        for y, off in ((gate_ps[n % 2], 0), (up_ps[n % 2], I_FFN)):
                            for c in range(C):
                                mm = pe.matmul(y[:, :], w_gu[:, c, off + n * P:off + (n + 1) * P],
                                               g.xt[:, c, bass.ts(t, TT)], start=c == 0, stop=c == C - 1)
                        mm.then_inc(gu_done, 1)
                    if n >= 1:
                        m = n - 1
                        pe.wait_ge(h_ready, t * G_F + m + 3)
                        if m == 0:
                            pe.wait_ge(y_copied, t + 1)
                        for k in range(C):
                            mm = pe.matmul(y_ps[:, k, :], w_d[:, m, k * P:(k + 1) * P], h[m % 2][:, :],
                                           start=m == 0, stop=m == G_F - 1)
                        mm.then_inc(h_used, 1)

        @block.scalar
        def _(act):
            act.sem_inc(y_copied, 1)
            with act.Fori(0, NT) as t:
                for n in range(G_F):
                    k = n % 2
                    act.wait_ge(gu_done, t * G_F + n + 1)
                    act.wait_ge(h_ready, t * G_F + max(n, 1) + 1)
                    act.activation(silu[k][:, :], gate_ps[k][:, :], ACT.Silu).then_inc(silu_done, 1)
                act.wait_ge(h_used, t * G_F + G_F + 2)
                act.activation(g.aux[:, :, bass.ts(t, TT)], y_ps[:, :, :], ACT.Copy).then_inc(y_copied, 1)

        @block.vector
        def _(dve):
            step = Chain(dve, step_sem)
            flat_gu = w_gu[:, :, :].rearrange("p c n -> p (c n)")
            flat_d = w_d[:, :, :].rearrange("p c n -> p (c n)")
            for n in range(N_PIECES):
                dve.wait_ge(landed[n % 2], 48 * (n // 2 + 1))
                decode_fp4(dve, step, g, raw[n % 2][:, :], tmp[:, :])
                m = n if n < N_PIECES_GU else n - N_PIECES_GU
                dst = (flat_gu if n < N_PIECES_GU else flat_d)[:, m * PIECE:(m + 1) * PIECE]
                dve.scalar_tensor_tensor(dst, raw[n % 2][:, :].bitcast(F8), FP8_GAIN, sc[n % 2][:, :],
                                         ALU.mult, ALU.mult).then_inc(piece_ready, 1)
            dve.sem_inc(h_ready, 2)
            dve.sem_inc(h_used, 2)
            with dve.Fori(0, NT) as t:
                for n in range(G_F):
                    k = n % 2
                    dve.wait_ge(silu_done, t * G_F + n + 1)
                    dve.wait_ge(h_used, t * G_F + max(n, 1) + 1)
                    dve.tensor_tensor(h[k][:, :], silu[k][:, :], up_ps[k][:, :], ALU.mult).then_inc(h_ready, 1)


def rms_residual(nc, g, a):
    with ExitStack() as ctx:
        def sb(name, shape, dt=F32):
            return [ctx.enter_context(nc.sbuf_tensor(f"z_{name}{i}", shape, dt)) for i in range(2)]

        def sem(name):
            return ctx.enter_context(nc.semaphore("z_" + name))

        squares, rs = sb("squares", [P, C, TT]), sb("rs", [P, TT])
        ms_ps = [ctx.enter_context(nc.psum_tensor(f"z_ms{i}", [P, TT], F32)) for i in range(2)]
        squared, summed, logged, rs_ready, step_sem = (
            sem(n) for n in ("squared", "summed", "logged", "rs_ready", "step"))
        eps = g.const("eps")[:, 1:2]
        block = ctx.enter_context(nc.Block())

        def tile(x, t):
            return x[:, :, t * TT:(t + 1) * TT]

        @block.tensor
        def _(pe):
            for t in range(NT):
                pe.wait_ge(squared, t + 1)
                if t >= 2:
                    pe.wait_ge(logged, t - 1)
                for c in range(C):
                    mm = pe.matmul(ms_ps[t % 2][:, :], g.const("mean"), squares[t % 2][:, c, :],
                                   start=c == 0, stop=c == C - 1)
                mm.then_inc(summed, 1)

        @block.scalar
        def _(act):
            def square(t):
                if t >= 2:
                    act.wait_ge(summed, t - 1)
                act.activation(squares[t % 2][:, :, :], tile(g.aux, t), ACT.Square).then_inc(squared, 1)

            square(0)
            for t in range(NT):
                if t + 1 < NT:
                    square(t + 1)
                act.wait_ge(summed, t + 1)
                if t >= 2:
                    act.wait_ge(step_sem, 2 * (t - 2) + 1)
                act.activation(rs[t % 2][:, :], ms_ps[t % 2][:, :], ACT.Ln, bias=eps).then_inc(logged, 1)
                act.wait_ge(logged, t + 1)
                act.activation(rs[t % 2][:, :], rs[t % 2][:, :], ACT.Exp, scale=-0.5).then_inc(rs_ready, 1)

        @block.vector
        def _(dve):
            step = Chain(dve, step_sem)
            for t in range(NT):
                dve.wait_ge(rs_ready, t + 1)
                step(dve.tensor_tensor(tile(g.aux, t), tile(g.aux, t), bc(rs[t % 2][:, :], 1, [P, C, TT]), ALU.mult))
                step(dve.tensor_tensor(tile(g.aux, t), tile(g.aux, t), tile(g.xt, t), ALU.add))


def decoder(nc, a, out, stop=99):
    with ExitStack() as ctx:
        g = Shared()
        g.xt = ctx.enter_context(nc.sbuf_tensor("residual", [P, C, T], F32))
        g.consts = ctx.enter_context(nc.sbuf_tensor("const_tables", [P, N_CONST], F32))
        g.shift = ctx.enter_context(nc.sbuf_tensor("fp4_shifts", [P, 4], I32))
        g.const = lambda name: g.consts[:, COL[name][0]:COL[name][1]]
        g.ln_sems = [ctx.enter_context(nc.semaphore("ln_" + n)) for n in
                     ("mean_ready", "centred_ready", "squares_ready", "var_ready", "ln_ready", "rs_ready", "normed")]
        g.stored = ctx.enter_context(nc.semaphore("stored"))
        g.stored_base = 0
        g.combine_dram = nc.dram_tensor("combine", [E_ROUTED + 1, T], F32, kind="Internal").ap()
        with ExitStack() as inner:
            g.keys = inner.enter_context(nc.sbuf_tensor("keys", [P, C, B, 4 * SLOTS], F32))
            g.values = inner.enter_context(nc.sbuf_tensor("values", [P, B, H0 // 2, 64], F32))
            sparse_select(nc, g, a)
            sparse_attention(nc, g, a)

        def with_aux(n, stage):
            with nc.sbuf_tensor(f"aux{n}", [P, C, T], F32) as g.aux:
                stage()

        def last_stages():
            feed_forward(nc, g, a)
            rms_residual(nc, g, a)
            layer_norm(nc, g, g.aux, g.xt, 5, out)

        plan = [lambda: layer_norm(nc, g, g.xt, g.xt, 0), lambda: with_aux(0, lambda: wkv(nc, g, a)),
                lambda: layer_norm(nc, g, g.xt, g.xt, 1), lambda: route(nc, g, a), lambda: experts(nc, g, a),
                lambda: layer_norm(nc, g, g.xt, g.xt, 2), lambda: causal_attention(nc, g, a),
                lambda: layer_norm(nc, g, g.xt, g.xt, 3), lambda: with_aux(1, lambda: cross_attention(nc, g, a)),
                lambda: layer_norm(nc, g, g.xt, g.xt, 4), lambda: with_aux(2, last_stages)]
        for k, phase in enumerate(plan):
            if k >= stop:
                break
            phase()
        if stop < len(plan):
            with nc.Block() as block:
                @block.sync
                def _(sp):
                    sp.dma_start(out, g.xt[:, :, :]).then_inc(g.stored, 16)
                    sp.wait_ge(g.stored, 16)


def lay_out(i):
    order = feature_order()
    i = {k: np.asarray(v) for k, v in i.items()}

    def chunks(w):
        return w.reshape(w.shape[0] // P, P, *w.shape[1:]).swapaxes(0, 1)

    def residual(w):
        return chunks(w)[order]

    def reorder(w, n=P):
        return w.reshape(*w.shape[:-1], w.shape[-1] // P, P)[..., order].reshape(w.shape)

    def nibbles(packed):
        *lead, rows, n = packed.shape
        b = np.ascontiguousarray(packed).view(np.uint8).reshape(-1, rows // 16, 16, n, 4)
        b = np.ascontiguousarray(b.transpose(0, 2, 4, 1, 3)).view(np.int32)
        return b.reshape(*lead, 64, rows // 16, n // 4)

    x = i["x"].reshape(T, D)
    tables, rope = constants()
    o = {"consts": tables, "rope": rope, "xt": residual(np.ascontiguousarray(x.T)),
         "ct": residual(np.ascontiguousarray(i["ctx_2048"].reshape(T, D).T)),
         "xtok": reorder(x).reshape(T // P, P, D).swapaxes(0, 1)}
    o["wi0"] = residual(i["L0_attn_Wi"])[:, :, 0]
    o["bi0"] = i["L0_attn_bi"].reshape(1, 1)
    for n in "qkv":
        o[f"w{n}0"] = residual(i[f"L0_attn_W{n}"])
    for n in "qk":
        o[f"b{n}0"] = chunks(i[f"L0_attn_b{n}"])
    o["bv0"] = i["L0_attn_bv"].reshape(1, D)
    o["wo0"] = chunks(reorder(i["L0_attn_Wo"]))
    o["bo0"] = residual(i["L0_attn_bo"])
    o["decay"], o["first"] = residual(i["L0_xattn_time_decay"]), residual(i["L0_xattn_time_first"])
    o["gate"] = residual(i["L0_ffn_gate_w"].T)
    o["one_row"] = np.ones((1, T), np.float32)

    def stack(name):
        return np.concatenate([i[f"L0_ffn_{name}"], i[f"L0_ffn_shared_{name}"][None]])

    o["gu"] = nibbles(reorder(stack("gate_up_packed")))
    o["d"] = nibbles(reorder(stack("down_packed")))
    o["gu_s"] = reorder(stack("gate_up_scales")).reshape(E_ROUTED + 1, G_D, 2, G_I, P)\
        .transpose(4, 0, 3, 2, 1).reshape(P, E_ROUTED + 1, 2 * G_I, G_D)
    o["d_s"] = reorder(stack("down_scales")).reshape(E_ROUTED + 1, -1)
    turn = np.concatenate([np.arange(1, D, 2), np.arange(0, D, 2)])
    for k, n in enumerate("qkv"):
        w, b = i["L1_attn_Wqkv"][k * D:(k + 1) * D], i["L1_attn_bqkv"][k * D:(k + 1) * D]
        o[f"w{n}1"] = residual(w.T)
        if n == "v":
            o["bv1"] = b.reshape(1, D)
        else:
            o[f"b{n}1"] = chunks(b)
            o[f"w{n}r1"], o[f"b{n}r1"] = residual(w[turn].T), chunks(b[turn])
    o["wo1"] = chunks(reorder(i["L1_attn_Wout"].T))
    o["bo1"] = residual(i["L1_attn_bout"])
    kv = np.concatenate([i["L1_xattn_Wk"], i["L1_xattn_Wv"]])
    o["wqx"], o["wkx"], o["wvx"] = (residual(w.T) for w in (i["L1_xattn_Wq"], kv[0::2], kv[1::2]))
    gu = nibbles(reorder(i["L1_ffn_gate_up_packed"].T)).reshape(64, -1)
    d = nibbles(reorder(i["L1_ffn_down_packed"].T)).reshape(64, -1)
    o["ffn"] = np.concatenate([gu, d], axis=1)
    o["ffn_s"] = np.concatenate([reorder(i["L1_ffn_gate_up_scales"]).reshape(1, -1),
                                 reorder(i["L1_ffn_down_scales"]).reshape(1, -1)], axis=1)
    shift = np.zeros((P, 4), np.int64)
    shift[:64, 0] = 4
    shift[:, 1], shift[:, 2], shift[:, 3] = 2, 0x1C1C1C1C, 0x80808080 - (1 << 32)
    o["shift"] = shift.astype(np.int32)
    return {k: np.ascontiguousarray(v) for k, v in o.items()}


def kernel(**inputs):
    import concourse.bacc as _bacc
    from concourse import mybir as _mybir
    from concourse.bass_utils import run_bass_kernel_spmd as _run

    nc = _bacc.Bacc("TRN2", target_bir_lowering=False, num_devices=1)
    arrays = lay_out(inputs)
    args = {n: nc.dram_tensor(n, v.shape, _mybir.dt.from_np(v.dtype), kind="ExternalInput").ap()
            for n, v in arrays.items()}
    out = nc.dram_tensor("out", (P, C, T), F32, kind="ExternalOutput").ap()
    decoder(nc, args, out)
    r = _run(nc, [arrays], core_ids=[0])
    got = np.asarray(r.results[0]["out"])
    natural = np.empty_like(got)
    natural[feature_order()] = got
    return np.ascontiguousarray(natural.swapaxes(0, 1).reshape(D, T).T).reshape(B, S, D)
```

```python
from contextlib import ExitStack

import numpy as np

import concourse.bass as bass
from concourse import mybir

F32 = mybir.dt.float32
F32R = mybir.dt.float32r
F16 = mybir.dt.float16
BF16 = mybir.dt.bfloat16
F8 = mybir.dt.float8e4
I32 = mybir.dt.int32
ALU = mybir.AluOpType
ACT = mybir.ActivationFunctionType
AX = mybir.AxisListType

P = 128
B, S, D = 8, 256, 512
T = B * S
C = D // P
TT = 512
NT = T // TT
LN_EPS = 1e-5

H0, HD0 = 16, 32
KEEP = min(max(1, int(S * 0.2)), S - 1)
MIN_TOKENS = 32
SLOTS = 64
assert max(KEEP, MIN_TOKENS) <= SLOTS

E_ROUTED, TOP_K, I_MOE, GS = 16, 4, 384, 128
G_D, G_I = D // GS, I_MOE // GS
I_FFN = 1408
G_F = I_FFN // GS
H1, HD1 = 16, 32
HX, HDX = 32, 16

_WIDTHS = [("ident", P), ("ones", P), ("mean", P), ("tri", 2 * S), ("slot", P), ("causal", P),
           ("head4", 4), ("head8", 8), ("blk16", P), ("perm", P), ("den16", 64), ("expert_lt", 256),
           ("cosc", 4), ("sinc", 4), ("eps", 3)]
COL = {}
_at = 0
for _n, _w in _WIDTHS:
    COL[_n] = (_at, _at + _w)
    _at += _w
N_CONST = _at


def feature_order():
    p = np.arange(P)
    return 2 * (p % 64) + p // 64


def constants():
    c = np.zeros((P, N_CONST), np.float32)

    def put(name, value):
        a, b = COL[name]
        c[:, a:b] = value

    p = np.arange(P)
    order = feature_order()
    put("ident", np.eye(P))
    put("ones", 1.0)
    put("mean", 1.0 / D)
    j = np.arange(S)
    put("tri", np.concatenate([(j[None, :] < (q * P + p)[:, None]) for q in range(2)], axis=1))
    put("slot", np.tile(np.arange(SLOTS), P // SLOTS)[None, :])
    put("causal", p[None, :] >= p[:, None])
    put("head4", (p[:, None] // 32 == np.arange(4)[None, :]) * (D ** -0.5))
    put("head8", p[:, None] // 16 == np.arange(8)[None, :])
    put("blk16", (p[:, None] // 16 == p[None, :] // 16) / 16.0)
    put("perm", p[:, None] == order[None, :])
    put("den16", np.concatenate([np.arange(32) < 16, np.arange(32) >= 16])[None, :])
    e = np.arange(E_ROUTED)
    put("expert_lt", (e[None, :] < e[:, None]).reshape(1, 256))
    freq = (np.float32(10000.0) ** (-(np.arange(0, D, 2, dtype=np.float32) / np.float32(D)))).astype(np.float32)
    angle = (np.float32(S) * np.repeat(freq, 2)).astype(np.float32)
    cos, sin = np.cos(angle), np.sin(angle)
    sin = np.where(np.arange(D) < D // 2, -sin, sin)
    put("cosc", cos.reshape(4, P).T)
    put("sinc", sin.reshape(4, P).T)
    put("eps", np.array([[LN_EPS, 1e-6, 0.0]]))
    return c, np.stack([cos, sin]).astype(np.float32).reshape(1, 2 * D)


class Chain:

    def __init__(self, eng, sem, base=0):
        self.eng, self.sem, self.base, self.n = eng, sem, base, 0

    def __call__(self, ins):
        self.n += 1
        ins.then_inc(self.sem, 1)
        self.eng.wait_ge(self.sem, self.base + self.n)


class Shared:
    pass


def bc(ap, axis, shape):
    return ap.unsqueeze(axis).to_broadcast(shape)


def layer_norm(nc, g, src, dst, layer, out_dram=None):
    with ExitStack() as ctx:
        def sb(name, shape, dt=F32):
            return ctx.enter_context(nc.sbuf_tensor(f"{name}_n{layer}", shape, dt))

        mean_ps = [ctx.enter_context(nc.psum_tensor(f"mean{i}_n{layer}", [P, TT], F32)) for i in range(2)]
        var_ps = [ctx.enter_context(nc.psum_tensor(f"var{i}_n{layer}", [P, TT], F32)) for i in range(2)]
        centred = [sb(f"centred{i}", [P, C, TT]) for i in range(2)]
        squares = [sb(f"squares{i}", [P, C, TT]) for i in range(2)]
        rs = [sb(f"rs{i}", [P, TT]) for i in range(2)]
        base = NT * layer
        mean_ready, centred_ready, squares_ready, var_ready, ln_ready, rs_ready, normed = g.ln_sems
        eps = g.const("eps")[:, 0:1]

        def tile(x, t):
            return x[:, :, t * TT:(t + 1) * TT]

        block = ctx.enter_context(nc.Block())

        @block.tensor
        def _(pe):
            def mean(t):
                if t >= 2:
                    pe.wait_ge(centred_ready, base + t - 1)
                for c in range(C):
                    mm = pe.matmul(mean_ps[t % 2][:, :], g.const("mean"), tile(src, t)[:, c, :],
                                   start=c == 0, stop=c == C - 1)
                mm.then_inc(mean_ready, 1)

            def var(t):
                pe.wait_ge(squares_ready, base + t + 1)
                if t >= 2:
                    pe.wait_ge(ln_ready, base + t - 1)
                for c in range(C):
                    mm = pe.matmul(var_ps[t % 2][:, :], g.const("mean"), squares[t % 2][:, c, :],
                                   start=c == 0, stop=c == C - 1)
                mm.then_inc(var_ready, 1)

            mean(0)
            for t in range(NT):
                if t + 1 < NT:
                    mean(t + 1)
                var(t)

        @block.vector
        def _(dve):
            def centre(t):
                dve.wait_ge(mean_ready, base + t + 1)
                if t >= 2:
                    dve.wait_ge(normed, base + t - 1)
                dve.tensor_tensor(centred[t % 2][:, :, :], tile(src, t), bc(mean_ps[t % 2][:, :], 1, [P, C, TT]),
                                  ALU.subtract).then_inc(centred_ready, 1)

            centre(0)
            for t in range(NT):
                if t + 1 < NT:
                    centre(t + 1)
                dve.wait_ge(rs_ready, base + t + 1)
                dve.tensor_tensor(tile(dst, t), centred[t % 2][:, :, :], bc(rs[t % 2][:, :], 1, [P, C, TT]),
                                  ALU.mult).then_inc(normed, 1)

        @block.scalar
        def _(act):
            def square(t):
                act.wait_ge(centred_ready, base + t + 1)
                if t >= 2:
                    act.wait_ge(var_ready, base + t - 1)
                act.activation(squares[t % 2][:, :, :], centred[t % 2][:, :, :], ACT.Square).then_inc(squares_ready, 1)

            square(0)
            for t in range(NT):
                if t + 1 < NT:
                    square(t + 1)
                act.wait_ge(var_ready, base + t + 1)
                if t >= 2:
                    act.wait_ge(normed, base + t - 1)
                act.activation(rs[t % 2][:, :], var_ps[t % 2][:, :], ACT.Ln, bias=eps).then_inc(ln_ready, 1)
                act.wait_ge(ln_ready, base + t + 1)
                act.activation(rs[t % 2][:, :], rs[t % 2][:, :], ACT.Exp, scale=-0.5).then_inc(rs_ready, 1)

        @block.sync
        def _(sp):
            sp.wait_ge(normed, base + NT)
            if out_dram is not None:
                sp.dma_start(out_dram, dst[:, :, :]).then_inc(g.stored, 16)
                sp.wait_ge(g.stored, g.stored_base + 16)


def sparse_select(nc, g, a):
    with ExitStack() as ctx:
        def sb(name, shape, dt=F32):
            return ctx.enter_context(nc.sbuf_tensor("s_" + name, shape, dt))

        def sem(name):
            return ctx.enter_context(nc.semaphore("s_" + name))

        wi = sb("wi", [P, C])
        wib = sb("wib", [P, C, P])
        bi = sb("bi", [P, 1])
        wk = sb("wk", [P, C, D])
        wv = sb("wv", [P, C, D])
        bk = sb("bk", [P, C])
        bv = sb("bv", [1, D])
        imp = sb("imp", [P, B, S])
        ge = sb("ge", [P, B, 2, S])
        gt = sb("gt", [P, B, 2, S])
        own = sb("own", [P, 2 * B])
        small = sb("small", [P, 4, 2 * B])
        sel = sb("sel", [P, 2 * B, P])
        xtok = [sb(f"xtok{i}", [P, 2, D]) for i in range(2)]
        xsel = sb("xsel", [P, C, B, P])
        valid = sb("valid", [P, B, P])
        imp_ps = ctx.enter_context(nc.psum_tensor("s_imp_ps", [P, T], F32))
        row_ps = [ctx.enter_context(nc.psum_tensor(f"s_row{i}", [P, 512], F32)) for i in range(2)]
        xsel_ps = [ctx.enter_context(nc.psum_tensor(f"s_xs{i}", [P, 512], F32)) for i in range(2)]

        loaded, weights, wib_ready = sem("loaded"), sem("weights"), sem("wib_ready")
        imp_done, imp_copied, dve_step, sel_ready = sem("imp_done"), sem("imp_copied"), sem("dve_step"), sem("sel_ready")
        zeroed = sem("zeroed")
        tok_loaded = [sem(f"tok_loaded{i}") for i in range(2)]
        gathered, xsel_copied = sem("gathered"), sem("xsel_copied")
        row_done, row_used = sem("row_done"), sem("row_used")

        block = ctx.enter_context(nc.Block())

        @block.sync
        def _(sp):
            sp.dma_start(g.consts[:, :], a["consts"]).then_inc(loaded, 16)
            sp.dma_start(g.shift[:, :], a["shift"]).then_inc(loaded, 16)
            sp.dma_start(wi[:, :], a["wi0"]).then_inc(loaded, 16)
            sp.dma_start(bi[:, :], a["bi0"].to_broadcast([P, 1])).then_inc(loaded, 16)
            for t in range(NT):
                sp.dma_start(g.xt[:, :, t * TT:(t + 1) * TT], a["xt"][:, :, t * TT:(t + 1) * TT]).then_inc(loaded, 16)
            for dst, src in ((wk[:, :, :], a["wk0"]), (wv[:, :, :], a["wv0"]), (bk[:, :], a["bk0"]), (bv[:, :], a["bv0"])):
                sp.dma_start(dst, src).then_inc(weights, 16)
            with sp.Fori(0, B // 2) as i:
                for u in range(2):
                    sp.wait_ge(gathered, 2 * i + u + 1)
                    sp.dma_start(xtok[u][:, :, :], a["xtok"][:, bass.ds(4 * i + 2 * u, 2), :]).then_inc(tok_loaded[u], 16)

        @block.gpsimd
        def _(pool):
            pool.memset(g.keys[:, :, :, :], 0.0).then_inc(zeroed, 1)
            pool.memset(g.values[:, :, :, :], 0.0).then_inc(zeroed, 1)

        @block.scalar
        def _(act):
            for t in range(NT):
                act.wait_ge(imp_done, t + 1)
                act.activation(imp[:, 2 * t:2 * t + 2, :], imp_ps[:, t * TT:(t + 1) * TT].rearrange("p (b s) -> p b s", b=2),
                               ACT.Identity, bias=bi[:, :]).then_inc(imp_copied, 1)
            with act.Fori(0, B // 2) as i:
                for u in range(2):
                    act.wait_ge(gathered, 2 * i + u + 3)
                    act.activation(xsel[:, :, bass.ds(2 * i + u, 1), :],
                                   xsel_ps[u][:, :].rearrange("p (c o s) -> p c o s", c=C, o=1),
                                   ACT.Copy).then_inc(xsel_copied, 1)

        @block.vector
        def _(dve):
            step = Chain(dve, dve_step)
            dve.wait_ge(loaded, 16 * (4 + NT))
            dve.tensor_copy(wib[:, :, :], bc(wi[:, :], 2, [P, C, P])).then_inc(wib_ready, 1)
            dve.wait_ge(imp_copied, NT)
            step(dve.tensor_tensor(sel[:, :, :], imp[:, :, :].rearrange("p b (q i) -> p (b q) i", q=2),
                                   bc(g.const("ident"), 1, [P, 2 * B, P]), ALU.mult))
            step(dve.tensor_reduce(own[:, :], sel[:, :, :], AX.X, ALU.add))
            own_v = own[:, :].rearrange("p (b q) -> p b q", q=2)
            for q in range(2):
                mine = bc(own_v[:, :, q], 2, [P, B, S])
                dve.tensor_tensor(ge[:, :, q, :], imp[:, :, :], mine, ALU.is_ge)
                last = dve.tensor_tensor(gt[:, :, q, :], imp[:, :, :], mine, ALU.is_gt)
            step(last)
            n_ge, n_gt, ties, keep = (small[:, k, :] for k in range(4))
            dve.tensor_reduce(n_ge, ge[:, :, :, :].rearrange("p b q j -> p (b q) j"), AX.X, ALU.add)
            step(dve.tensor_reduce(n_gt, gt[:, :, :, :].rearrange("p b q j -> p (b q) j"), AX.X, ALU.add))
            step(dve.tensor_tensor(ge[:, :, :, :], ge[:, :, :, :], gt[:, :, :, :], ALU.subtract))
            step(dve.tensor_tensor(ge[:, :, :, :].rearrange("p b q j -> p b (q j)"),
                                   ge[:, :, :, :].rearrange("p b q j -> p b (q j)"),
                                   bc(g.const("tri"), 1, [P, B, 2 * S]), ALU.mult))
            step(dve.tensor_reduce(ties, ge[:, :, :, :].rearrange("p b q j -> p (b q) j"), AX.X, ALU.add))
            step(dve.tensor_tensor(ties, ties, n_gt, ALU.add))
            dve.tensor_scalar(n_ge, n_ge, float(KEEP) + 0.5, None, ALU.is_lt)
            step(dve.tensor_scalar(keep, ties, float(MIN_TOKENS) - 0.5, None, ALU.is_lt))
            step(dve.tensor_tensor(keep, keep, n_ge, ALU.max))
            step(dve.tensor_tensor(sel[:, :, :], bc(g.const("slot"), 1, [P, 2 * B, P]), bc(ties, 2, [P, 2 * B, P]),
                                   ALU.is_equal))
            dve.tensor_tensor(sel[:, :, :], sel[:, :, :], bc(keep, 2, [P, 2 * B, P]), ALU.mult).then_inc(sel_ready, 1)
            for n in range(2):
                dve.wait_ge(row_done, n + 1)
                dve.tensor_copy(valid[:, 4 * n:4 * n + 4, :], row_ps[n][:, :].rearrange("p (b s) -> p b s", b=4))\
                   .then_inc(row_used, 1)
            dve.wait_ge(row_used, 2)
            dve.wait_ge(weights, 64)
            dve.wait_ge(zeroed, 2)
            for m in range(C):
                dve.wait_ge(row_done, 3 + m)
                ps = row_ps[m % 2][:, :].rearrange("p (b s) -> p b s", b=B)
                for j in range(4):
                    r = slice(32 * j, 32 * j + 32)
                    last = dve.scalar_tensor_tensor(g.keys[r, m, :, j * SLOTS:(j + 1) * SLOTS], valid[r, :, 0:SLOTS],
                                                    bk[r, m:m + 1], ps[r, :, :], ALU.mult, ALU.add)
                last.then_inc(row_used, 1)
            for b in range(B):
                dve.wait_ge(row_done, 3 + C + b)
                ps = row_ps[b % 2][:, :].rearrange("p (n two d) -> p n two d", two=2, d=HD0)
                for u in range(2):
                    r = slice(64 * u, 64 * u + 64)
                    last = dve.tensor_copy(g.values[r, b, :, 32 * u:32 * u + 32], ps[r, :, u, :])
                last.then_inc(row_used, 1)

        @block.tensor
        def _(pe):
            pe.wait_ge(wib_ready, 1)
            for t in range(NT):
                for c in range(C):
                    mm = pe.matmul(imp_ps[:, t * TT:(t + 1) * TT], wib[:, c, :], g.xt[:, c, t * TT:(t + 1) * TT],
                                   start=c == 0, stop=c == C - 1)
                mm.then_inc(imp_done, 1)
            pe.wait_ge(sel_ready, 1)
            sel_v = sel[:, :, :].rearrange("p (b q) s -> p b q s", q=2)
            for n in range(2):
                for q in range(2):
                    mm = pe.matmul(row_ps[n][:, :], g.const("ones"), sel_v[:, 4 * n:4 * n + 4, q, :],
                                   start=q == 0, stop=q == 1)
                mm.then_inc(row_done, 1)
            pe.sem_inc(gathered, 2)
            pe.sem_inc(xsel_copied, 2)
            with pe.Fori(0, B // 2) as i:
                for u in range(2):
                    pe.wait_ge(tok_loaded[u], 16 * i + 16)
                    pe.wait_ge(xsel_copied, 2 * i + u + 1)
                    for c in range(C):
                        for q in range(2):
                            mm = pe.matmul(xsel_ps[u][:, c * P:(c + 1) * P], xtok[u][:, q, c * P:(c + 1) * P],
                                           sel[:, bass.ds(4 * i + 2 * u + q, 1), :], start=q == 0, stop=q == 1)
                    mm.then_inc(gathered, 1)
            pe.wait_ge(xsel_copied, B + 2)
            pe.wait_ge(weights, 64)
            for m in range(C):
                pe.wait_ge(row_used, m + 1)
                for c in range(C):
                    mm = pe.matmul(row_ps[m % 2][:, :], wk[:, c, m * P:(m + 1) * P], xsel[:, c, :, 0:SLOTS],
                                   start=c == 0, stop=c == C - 1)
                mm.then_inc(row_done, 1)
            for b in range(B):
                pe.wait_ge(row_used, C + b + 1)
                for c in range(C):
                    pe.matmul(row_ps[b % 2][:, :], xsel[:, c, b, :], wv[:, c, :], start=c == 0, stop=False)
                pe.matmul(row_ps[b % 2][:, :], valid[0:1, b, :], bv[:, :], start=False, stop=True).then_inc(row_done, 1)


def sparse_attention(nc, g, a):
    scale = HD0 ** -0.5
    with ExitStack() as ctx:
        def sb(name, shape, dt=F32):
            return ctx.enter_context(nc.sbuf_tensor("a0_" + name, shape, dt))

        def sem(name):
            return ctx.enter_context(nc.semaphore("a0_" + name))

        def ps(name, shape):
            return ctx.enter_context(nc.psum_tensor("a0_" + name, shape, F32))

        wq = sb("wq", [P, C, D])
        wo = sb("wo", [P, C, D])
        bq = sb("bq", [P, C])
        bo = sb("bo", [P, C])
        q_sb = sb("q", [P, C, S])
        v_sb = sb("v", [P, H0 // 2, 64])
        e_sb = [sb(f"e{i}", [P, H0, SLOTS]) for i in range(2)]
        mx = [sb(f"mx{i}", [P, H0]) for i in range(2)]
        e0 = [sb(f"e0{i}", [P, H0]) for i in range(2)]
        den = [sb(f"den{i}", [P, H0]) for i in range(2)]
        pt = sb("pt", [P, H0 // 2, S])
        at = sb("at", [P, C, S])
        head_ps = ps("head", [P, C, S])
        s_ps = [ps(f"s{i}", [P, H0, SLOTS]) for i in range(2)]
        pt_ps = ps("pt_ps", [P, H0 // 2, P])
        o_ps = s_ps[0][:, :, :].rearrange("p h s -> p (h s)").rearrange("p (c q) -> p c q", c=C)

        weights = sem("weights")
        q_done, q_copied, s_done, shifted, exped, p_ready = (sem(n) for n in ("q_done", "q_copied", "s_done", "shifted", "exped", "p_ready"))
        t_done, t_copied, v_copied, av_done, av_copied, o_done, added, step_sem = (
            sem(n) for n in ("t_done", "t_copied", "v_copied", "av_done", "av_copied", "o_done", "added", "step"))

        block = ctx.enter_context(nc.Block())

        @block.sync
        def _(sp):
            for dst, src in ((wq[:, :, :], a["wq0"]), (wo[:, :, :], a["wo0"]), (bq[:, :], a["bq0"]), (bo[:, :], a["bo0"])):
                sp.dma_start(dst, src).then_inc(weights, 16)

        @block.gpsimd
        def _(pool):
            with pool.Fori(0, B) as b:
                pool.wait_ge(av_done, b + 1)
                pool.tensor_copy(v_sb[:, :, :].rearrange("p n d -> p (n d)"),
                                 g.values[:, bass.ds(b, 1), :, :].rearrange("p b n d -> p (b n d)"))\
                    .then_inc(v_copied, 1)

        @block.tensor
        def _(pe):
            pe.wait_ge(weights, 64)
            pe.sem_inc(av_done, 1)
            with pe.Fori(0, B) as b:
                pe.wait_ge(av_copied, b + 1)
                for m in range(C):
                    for c in range(C):
                        mm = pe.matmul(head_ps[:, m, :], wq[:, c, m * P:(m + 1) * P], g.xt[:, c, bass.ts(b, S)],
                                       start=c == 0, stop=c == C - 1)
                mm.then_inc(q_done, 1)
                pe.wait_ge(q_copied, b + 1)
                pe.wait_ge(added, b + 1)
                for q in range(2):
                    for c in range(C):
                        mm = pe.matmul(s_ps[q][:, 4 * c:4 * c + 4, :], q_sb[:, c, q * P:(q + 1) * P],
                                       g.keys[:, c, bass.ds(b, 1), :], start=True, stop=True)
                    mm.then_inc(s_done, 1)
                for q in range(2):
                    pe.wait_ge(p_ready, 2 * b + q + 1)
                    pe.wait_ge(t_copied, 2 * b + q + 1)
                    for n in range(H0 // 2):
                        mm = pe.transpose(pt_ps[:, n, :], e_sb[q][:, 2 * n:2 * n + 2, :].rearrange("p h s -> p (h s)"),
                                          g.const("ident"))
                    mm.then_inc(t_done, 1)
                pe.wait_ge(t_copied, 2 * b + 3)
                pe.wait_ge(v_copied, b + 1)
                for n in range(H0 // 2):
                    r = 64 * (n % 2)
                    mm = pe.matmul(head_ps[r:r + 64, n // 2, :], v_sb[:, n, :], pt[:, n, :], start=True, stop=True)
                mm.then_inc(av_done, 1)
                pe.wait_ge(av_copied, b + 2)
                for m in range(C):
                    for c in range(C):
                        mm = pe.matmul(o_ps[:, m, :], wo[:, c, m * P:(m + 1) * P], at[:, c, :],
                                       start=c == 0, stop=c == C - 1)
                mm.then_inc(o_done, 1)

        @block.scalar
        def _(act):
            act.wait_ge(weights, 64)
            act.sem_inc(av_copied, 1)
            act.sem_inc(t_copied, 1)
            with act.Fori(0, B) as b:
                act.wait_ge(q_done, b + 1)
                for m in range(C):
                    last = act.activation(q_sb[:, m, :], head_ps[:, m, :], ACT.Identity, bias=bq[:, m:m + 1])
                last.then_inc(q_copied, 1)
                for q in range(2):
                    act.wait_ge(shifted, 2 * b + q + 1)
                    act.activation(e0[q][:, :], mx[q][:, :], ACT.Exp, scale=-scale)
                    act.activation(e_sb[q][:, :, :], e_sb[q][:, :, :], ACT.Exp, scale=scale).then_inc(exped, 1)
                for q in range(2):
                    act.wait_ge(t_done, 2 * b + q + 1)
                    act.activation(pt[:, :, q * P:(q + 1) * P], pt_ps[:, :, :], ACT.Copy).then_inc(t_copied, 1)
                act.wait_ge(av_done, b + 2)
                act.activation(at[:, :, :], head_ps[:, :, :], ACT.Copy).then_inc(av_copied, 1)

        @block.vector
        def _(dve):
            dve.wait_ge(weights, 64)
            dve.sem_inc(added, 1)
            steps = 2 * 2 + 2 * 3
            with dve.Fori(0, B) as b:
                step = Chain(dve, step_sem, b * steps)
                for q in range(2):
                    dve.wait_ge(s_done, 2 * b + q + 1)
                    step(dve.tensor_reduce(mx[q][:, :], s_ps[q][:, :, :], AX.X, ALU.max))
                    step(dve.tensor_scalar(mx[q][:, :], mx[q][:, :], 0.0, None, ALU.max))
                    dve.tensor_tensor(e_sb[q][:, :, :], s_ps[q][:, :, :], bc(mx[q][:, :], 2, [P, H0, SLOTS]),
                                      ALU.subtract).then_inc(shifted, 1)
                for q in range(2):
                    dve.wait_ge(exped, 2 * b + q + 1)
                    step(dve.tensor_reduce(den[q][:, :], e_sb[q][:, :, :], AX.X, ALU.add))
                    step(dve.scalar_tensor_tensor(den[q][:, :], e0[q][:, :], float(S - SLOTS), den[q][:, :],
                                                  ALU.mult, ALU.add))
                    step(dve.reciprocal(den[q][:, :], den[q][:, :]))
                    dve.tensor_tensor(e_sb[q][:, :, :], e_sb[q][:, :, :], bc(den[q][:, :], 2, [P, H0, SLOTS]),
                                      ALU.mult).then_inc(p_ready, 1)
                assert step.n == steps
                dve.wait_ge(o_done, b + 1)
                for m in range(C):
                    x = g.xt[:, m, bass.ts(b, S)]
                    last = dve.scalar_tensor_tensor(x, o_ps[:, m, :], bo[:, m:m + 1], x, ALU.add, ALU.add)
                last.then_inc(added, 1)


def wkv(nc, g, a):
    FAR = -1e38
    BP = 4
    PIECES = C * (B // BP)
    with ExitStack() as ctx:
        def sb(name, shape, dt=F32):
            return ctx.enter_context(nc.sbuf_tensor("w_" + name, shape, dt))

        def sem(name):
            return ctx.enter_context(nc.semaphore("w_" + name))

        decay = sb("decay", [P, C])
        first = sb("first", [P, C])
        w_dec = sb("w_dec", [P, C])
        w_row = sb("w_row", [P, C, BP, S])
        names = ("pp", "prev", "eb", "kb", "kv", "aa", "bb", "e1", "e2", "num")
        buf = {n: [sb(f"{n}{i}", [P, BP, S]) for i in range(2)] for n in names}

        loaded, w_ready, row_ready = sem("loaded"), sem("w_ready"), sem("row_ready")
        den_ready, logged, inverted = sem("den_ready"), sem("logged"), sem("inverted")
        pp_done, prev_ready, diffs, exps_a, kv_ready, scanned, yexp, done, step_sem, kb_sub, e2v = (
            sem(n) for n in ("pp_done", "prev_ready", "diffs", "exps_a", "kv_ready", "scanned", "yexp", "done", "step",
                             "kb_sub", "e2v"))

        def piece(n):
            c, h = n // (B // BP), n % (B // BP)
            sl = slice(h * BP * S, (h + 1) * BP * S)
            k = g.xt[:, c, sl].rearrange("p (b s) -> p b s", b=BP)
            v = g.aux[:, c, sl].rearrange("p (b s) -> p b s", b=BP)
            return c, k, v

        def flat(x):
            return x[:, :, :].rearrange("p b s -> p (b s)")

        block = ctx.enter_context(nc.Block())

        @block.sync
        def _(sp):
            sp.dma_start(decay[:, :], a["decay"]).then_inc(loaded, 16)
            sp.dma_start(first[:, :], a["first"]).then_inc(loaded, 16)
            sp.dma_start(g.aux[:, :, :], a["ct"]).then_inc(loaded, 16)

        @block.scalar
        def _(act):
            act.wait_ge(loaded, 48)
            act.activation(w_dec[:, :], decay[:, :], ACT.Exp).then_inc(w_ready, 1)

            def early_prev(n):
                i = n % 2
                act.wait_ge(pp_done, n + 1)
                if n >= 2:
                    act.wait_ge(diffs, n - 1)
                act.activation(buf["prev"][i][:, :, 1:S], buf["pp"][i][:, :, 0:S - 1], ACT.Copy).then_inc(prev_ready, 1)

            def early(n):
                i = n % 2
                c, k, v = piece(n)
                if n == 0:
                    early_prev(n)
                act.wait_ge(diffs, n + 1)
                act.activation(buf["eb"][i][:, :, :], buf["eb"][i][:, :, :], ACT.Exp, bias=w_dec[:, c:c + 1])
                act.wait_ge(kb_sub, n + 1)
                act.activation(buf["kb"][i][:, :, :], buf["kb"][i][:, :, :], ACT.Exp).then_inc(exps_a, 1)
                act.activation(buf["e2"][i][:, :, :], buf["e2"][i][:, :, :], ACT.Exp)
                act.activation(buf["e1"][i][:, :, :], buf["e1"][i][:, :, :], ACT.Exp, scale=-1.0).then_inc(yexp, 1)

            def invert(n):
                x = buf["kv"][n % 2][:, :, :]
                act.wait_ge(den_ready, n + 1)
                act.activation(x, x, ACT.Ln).then_inc(logged, 1)
                act.wait_ge(logged, n + 1)
                act.activation(x, x, ACT.Exp, scale=-1.0).then_inc(inverted, 1)

            early(0)
            for n in range(PIECES):
                if n + 1 < PIECES:
                    early_prev(n + 1)
                invert(n)
                if n + 1 < PIECES:
                    early(n + 1)

        @block.gpsimd
        def _(pool):
            for i in range(2):
                pool.memset(buf["prev"][i][:, :, 0:1], FAR).then_inc(prev_ready, 1)
            pool.memset(w_row[:, :, :, :], 0.0).then_inc(row_ready, 1)
            for n in range(PIECES):
                i = n % 2
                c, k, v = piece(n)
                pool.wait_ge(pp_done, n + 1)
                if n >= 2:
                    pool.wait_ge(done, n - 1)
                pool.tensor_tensor(buf["kb"][i][:, :, :], k, buf["pp"][i][:, :, :], ALU.subtract).then_inc(kb_sub, 1)
                pool.wait_ge(exps_a, n + 1)
                pool.tensor_tensor(buf["kv"][i][:, :, :], buf["kb"][i][:, :, :], v, ALU.mult).then_inc(kv_ready, 1)
                pool.wait_ge(yexp, n + 1)
                pool.tensor_tensor(buf["num"][i][:, :, :], buf["e2"][i][:, :, :], v, ALU.mult).then_inc(e2v, 1)

        @block.vector
        def _(dve):
            step = Chain(dve, step_sem)
            dve.wait_ge(w_ready, 1)
            step(dve.tensor_scalar(w_dec[:, :], w_dec[:, :], -1.0, None, ALU.mult))
            dve.wait_ge(row_ready, 1)
            for c in range(C):
                last = dve.tensor_scalar(w_row[:, c, :, :], w_row[:, c, :, :], w_dec[:, c:c + 1], None, ALU.add)
            step(last)
            step(dve.memset(w_row[:, :, :, 0:1], 3 * FAR))
            dve.wait_ge(prev_ready, 2)

            def front(n):
                i = n % 2
                c, k, v = piece(n)
                if n >= 2:
                    dve.wait_ge(kb_sub, n - 1)
                    dve.wait_ge(prev_ready, 2 + n - 1)
                    dve.wait_ge(diffs, n - 1)
                dve.tensor_tensor_scan(flat(buf["pp"][i]), w_row[:, c, :, :].rearrange("p b s -> p (b s)"),
                                       k.rearrange("p b s -> p (b s)"), FAR, ALU.add, ALU.max).then_inc(pp_done, 1)

            def middle(n):
                i = n % 2
                c, k, v = piece(n)
                dve.wait_ge(prev_ready, 2 + n + 1)
                dve.wait_ge(pp_done, n + 1)
                if n >= 2:
                    dve.wait_ge(done, n - 1)
                prev = buf["prev"][i][:, :, :]
                step(dve.scalar_tensor_tensor(flat(buf["e1"][i]), k.rearrange("p b s -> p (b s)"), first[:, c:c + 1],
                                              flat(buf["prev"][i]), ALU.add, ALU.subtract))
                step(dve.tensor_scalar(flat(buf["e2"][i]), flat(buf["e1"][i]), 0.0, None, ALU.min))
                dve.tensor_scalar(flat(buf["e1"][i]), flat(buf["e1"][i]), 0.0, None, ALU.max)
                dve.tensor_tensor(buf["eb"][i][:, :, :], prev, buf["pp"][i][:, :, :], ALU.subtract).then_inc(diffs, 1)

            def scans(n):
                i = n % 2
                dve.wait_ge(exps_a, n + 1)
                dve.tensor_tensor_scan(flat(buf["bb"][i]), flat(buf["eb"][i]), flat(buf["kb"][i]), 0.0, ALU.mult, ALU.add)
                dve.wait_ge(kv_ready, n + 1)
                step(dve.tensor_tensor_scan(flat(buf["aa"][i]), flat(buf["eb"][i]), flat(buf["kv"][i]), 0.0,
                                            ALU.mult, ALU.add))

            def back(n):
                i = n % 2
                c, k, v = piece(n)
                e1, e2, aa, bb, num = (buf[x][i] for x in ("e1", "e2", "aa", "bb", "num"))
                dve.wait_ge(yexp, n + 1)
                t1, t2 = buf["kb"][i], buf["kv"][i]
                dve.tensor_tensor(t1[:, :, 1:S], e1[:, :, 1:S], aa[:, :, 0:S - 1], ALU.mult)
                dve.tensor_tensor(t2[:, :, 1:S], e1[:, :, 1:S], bb[:, :, 0:S - 1], ALU.mult)
                dve.memset(t1[:, :, 0:1], 0.0)
                step(dve.memset(t2[:, :, 0:1], 0.0))
                dve.wait_ge(e2v, n + 1)
                dve.tensor_tensor(t1[:, :, :], t1[:, :, :], num[:, :, :], ALU.add)
                dve.tensor_tensor(t2[:, :, :], t2[:, :, :], e2[:, :, :], ALU.add).then_inc(den_ready, 1)

            def finish(n):
                i = n % 2
                c, k, v = piece(n)
                t1, t2 = buf["kb"][i], buf["kv"][i]
                dve.wait_ge(inverted, n + 1)
                dve.wait_ge(den_ready, n + 1)
                step(dve.tensor_tensor(flat(t1), flat(t1), flat(t2), ALU.mult))
                dve.tensor_tensor(k, k, t1[:, :, :], ALU.add).then_inc(done, 1)

            front(0)
            middle(0)
            for n in range(PIECES):
                if n + 1 < PIECES:
                    front(n + 1)
                scans(n)
                if n >= 1:
                    finish(n - 1)
                if n + 1 < PIECES:
                    middle(n + 1)
                back(n)
            finish(PIECES - 1)


def route(nc, g, a):
    NTOK = T // P
    E = E_ROUTED
    with ExitStack() as ctx:
        def sb(name, shape, dt=F32):
            return ctx.enter_context(nc.sbuf_tensor("r_" + name, shape, dt))

        def sem(name):
            return ctx.enter_context(nc.semaphore("r_" + name))

        wg = sb("wg", [P, C, E])
        lt = sb("lt", [E, T])
        p = sb("p", [P, NTOK, E])
        big = [sb(f"big{i}", [P, NTOK, E, E]) for i in range(2)]
        m = sb("m", [P, NTOK])
        rank = sb("rank", [P, NTOK, E])
        ct = sb("ct", [E, T])
        logit_ps = ctx.enter_context(nc.psum_tensor("r_logit", [E, T], F32))
        tok_ps = ctx.enter_context(nc.psum_tensor("r_tok", [P, NTOK, E], F32))
        loaded, logits, copied, turned, shifted, exped, ready, back, ct_ready, stored, step_sem = (
            sem(n) for n in ("loaded", "logits", "copied", "turned", "shifted", "exped", "ready", "back", "ct_ready",
                             "stored", "step"))
        block = ctx.enter_context(nc.Block())

        @block.sync
        def _(sp):
            sp.dma_start(wg[:, :, :], a["gate"]).then_inc(loaded, 16)
            sp.dma_start(g.combine_dram[E:E + 1, :], a["one_row"]).then_inc(stored, 16)
            sp.wait_ge(ct_ready, NT)
            sp.dma_start(g.combine_dram[0:E, :], ct[:, :]).then_inc(stored, 16)
            sp.wait_ge(stored, 32)

        @block.tensor
        def _(pe):
            pe.wait_ge(loaded, 16)
            for t in range(NT):
                for c in range(C):
                    mm = pe.matmul(logit_ps[:, t * TT:(t + 1) * TT], wg[:, c, :], g.xt[:, c, t * TT:(t + 1) * TT],
                                   start=c == 0, stop=c == C - 1)
                mm.then_inc(logits, 1)
            pe.wait_ge(copied, NT)
            for n in range(NTOK):
                mm = pe.transpose(tok_ps[:, n, :], lt[:, n * P:(n + 1) * P], g.const("ident")[0:E, 0:E])
            mm.then_inc(turned, 1)
            pe.wait_ge(ready, 1)
            for n in range(NTOK):
                mm = pe.transpose(logit_ps[:, n * P:(n + 1) * P], p[:, n, :], g.const("ident"))
                if n % 4 == 3:
                    mm.then_inc(back, 1)

        @block.scalar
        def _(act):
            for t in range(NT):
                act.wait_ge(logits, t + 1)
                act.activation(lt[:, t * TT:(t + 1) * TT], logit_ps[:, t * TT:(t + 1) * TT], ACT.Copy).then_inc(copied, 1)
            act.wait_ge(shifted, 1)
            act.activation(p[:, :, :], p[:, :, :], ACT.Exp).then_inc(exped, 1)
            for t in range(NT):
                act.wait_ge(back, t + 1)
                act.activation(ct[:, t * TT:(t + 1) * TT], logit_ps[:, t * TT:(t + 1) * TT], ACT.Copy).then_inc(ct_ready, 1)

        @block.vector
        def _(dve):
            step = Chain(dve, step_sem)
            full, small = [P, NTOK, E, E], [P, NTOK, E]
            dve.wait_ge(turned, 1)
            step(dve.tensor_reduce(m[:, :], tok_ps[:, :, :], AX.X, ALU.max))
            dve.tensor_tensor(p[:, :, :], tok_ps[:, :, :], bc(m[:, :], 2, small), ALU.subtract).then_inc(shifted, 1)
            dve.wait_ge(exped, 1)
            step(dve.tensor_reduce(m[:, :], p[:, :, :], AX.X, ALU.add))
            step(dve.reciprocal(m[:, :], m[:, :]))
            step(dve.tensor_tensor(p[:, :, :], p[:, :, :], bc(m[:, :], 2, small), ALU.mult))
            other, mine = bc(p[:, :, :], 2, full), bc(p[:, :, :], 3, full)
            dve.tensor_tensor(big[0][:, :, :, :], other, mine, ALU.is_gt)
            step(dve.tensor_tensor(big[1][:, :, :, :], other, mine, ALU.is_equal))
            step(dve.tensor_tensor(big[1][:, :, :, :].rearrange("p n e f -> p n (e f)"),
                                   big[1][:, :, :, :].rearrange("p n e f -> p n (e f)"),
                                   bc(g.const("expert_lt"), 1, [P, NTOK, E * E]), ALU.mult))
            step(dve.tensor_tensor(big[0][:, :, :, :], big[0][:, :, :, :], big[1][:, :, :, :], ALU.add))
            step(dve.tensor_reduce(rank[:, :, :], big[0][:, :, :, :], AX.X, ALU.add))
            step(dve.tensor_scalar(rank[:, :, :], rank[:, :, :], TOP_K - 0.5, None, ALU.is_lt))
            step(dve.tensor_tensor(p[:, :, :], p[:, :, :], rank[:, :, :], ALU.mult))
            step(dve.tensor_reduce(m[:, :], p[:, :, :], AX.X, ALU.add))
            step(dve.reciprocal(m[:, :], m[:, :]))
            dve.tensor_tensor(p[:, :, :], p[:, :, :], bc(m[:, :], 2, small), ALU.mult).then_inc(ready, 1)


def decode_fp4(dve, step, g, raw, tmp):
    step(dve.tensor_scalar(raw, raw, g.shift[:, 0:1], None, ALU.logical_shift_left))
    step(dve.tensor_scalar(tmp, raw, g.shift[:, 1:2], g.shift[:, 2:3], ALU.logical_shift_right, ALU.bitwise_and))
    step(dve.scalar_tensor_tensor(raw, raw, g.shift[:, 3:4], tmp, ALU.bitwise_and, ALU.bitwise_or))


FP8_GAIN = 64.0


def experts(nc, g, a):
    N_GU, N_D = 2 * I_MOE, D
    NO = 2 * G_I
    PER = NT * G_I
    T_RING, G_RING, Y_RING = 4, 6, 2
    DOWN_AT = {3: (0, 1), 4: (2,), 5: (3,)}
    Y_CREDIT = 5
    with ExitStack() as ctx:
        def sb(name, shape, dt=F32):
            return ctx.enter_context(nc.sbuf_tensor(f"x_{name}", shape, dt))

        def sem(name):
            return ctx.enter_context(nc.semaphore("x_" + name))

        x_hi, x_lo = sb("x_hi", [P, C, T], F32R), sb("x_lo", [P, C, T], F32R)
        raw_gu, raw_d = sb("raw_gu", [P, G_D, N_GU // 4], I32), sb("raw_d", [P, G_I, N_D // 4], I32)
        tmp = sb("tmp", [P, G_D, N_GU // 4], I32)
        mark, mark_act = sb("mark", [P, 1], I32), sb("mark_act", [P, 1])
        w_gu = [sb(f"w_gu{u}", [P, G_D, N_GU], F32R) for u in range(2)]
        s_gu = sb("s_gu", [P, E_ROUTED + 1, NO, G_D])
        s_gu_now = sb("s_gu_now", [P, 2, NO, G_D])
        w_d = sb("w_d", [P, G_I, N_D])
        d_hi, d_lo = sb("d_hi", [P, G_I, N_D], F32R), sb("d_lo", [P, G_I, N_D], F32R)
        part = [[sb(f"part{k}{j}", [P, TT]) for j in range(2)] for k in range(T_RING)]
        h = [sb(f"h{i}", [P, TT]) for i in range(2)]
        h_hi = [sb(f"h_hi{i}", [P, G_I, TT], F32R) for i in range(2)]
        h_lo = [sb(f"h_lo{i}", [P, G_I, TT], F32R) for i in range(2)]
        cmb = [sb(f"cmb{i}", [P, TT]) for i in range(2)]
        group_ps = [ctx.enter_context(nc.psum_tensor(f"x_group{i}", [P, TT], F32)) for i in range(G_RING)]
        y_ps = [ctx.enter_context(nc.psum_tensor(f"x_y{i}", [P, TT], F32)) for i in range(Y_RING)]
        raw_landed, sc_landed, x_high, x_ready = sem("raw_landed"), sem("sc_landed"), sem("x_high"), sem("x_ready")
        cmb_landed = [sem(f"cmb_landed{i}") for i in range(2)]
        gu_groups = sem("gu_groups")
        decoded, gu_ready, wd_ready, d_high, d_ready, step_sem, scales_ready = (
            sem(n) for n in ("decoded", "gu_ready", "wd_ready", "d_high", "d_ready", "step", "scales_ready"))
        group_done, ev_act, ev_dve, summed, silu_done, weighted, h_done, h_high, h_ready, y_done, y_added = (
            sem(n) for n in ("group_done", "ev_act", "ev_dve", "summed", "silu_done", "weighted", "h_done", "h_high",
                             "h_ready", "y_done", "y_added"))
        block = ctx.enter_context(nc.Block())

        def each_tile(eng, output, product, down, between, late=0):
            def tile(tau, e, u, t, first=False):
                for o in range(NO):
                    output(tau, e, u, t, o)
                    if o % 2 == late:
                        if o >= 2:
                            product(tau, t, o // 2 - 1)
                        elif not first:
                            product(tau - 1, (t - 1) % NT, G_I - 1)
                    if not first:
                        for c in DOWN_AT.get(o, ()):
                            down(tau - 1, (t - 1) % NT, c)
                    if o % G_I == G_I - 1:
                        between(e, u, t + (o + 1) / NO)

            tile(0, 0, 0, 0, first=True)
            with eng.Fori(0, E_ROUTED // 2) as i:
                for k in range(1, 2 * NT + 1):
                    tile(2 * NT * i + k, 2 * i + k // NT, k // NT % 2, k % NT)
            last = E_ROUTED * NT
            for k in range(1, NT):
                tile(last + k, E_ROUTED, 0, k)
            product(last + NT - 1, NT - 1, G_I - 1)
            for c in range(C):
                down(last + NT - 1, NT - 1, c)

        def nothing(*_):
            pass

        def more(e):
            return not (isinstance(e, int) and e == E_ROUTED)

        def part_of(t, o):
            return (t * NO + o) % T_RING

        @block.sync
        def _(sp):
            def raw(e):
                for half in range(2):
                    r = slice(64 * half, 64 * half + 64)
                    sp.dma_start(raw_gu[r, :, :], a["gu"][bass.ds(e, 1)].rearrange("o r g n -> (o r) g n"))\
                      .then_inc(raw_landed, 16)
                    sp.dma_start(raw_d[r, :, :], a["d"][bass.ds(e, 1)].rearrange("o r g n -> (o r) g n"))\
                      .then_inc(raw_landed, 16)

            def scales(e):
                sp.dma_start(w_d[:, :, :].rearrange("p g n -> p (g n)"),
                             a["d_s"][bass.ds(e, 1), :].to_broadcast([P, G_I * N_D])).then_inc(sc_landed, 16)

            def weights_of(tau, t):
                sp.wait_ge(weighted, G_I * tau + G_I)
                sp.dma_start(cmb[t % 2][:, :], g.combine_dram[bass.ds(tau // NT if isinstance(tau, int) else tau_e[0], 1),
                                                              t * TT:(t + 1) * TT].to_broadcast([P, TT]))\
                  .then_inc(cmb_landed[t % 2], 16)

            tau_e = [None]

            def expert(e, raw_after, scales_after):
                tau_e[0] = e
                weights_of(NT * e, 0)
                weights_of(NT * e + 1, 1)
                if scales_after:
                    sp.wait_ge(d_ready, e + 1)
                    scales(e + 1)
                weights_of(NT * e + 2, 2)
                weights_of(NT * e + 3, 3)
                if raw_after:
                    sp.wait_ge(gu_ready, e + 2)
                    sp.wait_ge(wd_ready, e + 2)
                    raw(e + 2)

            sp.dma_start(s_gu[:, :, :, :], a["gu_s"]).then_inc(scales_ready, 16)
            raw(0)
            scales(0)
            sp.wait_ge(gu_ready, 1)
            sp.wait_ge(wd_ready, 1)
            raw(1)
            with sp.Fori(0, E_ROUTED - 1) as e:
                expert(e, True, True)
            expert(E_ROUTED - 1, False, True)
            expert(E_ROUTED, False, False)

        @block.tensor
        def _(pe):
            pe.sem_inc(y_done, Y_CREDIT)

            def output(tau, e, u, t, o):
                G = NO * tau + o
                if t == 0 and o == 0:
                    pe.wait_ge(gu_ready, e + 1)
                if isinstance(e, int) and e == 0 and o == 0:
                    pe.wait_ge(x_ready, t + 1)
                elif t > 0 and o == 0:
                    pe.wait_ge(x_ready, NT)
                col = (o % 2) * I_MOE + (o // 2) * P
                for q in range(G_D):
                    pe.wait_ge(*((ev_dve, 2 * G + q + 1) if q < 2 else (ev_act, 2 * G + q - 1)))
                    out = group_ps[(o * G_D + q) % G_RING]
                    for k, x in enumerate((x_hi, x_lo)):
                        mm = pe.matmul(out[:, :], w_gu[u][:, q, col:col + P], x[:, q, t * TT:(t + 1) * TT],
                                       start=k == 0, stop=k == 1)
                    mm.then_inc(group_done, 1)

            def down(tau, t, c):
                if c == 0:
                    pe.wait_ge(h_ready, G_I * tau + G_I + 2)
                    if t == 0:
                        pe.wait_ge(d_ready, tau_expert(tau) + 1)
                pe.wait_ge(y_added, C * tau + c + 1)
                n = 0
                for k in range(G_I):
                    for w, x in ((d_hi, h_hi), (d_hi, h_lo), (d_lo, h_hi)):
                        mm = pe.matmul(y_ps[c % Y_RING][:, :], w[:, k, c * P:(c + 1) * P], x[t % 2][:, k, :],
                                       start=n == 0, stop=n == 3 * G_I - 1)
                        n += 1
                mm.then_inc(y_done, 1)

            expert_now = [0]

            def tau_expert(tau):
                return expert_now[0]

            def between(e, u, at):
                if at >= 1:
                    expert_now[0] = e

            each_tile(pe, output, nothing, down, between)

        @block.scalar
        def _(act):
            for t in range(NT):
                cols = slice(t * TT, (t + 1) * TT)
                act.activation(x_hi[:, :, cols], g.xt[:, :, cols], ACT.Copy).then_inc(x_high, 1)
                if t == 0:
                    convert_first = True
            act.sem_inc(ev_act, 2)

            def convert(e, u, groups):
                act.wait_ge(decoded, e + 1)
                act.activation(mark_act[:, :], raw_gu[:, 0, 0:1].bitcast(F32), ACT.Copy)
                act.activation(w_gu[u][:, groups, :], raw_gu[:, groups, :].bitcast(F8), ACT.Copy, scale=FP8_GAIN)\
                   .then_inc(gu_groups, 1)

            def output(tau, e, u, t, o):
                G = NO * tau + o
                k = part_of(t, o)
                if t == 0 and o == 0:
                    act.wait_ge(scales_ready, e + 17)
                act.wait_ge(h_done, G_I * tau + o // 2 + 1)
                for j in range(2):
                    act.wait_ge(group_done, G_D * G + j + 1)
                    act.activation(part[k][j][:, :], group_ps[(o * G_D + j) % G_RING][:, :], ACT.Copy,
                                   scale=s_gu_now[:, u, o, j:j + 1]).then_inc(ev_act, 1)
                if o % 2:
                    act.wait_ge(summed, G)
                    x = part[part_of(t, o - 1)][0]
                    act.activation(x[:, :], x[:, :], ACT.Silu).then_inc(silu_done, 1)

            def product(tau, t, n):
                N = G_I * tau + n
                act.wait_ge(h_done, N + 3)
                act.wait_ge(y_done, C * tau + 1)
                act.activation(h_hi[t % 2][:, n, :], h[(t * G_I + n) % 2][:, :], ACT.Copy).then_inc(h_high, 1)

            def split_down(e):
                act.wait_ge(wd_ready, e + 1)
                act.wait_ge(y_done, NT * C * e + Y_CREDIT)
                act.activation(d_hi[:, :, :], w_d[:, :, :], ACT.Copy).then_inc(d_high, 1)

            def between(e, u, at):
                if at == 1:
                    split_down(e)
                if at > 2 and more(e):
                    q = int(2 * at) - 5
                    convert(e + 1, 1 - u, slice(q, q + 1))
                if at == NT and more(e):
                    act.wait_ge(gu_groups, G_D * (e + 2))
                    act.sem_inc(gu_ready, 1)

            convert(0, 0, slice(0, G_D))
            act.wait_ge(gu_groups, 1)
            act.sem_inc(gu_ready, 1)
            act.sem_inc(gu_groups, G_D - 1)
            each_tile(act, output, product, nothing, between, late=1)

        @block.gpsimd
        def _(pool):
            pool.sem_inc(weighted, 2 * G_I)
            pool.sem_inc(h_ready, 2)

            def output(tau, e, u, t, o):
                G = NO * tau + o
                x = part[part_of(t, o)]
                pool.wait_ge(ev_dve, 2 * G + 6)
                pool.tensor_tensor(x[0][:, :], x[0][:, :], x[1][:, :], ALU.add).then_inc(summed, 1)
                if o % 2:
                    pool.wait_ge(silu_done, G_I * tau + o // 2 + 1)
                    if o == 1:
                        pool.wait_ge(cmb_landed[t % 2], landed_of(e, t))
                    x = part[part_of(t, o - 1)][0]
                    pool.tensor_tensor(x[:, :], x[:, :], cmb[t % 2][:, :], ALU.mult).then_inc(weighted, 1)

            def landed_of(e, t):
                return 32 * e + 16 * (t // 2) + 16

            def product(tau, t, n):
                pool.wait_ge(h_high, G_I * tau + n + 1)
                pool.tensor_tensor(h_lo[t % 2][:, n, :], h[(t * G_I + n) % 2][:, :],
                                   h_hi[t % 2][:, n, :].bitcast(F32), ALU.subtract).then_inc(h_ready, 1)

            each_tile(pool, output, product, nothing, nothing)

        @block.vector
        def _(dve):
            steps = 6

            def decode(e):
                step = Chain(dve, step_sem, e * steps)
                dve.wait_ge(raw_landed, 64 * e + 64)
                decode_fp4(dve, step, g, raw_gu[:, :, :], tmp[:, :, :])
                dve.sem_inc(decoded, 1)

            def decode_down(e):
                step = Chain(dve, step_sem, e * steps + steps // 2)
                decode_fp4(dve, step, g, raw_d[:, :, :], tmp[:, 0:G_I, 0:N_D // 4])
                assert step.n == steps // 2

            def weigh_down(e):
                dve.wait_ge(sc_landed, 16 * e + 16)
                dve.tensor_copy(mark[:, :], raw_d[:, 0, 0:1])
                dve.scalar_tensor_tensor(w_d[:, :, :], raw_d[:, :, :].bitcast(F8), FP8_GAIN, w_d[:, :, :],
                                         ALU.mult, ALU.mult).then_inc(wd_ready, 1)

            def scales_now(e, u):
                dve.tensor_copy(s_gu_now[:, u, :, :], s_gu[:, bass.ds(e, 1), :, :].rearrange("p e o g -> p (e o) g"))\
                   .then_inc(scales_ready, 1)

            def output(tau, e, u, t, o):
                G = NO * tau + o
                k = part_of(t, o)
                if t == 0 and o == 0:
                    dve.wait_ge(scales_ready, e + 17)
                for j in range(2):
                    dve.wait_ge(group_done, G_D * G + j + 3)
                    dve.wait_ge(ev_act, 2 * G + j + 3)
                    x = part[k][j][:, :]
                    dve.scalar_tensor_tensor(x, group_ps[(o * G_D + 2 + j) % G_RING][:, :],
                                             s_gu_now[:, u, o, 2 + j:3 + j], x, ALU.mult, ALU.add).then_inc(ev_dve, 1)

            def product(tau, t, n):
                N = G_I * tau + n
                dve.wait_ge(weighted, N + 1 + 2 * G_I)
                dve.wait_ge(summed, 2 * N + 2)
                dve.wait_ge(h_ready, N + 1)
                gate, up = part[part_of(t, 2 * n)][0], part[part_of(t, 2 * n + 1)][0]
                dve.tensor_tensor(h[N_par(t, n)][:, :], gate[:, :], up[:, :], ALU.mult).then_inc(h_done, 1)

            def N_par(t, n):
                return (t * G_I + n) % 2

            def down(tau, t, c):
                dve.wait_ge(y_done, C * tau + c + 1 + Y_CREDIT)
                dve.wait_ge(y_added, C * tau + c + 1)
                x = g.xt[:, c, t * TT:(t + 1) * TT]
                dve.tensor_tensor(x, x, y_ps[c % Y_RING][:, :], ALU.add).then_inc(y_added, 1)

            def between(e, u, at):
                if at == 1:
                    dve.wait_ge(d_high, e + 1)
                    dve.tensor_tensor(d_lo[:, :, :], w_d[:, :, :], d_hi[:, :, :].bitcast(F32), ALU.subtract)\
                       .then_inc(d_ready, 1)
                for at_which, part_of_it in ((1.5, decode), (2, decode_down), (2.5, weigh_down)):
                    if at == at_which and more(e):
                        part_of_it(e + 1)
                if at == NT and more(e):
                    dve.wait_ge(ev_act, scaled_of(e))
                    scales_now(e + 1, 1 - u)

            def scaled_of(e):
                return 2 * NO * NT * e + 2

            dve.wait_ge(scales_ready, 16)
            dve.sem_inc(ev_dve, 4)
            dve.sem_inc(h_done, 2)
            dve.sem_inc(y_added, Y_RING)
            decode(0)
            decode_down(0)
            weigh_down(0)
            scales_now(0, 0)
            for t in range(NT):
                cols = slice(t * TT, (t + 1) * TT)
                dve.wait_ge(x_high, t + 1)
                dve.tensor_tensor(x_lo[:, :, cols], g.xt[:, :, cols], x_hi[:, :, cols].bitcast(F32), ALU.subtract)\
                   .then_inc(x_ready, 1)
            dve.wait_ge(x_ready, NT)
            each_tile(dve, output, product, down, between)


LAG = 2
RING = 8
X_RING = 16


def causal_attention(nc, g, a):
    SIDE_AT = {"queries": 0, "keys": 3, "norms": 7, "values": 9, "output": 13}
    FRONT = ("queries", "keys", "norms", "values")

    def use(b, name):
        return 5 * b + (14 if name == "output" else FRONT.index(name))

    LAST_USES = 5 * B

    with ExitStack() as ctx:
        def sb(name, shape, dt=F32):
            return ctx.enter_context(nc.sbuf_tensor("c_" + name, shape, dt))

        def sem(name):
            return ctx.enter_context(nc.semaphore("c_" + name))

        def ps(name, shape):
            return ctx.enter_context(nc.psum_tensor("c_" + name, shape, F32))

        w = {n: sb(n, [P, C, D]) for n in ("wq", "wqr", "wk", "wkr", "wv", "wo")}
        bias = {n: sb(n, [P, C]) for n in ("bq", "bqr", "bk", "bkr", "bo")}
        bv = sb("bv", [P, D])
        rope = sb("rope", [P, 2, D])
        xb = sb("xb", [P, C, S])
        q_raw, k_raw = sb("q_raw", [P, C, S]), sb("k_raw", [P, C, S])
        sq, sk = sb("sq", [P, C, S]), sb("sk", [P, C, S])
        nrm = sb("nrm", [P, 2, S])
        q_sb = [sb(f"q{i}", [P, C, S]) for i in range(2)]
        k_sb = sb("k", [P, C, S])
        kp = [sb(f"kp{i}", [P, 4, S]) for i in range(2)]
        v_sb = [sb(f"v{i}", [P, 2, D]) for i in range(2)]
        pt = [sb(f"pt{i}", [P, 3, P]) for i in range(RING)]
        at = [sb(f"at{i}", [P, C, S]) for i in range(2)]
        out_ps, den_ps, work = ps("out_ps", [P, C, S]), ps("den_ps", [P, C, S]), ps("work", [P, C, S])
        work_v = work[:, :, :].rearrange("p (k n) s -> p k (n s)", k=2)
        s_ps = [ps(f"s{i}", [P, 3, P]) for i in range(2)]
        q_loaded, k_loaded, v_loaded, o_loaded = (sem(n + "_loaded") for n in "qkvo")
        (folded, xb_ready, work_done, work_read, normed, kp_ready, s_done, exped, masked, av_done, at_ready, step_sem) = (
            sem(n) for n in ("folded", "xb_ready", "work_done", "work_read", "normed", "kp_ready", "s_done", "exped",
                             "masked", "av_done", "at_ready", "step"))
        block = ctx.enter_context(nc.Block())

        def every_batch(eng, heads):
            heads(0, 0, False, True)
            with eng.Fori(0, B // 2 - 1) as i:
                heads(2 * i + 1, 1, True, True)
                heads(2 * i + 2, 0, True, True)
            heads(B - 1, 1, True, False)

        def sides(h, b, last, following):
            for name in SIDE_AT:
                if SIDE_AT[name] == h:
                    if name == "output":
                        yield name if last else "nothing", b - 1, use(b - 1, name) if following else LAST_USES
                    elif following:
                        yield name, b + 1, use(b + 1, name)

        @block.sync
        def _(sp):
            sp.dma_start(rope[:, :, :].rearrange("p a n -> p (a n)"), a["rope"].to_broadcast([P, 2 * D]))\
              .then_inc(q_loaded, 16)
            for x, landed in (("q", q_loaded), ("k", k_loaded)):
                for n in ("w" + x, "w" + x + "r"):
                    sp.dma_start(w[n][:, :, :], a[n + "1"]).then_inc(landed, 16)
                for n in ("b" + x, "b" + x + "r"):
                    sp.dma_start(bias[n][:, :], a[n + "1"]).then_inc(landed, 16)
            sp.dma_start(w["wv"][:, :, :], a["wv1"]).then_inc(v_loaded, 16)
            sp.dma_start(bv[:, :], a["bv1"].to_broadcast([P, D])).then_inc(v_loaded, 16)
            sp.dma_start(w["wo"][:, :, :], a["wo1"]).then_inc(o_loaded, 16)
            sp.dma_start(bias["bo"][:, :], a["bo1"]).then_inc(o_loaded, 16)

        @block.gpsimd
        def _(pool):
            def copy(b, first=False):
                if not first:
                    pool.wait_ge(work_done, use(b - 1, "values") + 1)
                pool.tensor_copy(xb[:, :, :], g.xt[:, :, bass.ts(b, S)]).then_inc(xb_ready, 1)

            def heads(b, i, last, following):
                for h in range(H1):
                    pool.wait_ge(exped, H1 * b + h + 3)
                    diagonal = pt[h % RING][:, 0:3:2, :]
                    pool.tensor_tensor(diagonal, diagonal, bc(g.const("causal"), 1, [P, 2, P]), ALU.mult)\
                        .then_inc(masked, 1)
                    if h == 0 and following:
                        copy(b + 1)

            copy(0, True)
            every_batch(pool, heads)

        @block.tensor
        def _(pe):
            def project(w, x):
                for m in range(C):
                    for c in range(C):
                        mm = pe.matmul(work[:, m, :], w[:, c, m * P:(m + 1) * P], x(c), start=c == 0, stop=c == C - 1)
                return mm

            def side(name, b, i, n, first=False):
                if not first:
                    pe.wait_ge(work_read, n)
                if name == "nothing":
                    pe.sem_inc(work_done, 1)
                    return
                if name in ("queries", "keys"):
                    mm = project(w["w" + name[0]], lambda c: g.xt[:, c, bass.ts(b, S)])
                if name == "values":
                    pe.wait_ge(xb_ready, b + 1)
                    for k in range(2):
                        for c in range(C):
                            mm = pe.matmul(work_v[:, k, :], xb[:, c, k * P:(k + 1) * P], w["wv"][:, c, :],
                                           start=c == 0, stop=c == C - 1)
                if name == "norms":
                    for k, x in enumerate((sq, sk)):
                        for c in range(C):
                            mm = pe.matmul(work[:, k, :], g.const("ones"), x[:, c, :], start=c == 0, stop=c == C - 1)
                if name == "output":
                    pe.wait_ge(at_ready, b + 1)
                    mm = project(w["wo"], lambda c: at[i][:, c, :])
                mm.then_inc(work_done, 1)

            def score(b, i, h):
                c, j = h // 4, h % 4
                if j == 0:
                    pe.wait_ge(kp_ready, C * b + c + 1)
                pe.wait_ge(exped, H1 * b + h + 1)
                pe.matmul(s_ps[h % 2][:, 0:2, :], kp[c % 2][:, j, 0:P], q_sb[i][:, c, :], start=True, stop=True)
                pe.matmul(s_ps[h % 2][:, 2, :], kp[c % 2][:, j, P:S], q_sb[i][:, c, P:S], start=True, stop=True)\
                  .then_inc(s_done, 1)

            def values(b, i, c, last):
                pe.wait_ge(masked, H1 * b + 4 * c + 4)
                if c == 0 and last:
                    pe.wait_ge(at_ready, b)
                for y in (out_ps, den_ps):
                    for k in range(2):
                        for j in range(4):
                            h = 4 * c + j
                            r = slice(32 * j, 32 * j + 32)
                            x = pt[h % RING]
                            wt = v_sb[i][:, k, h * HD1:(h + 1) * HD1] if y is out_ps else g.const("ones")[:, 0:32]
                            if k == 0:
                                pe.matmul(y[r, c, :], wt, x[:, 0:2, :], start=True, stop=False, skip_group_check=True)
                            else:
                                mm = pe.matmul(y[r, c, P:S], wt, x[:, 2, :], start=False, stop=True,
                                               skip_group_check=True)
                mm.then_inc(av_done, 4)

            def heads(b, i, last, following):
                for h in range(H1 + LAG):
                    if h < H1:
                        score(b, i, h)
                    for name, of, n in sides(h, b, last, following):
                        side(name, of, 1 - i, n)
                    if h >= LAG and (h - LAG) % 4 == 3:
                        values(b, i, (h - LAG) // 4, last)

            pe.wait_ge(folded, 1)
            for name in FRONT:
                if name == "keys":
                    pe.wait_ge(folded, 2)
                if name == "values":
                    pe.wait_ge(v_loaded, 32)
                side(name, 0, 0, use(0, name), name == "queries")
            side("nothing", -1, 0, len(FRONT))
            pe.wait_ge(o_loaded, 32)
            every_batch(pe, heads)
            side("output", B - 1, 1, LAST_USES + 1)

        @block.scalar
        def _(act):
            def side(name, b, n, first=False):
                if name in ("queries", "keys"):
                    x, x2, bias_x = (q_raw, sq, bias["bq"]) if name == "queries" else (k_raw, sk, bias["bk"])
                    act.wait_ge(work_done, n + 1)
                    if not first:
                        act.wait_ge(normed, b)
                    for m in range(C):
                        act.activation(x2[:, m, :], work[:, m, :], ACT.Square, bias=bias_x[:, m:m + 1])
                        last = act.activation(x[:, m, :], work[:, m, :], ACT.Identity, bias=bias_x[:, m:m + 1])
                    last.then_inc(work_read, 1)
                if name == "norms":
                    act.wait_ge(work_done, n + 1)
                    act.activation(nrm[:, :, :], work[:, 0:2, :], ACT.Sqrt).then_inc(work_read, 1)

            def heads(b, i, last, following):
                for h in range(H1):
                    act.wait_ge(s_done, H1 * b + h + 1)
                    act.wait_ge(av_done, H1 * b + h + 1)
                    act.activation(pt[h % RING][:, :, :], s_ps[h % 2][:, :, :], ACT.Exp).then_inc(exped, 1)
                    for name, of, n in sides(h, b, last, following):
                        side(name, of, n)

            act.sem_inc(exped, 2)
            act.wait_ge(folded, 1)
            for name in FRONT:
                side(name, 0, use(0, name), True)
            every_batch(act, heads)

        @block.vector
        def _(dve):
            def side(name, b, i, n, step, first=False):
                if name == "nothing":
                    dve.wait_ge(work_done, n + 1)
                    dve.sem_inc(work_read, 1)
                if name == "output":
                    dve.wait_ge(work_done, n + 1)
                    for m in range(C):
                        x = g.xt[:, m, bass.ts(b, S)]
                        last = dve.scalar_tensor_tensor(x, work[:, m, :], bias["bo"][:, m:m + 1], x, ALU.add, ALU.add)
                    last.then_inc(work_read, 1)
                if name == "values":
                    dve.wait_ge(work_done, n + 1)
                    dve.tensor_tensor(v_sb[i][:, :, :], work_v, bc(bv[:, :], 1, [P, 2, D]), ALU.add).then_inc(work_read, 1)
                if name == "norms":
                    dve.wait_ge(work_read, n + 1)
                    step(dve.tensor_scalar(nrm[:, :, :], nrm[:, :, :], 1e-12, None, ALU.max))
                    step(dve.reciprocal(nrm[:, :, :], nrm[:, :, :]))
                    if not first:
                        dve.wait_ge(kp_ready, C * b)
                    dve.tensor_tensor(k_sb[:, :, :], k_raw[:, :, :], bc(nrm[:, 1, :], 1, [P, C, S]), ALU.mult)
                    dve.tensor_tensor(q_sb[i][:, :, :], q_raw[:, :, :], bc(nrm[:, 0, :], 1, [P, C, S]), ALU.mult)\
                       .then_inc(normed, 1)
                    dve.wait_ge(normed, b + 1)

            def spread(b, c, first=False):
                if not first:
                    dve.wait_ge(s_done, H1 * b + 4 * (c - 1))
                dve.tensor_tensor(kp[c % 2][:, :, :], bc(k_sb[:, c, :], 1, [P, 4, S]), bc(g.const("head4"), 2, [P, 4, S]),
                                  ALU.mult).then_inc(kp_ready, 1)

            def divide(b, i, c, step):
                pair = slice(c - 1, c + 1)
                dve.wait_ge(av_done, H1 * b + 4 * c + 4 + RING)
                step(dve.reciprocal(at[i][:, pair, :], den_ps[:, pair, :]))
                last = dve.tensor_tensor(at[i][:, pair, :], out_ps[:, pair, :], at[i][:, pair, :], ALU.mult)
                if c == C - 1:
                    last.then_inc(at_ready, 1)

            def heads(b, i, last, following):
                step = Chain(dve, step_sem, base + 4 * b)
                for h in range(H1 + LAG):
                    if h == 4:
                        spread(b, 2)
                    if h == 7:
                        spread(b, 3)
                    for name, of, n in sides(h, b, last, following):
                        side(name, of, 1 - i, n, step)
                    if h == 12 and following:
                        spread(b + 1, 0)
                    if h == H1 and following:
                        spread(b + 1, 1)
                    if h >= LAG and (h - LAG) % 8 == 7:
                        divide(b, i, (h - LAG) // 4, step)

            dve.sem_inc(av_done, RING)
            cos, sin = (bc(rope[:, n, :], 1, [P, C, D]) for n in range(2))
            step = Chain(dve, step_sem)
            for x, landed, count in (("q", q_loaded, 80), ("k", k_loaded, 64)):
                dve.wait_ge(landed, count)
                wx, wr, bx, br = w["w" + x][:, :, :], w["w" + x + "r"][:, :, :], bias["b" + x][:, :], bias["b" + x + "r"][:, :]
                dve.tensor_tensor(wx, wx, cos, ALU.mult)
                dve.tensor_tensor(bx, bx, g.const("cosc"), ALU.mult)
                dve.tensor_tensor(br, br, g.const("sinc"), ALU.mult)
                step(dve.tensor_tensor(wr, wr, sin, ALU.mult))
                dve.tensor_tensor(bx, bx, br, ALU.add)
                step(dve.tensor_tensor(wx, wx, wr, ALU.add))
                dve.sem_inc(folded, 1)
            dve.wait_ge(v_loaded, 32)
            side("norms", 0, 0, use(0, "norms"), step, True)
            side("values", 0, 0, use(0, "values"), step, True)
            side("nothing", -1, 0, len(FRONT), step)
            base = step.n
            spread(0, 0, True)
            spread(0, 1, True)
            dve.wait_ge(o_loaded, 32)
            every_batch(dve, heads)
            side("output", B - 1, 1, LAST_USES + 1, step)


def cross_attention(nc, g, a):
    SIDE_AT = {"output": 5, "queries": 8, "keys": 12, "values": 15, "query_norm": 20, "key_norm": 25}
    FRONT = ("queries", "keys", "values", "query_norm", "key_norm")

    def use(b, name):
        return 6 * b + (11 if name == "output" else FRONT.index(name))

    LAST_USE = 6 * B

    with ExitStack() as ctx:
        def sb(name, shape, dt=F32):
            return ctx.enter_context(nc.sbuf_tensor("y_" + name, shape, dt))

        def sem(name):
            return ctx.enter_context(nc.semaphore("y_" + name))

        def ps(name, shape):
            return ctx.enter_context(nc.psum_tensor("y_" + name, shape, F32))

        wq, wk, wv = (sb(n, [P, C, D]) for n in ("wq", "wk", "wv"))
        cb = sb("cb", [P, C, S])
        q_raw, k_raw = sb("q_raw", [P, C, S]), sb("k_raw", [P, C, S])
        sq, sk = sb("sq", [P, C, S]), sb("sk", [P, C, S])
        q_sb = [sb(f"q{i}", [P, C, S]) for i in range(2)]
        k_sb = sb("k", [P, C, S])
        kp = [sb(f"kp{i}", [P, 8, S]) for i in range(2)]
        vp = [[sb(f"vp{i}{e}", [P, 2, HX // 2, 2, HDX]) for e in range(2)] for i in range(2)]
        pt = [sb(f"pt{i}", [P, 2, S]) for i in range(X_RING)]
        at = sb("at", [P, C, S])
        out_ps, den_ps = ps("out_ps", [P, C, S]), ps("den_ps", [P, C, S])
        work = ps("work", [P, C, S])
        work_v = work[:, :, :].rearrange("p (k n) s -> p k (n s)", k=2)
        s_ps = ps("s_ps", [P, 2, 2, S])
        q_loaded, k_loaded, v_loaded, ct_loaded = (sem(n + "_loaded") for n in ("q", "k", "v", "ct"))
        (zeroed, cb_ready, work_done, work_read, root_ready, normed, kp_ready, s_done, exped, av_done,
         at_ready, step_sem) = (
            sem(n) for n in ("zeroed", "cb_ready", "work_done", "work_read", "root_ready", "normed",
                             "kp_ready", "s_done", "exped", "av_done", "at_ready", "step"))
        eps = g.const("eps")[:, 1:2]
        block = ctx.enter_context(nc.Block())

        def every_batch(eng, heads):
            heads(0, 0, False, True)
            with eng.Fori(0, B // 2 - 1) as i:
                heads(2 * i + 1, 1, True, True)
                heads(2 * i + 2, 0, True, True)
            heads(B - 1, 1, True, False)

        def sides(h, b, last, following):
            for name in SIDE_AT:
                if SIDE_AT[name] == h:
                    if name == "output" and last:
                        yield name, b - 1
                    if name != "output" and following:
                        yield name, b + 1

        @block.sync
        def _(sp):
            first, rest = slice(0, 2 * S), slice(2 * S, T)
            sp.dma_start(wq[:, :, :], a["wqx"]).then_inc(q_loaded, 16)
            sp.dma_start(g.aux[:, :, first], a["ct"][:, :, first]).then_inc(ct_loaded, 16)
            sp.dma_start(wk[:, :, :], a["wkx"]).then_inc(k_loaded, 16)
            sp.dma_start(wv[:, :, :], a["wvx"]).then_inc(v_loaded, 16)
            sp.wait_ge(ct_loaded, 16)
            sp.dma_start(g.aux[:, :, rest], a["ct"][:, :, rest]).then_inc(ct_loaded, 16)

        @block.gpsimd
        def _(pool):
            for i in range(2):
                for e in range(2):
                    pool.memset(vp[i][e][:, :, :, :, :], 0.0).then_inc(zeroed, 1)
            pool.wait_ge(ct_loaded, 16)
            pool.tensor_copy(cb[:, :, :], g.aux[:, :, 0:S]).then_inc(cb_ready, 1)
            pool.wait_ge(ct_loaded, 32)
            with pool.Fori(1, B) as b:
                pool.wait_ge(work_done, use(b - 1, "values") + 1)
                pool.tensor_copy(cb[:, :, :], g.aux[:, :, bass.ts(b, S)]).then_inc(cb_ready, 1)

        @block.tensor
        def _(pe):
            def project(w, x):
                for m in range(C):
                    for c in range(C):
                        mm = pe.matmul(work[:, m, :], w[:, c, m * P:(m + 1) * P], x(c), start=c == 0, stop=c == C - 1)
                return mm

            def side(name, b, n, first=False):
                if not first:
                    pe.wait_ge(work_read, n)
                if name == "queries":
                    mm = project(wq, lambda c: g.xt[:, c, bass.ts(b, S)])
                if name == "keys":
                    pe.wait_ge(cb_ready, b + 1)
                    mm = project(wk, lambda c: cb[:, c, :])
                if name == "values":
                    for k in range(2):
                        for c in range(C):
                            mm = pe.matmul(work_v[:, k, :], cb[:, c, k * P:(k + 1) * P], wv[:, c, :],
                                           start=c == 0, stop=c == C - 1)
                if name in ("query_norm", "key_norm"):
                    x = sq if name == "query_norm" else sk
                    for c in range(C):
                        mm = pe.matmul(work[:, c, :], g.const("blk16"), x[:, c, :], start=True, stop=True)
                if name == "output":
                    pe.wait_ge(at_ready, b + 1)
                    for m in range(C):
                        mm = pe.matmul(work[:, m, :], g.const("perm"), at[:, m, :], start=True, stop=True)
                mm.then_inc(work_done, 1)

            def score(b, i, h):
                c, j = h // 8, h % 8
                if j == 0:
                    pe.wait_ge(kp_ready, C * b + c + 1)
                pe.wait_ge(exped, HX * b + h + 1)
                for k in range(2):
                    mm = pe.matmul(s_ps[:, h % 2, k, :], kp[c % 2][:, j, k * P:(k + 1) * P], q_sb[i][:, c, :],
                                   start=True, stop=True)
                mm.then_inc(s_done, 1)

            def values(b, i, c, last):
                pe.wait_ge(exped, HX * b + 8 * c + 8 + 2)
                if c == 0 and last:
                    pe.wait_ge(at_ready, b)
                for y in (out_ps, den_ps):
                    for e in range(2):
                        for k in range(2):
                            for j in range(4):
                                pair = 4 * c + j
                                w = vp[i][e][:, k, pair, :, :] if y is out_ps else g.const("den16")[:, 32 * e:32 * e + 32]
                                mm = pe.matmul(y[32 * j:32 * j + 32, c, :], w, pt[(2 * pair + e) % X_RING][:, k, :],
                                               start=e == 0 and k == 0, stop=e == 1 and k == 1,
                                               skip_group_check=True)
                mm.then_inc(av_done, 8)

            def heads(b, i, last, following):
                for h in range(HX + LAG):
                    if h < HX:
                        score(b, i, h)
                    for name, of in sides(h, b, last, following):
                        side(name, of, use(of, name))
                        if name == "queries" and not last:
                            pe.sem_inc(work_done, 1)
                    if h >= LAG and (h - LAG) % 8 == 7:
                        values(b, i, (h - LAG) // 8, last)

            pe.wait_ge(zeroed, 4)
            for name in FRONT:
                if name in ("queries", "keys", "values"):
                    pe.wait_ge({"queries": q_loaded, "keys": k_loaded, "values": v_loaded}[name], 16)
                side(name, 0, use(0, name), name == "queries")
            every_batch(pe, heads)
            side("output", B - 1, LAST_USE)

        @block.scalar
        def _(act):
            def side(name, b, n, first=False):
                if name in ("queries", "keys"):
                    x, x2, k = (q_raw, sq, 1) if name == "queries" else (k_raw, sk, 2)
                    act.wait_ge(work_done, n + 1)
                    if not first:
                        act.wait_ge(normed, 2 * b - 2 + k)
                    act.activation(x2[:, :, :], work[:, :, :], ACT.Square)
                    act.activation(x[:, :, :], work[:, :, :], ACT.Copy).then_inc(work_read, 1)
                if name in ("query_norm", "key_norm"):
                    x2 = sq if name == "query_norm" else sk
                    act.wait_ge(work_done, n + 1)
                    act.activation(x2[:, :, :], work[:, :, :], ACT.Ln, bias=eps).then_inc(work_read, 1)
                    act.wait_ge(work_read, n + 1)
                    act.activation(x2[:, :, :], x2[:, :, :], ACT.Exp, scale=-0.5).then_inc(root_ready, 1)

            def heads(b, i, last, following):
                for h in range(HX):
                    act.wait_ge(s_done, HX * b + h + 1)
                    act.wait_ge(av_done, HX * b + h + 1)
                    act.activation(pt[h % X_RING][:, :, :], s_ps[:, h % 2, :, :], ACT.Exp, scale=HDX ** -0.5)\
                       .then_inc(exped, 1)
                    for name, of in sides(h, b, last, following):
                        side(name, of, use(of, name))

            act.sem_inc(exped, 2)
            for name in FRONT:
                side(name, 0, use(0, name), True)
            act.sem_inc(work_read, 1)
            every_batch(act, heads)

        @block.vector
        def _(dve):
            def side(name, b, i, n, first=False):
                if name == "output":
                    x = g.xt[:, :, bass.ts(b, S)]
                    dve.wait_ge(work_done, n + 1)
                    dve.tensor_tensor(x, work[:, :, :], x, ALU.add).then_inc(work_read, 1)
                if name == "values":
                    dve.wait_ge(work_done, n + 1)
                    v = work_v.rearrange("p k (n e d) -> p k n e d", e=2, d=HDX)
                    for e in range(2):
                        last = dve.tensor_copy(vp[i][e][:, :, :, e, :], v[:, :, :, e, :])
                    last.then_inc(work_read, 1)
                if name == "query_norm":
                    dve.wait_ge(root_ready, 2 * b + 1)
                    dve.tensor_tensor(q_sb[i][:, :, :], q_raw[:, :, :], sq[:, :, :], ALU.mult).then_inc(normed, 1)
                if name == "key_norm":
                    dve.wait_ge(root_ready, 2 * b + 2)
                    if not first:
                        dve.wait_ge(kp_ready, C * b)
                    dve.tensor_tensor(k_sb[:, :, :], k_raw[:, :, :], sk[:, :, :], ALU.mult).then_inc(normed, 1)
                    dve.wait_ge(normed, 2 * b + 2)

            def spread(b, c, first=False):
                if not first:
                    dve.wait_ge(s_done, HX * b + 8 * (c - 1))
                dve.tensor_tensor(kp[c % 2][:, :, :], bc(k_sb[:, c, :], 1, [P, 8, S]), bc(g.const("head8"), 2, [P, 8, S]),
                                  ALU.mult).then_inc(kp_ready, 1)

            def divide(b, c, step):
                pair = slice(c - 1, c + 1)
                dve.wait_ge(av_done, HX * b + 8 * c + 8 + X_RING)
                step(dve.reciprocal(at[:, pair, :], den_ps[:, pair, :]))
                last = dve.tensor_tensor(at[:, pair, :], out_ps[:, pair, :], at[:, pair, :], ALU.mult)
                if c == C - 1:
                    last.then_inc(at_ready, 1)

            def heads(b, i, last, following):
                step = Chain(dve, step_sem, C // 2 * b)
                for h in range(HX + LAG):
                    for name, of in sides(h, b, last, following):
                        side(name, of, i if name == "output" else 1 - i, use(of, name))
                        if name == "key_norm":
                            spread(of, 0)
                    if h in (8, 16):
                        spread(b, h // 8 + 1)
                    if h == HX - 1 and following:
                        spread(b + 1, 1)
                    if h >= LAG and (h - LAG) % 16 == 15:
                        divide(b, (h - LAG) // 8, step)

            dve.sem_inc(av_done, X_RING)
            dve.wait_ge(zeroed, 4)
            for name in FRONT[2:]:
                side(name, 0, 0, use(0, name), True)
            spread(0, 0, True)
            spread(0, 1, True)
            every_batch(dve, heads)
            side("output", B - 1, 1, LAST_USE)


def feed_forward(nc, g, a):
    GATE, UP, DOWN, BLOCKS = 0, C, 2 * C, 3 * C
    SLICE = BLOCKS * P
    with ExitStack() as ctx:
        def sb(name, shape, dt=F32):
            return ctx.enter_context(nc.sbuf_tensor("f_" + name, shape, dt))

        def sem(name):
            return ctx.enter_context(nc.semaphore("f_" + name))

        def ps(name, shape):
            return ctx.enter_context(nc.psum_tensor("f_" + name, shape, F32))

        w_hi, w_lo = sb("w_hi", [P, G_F, BLOCKS, P], F32R), sb("w_lo", [P, G_F, BLOCKS, P], BF16)
        x_hi, x_lo, x_b = sb("x_hi", [P, C, TT], F32R), sb("x_lo", [P, C, TT], F32R), sb("x_b", [P, C, TT], BF16)
        h = [sb(f"h{i}", [P, TT]) for i in range(2)]
        h_hi, h_lo = ([sb(f"{n}{i}", [P, TT], F32R) for i in range(2)] for n in ("h_hi", "h_lo"))
        h_b = [sb(f"h_b{i}", [P, TT], BF16) for i in range(2)]
        flat = g.aux[:, :, :].rearrange("p c t -> p (c t)")
        scratch = {}
        at = 0
        for name, words in (("w", SLICE), ("raw", SLICE // 4), ("scales", SLICE // 2)):
            scratch[name] = [flat[:, at + i * words:at + (i + 1) * words] for i in range(2)]
            at += 2 * words
        w32 = scratch["w"]
        raw = [x.bitcast(I32) for x in scratch["raw"]]
        raw8 = [x.bitcast(F8) for x in scratch["raw"]]
        scales = [x.bitcast(F16) for x in scratch["scales"]]
        tmp = flat[:, at:at + SLICE // 4].bitcast(I32)
        assert at + SLICE // 4 <= C * T

        gate_ps = [ps(f"gate{i}", [P, TT]) for i in range(2)]
        up_ps = [ps(f"up{i}", [P, TT]) for i in range(2)]
        y_ps = ps("y", [P, C, TT])
        landed = [sem(f"landed{i}") for i in range(2)]
        (w_ready, w_high, w_split, x_high, x_ready, gu_done, silu_done, h_done, h_high, h_ready, h_used, y_copied,
         step_sem) = (
            sem(n) for n in ("w_ready", "w_high", "w_split", "x_high", "x_ready", "gu_done", "silu_done", "h_done",
                             "h_high", "h_ready", "h_used", "y_copied", "step"))
        block = ctx.enter_context(nc.Block())

        def wait_past(eng, sem, count):
            if not isinstance(count, int) or count > 0:
                eng.wait_ge(sem, count)

        def before(t, n):
            return t * G_F + (n - 1 if n > 0 else 0)

        def every_tile(eng, tile):
            tile(0, True)
            with eng.Fori(1, NT) as t:
                tile(t, False)

        @block.sync
        def _(sp):
            for n in range(G_F):
                if n >= 2:
                    sp.wait_ge(w_ready, n - 1)
                for half in range(2):
                    sp.dma_start(raw[n % 2][64 * half:64 * half + 64, :], a["ffn"][:, n, :]).then_inc(landed[n % 2], 16)
                sp.dma_start(scales[n % 2], a["ffn_s"][:, n, :].to_broadcast([P, SLICE])).then_inc(landed[n % 2], 16)

        @block.tensor
        def _(pe):
            def three(y, n, block, hi, lo, b, start, stop):
                wh, wl = w_hi[:, n, block, :], w_lo[:, n, block, :]
                pe.matmul(y, wh, hi, start=start, stop=False)
                pe.matmul(y, wh, lo, start=False, stop=False)
                return pe.matmul(y, wl, b, start=False, stop=stop)

            def gate_up(t, n, first):
                if first:
                    pe.wait_ge(w_split, n + 1)
                if n == 0:
                    pe.wait_ge(x_ready, t + 1)
                wait_past(pe, h_done, before(t, n))
                for y, block in ((gate_ps[n % 2], GATE), (up_ps[n % 2], UP)):
                    for c in range(C):
                        mm = three(y[:, :], n, block + c, x_hi[:, c, :], x_lo[:, c, :], x_b[:, c, :], c == 0, c == C - 1)
                mm.then_inc(gu_done, 1)

            def down(t, m):
                pe.wait_ge(h_ready, t * G_F + m + 1)
                if m == 0:
                    wait_past(pe, y_copied, t)
                for k in range(C):
                    mm = three(y_ps[:, k, :], m, DOWN + k, h_hi[m % 2][:, :], h_lo[m % 2][:, :], h_b[m % 2][:, :],
                               m == 0, m == G_F - 1)
                mm.then_inc(h_used, 1)

            def tile(t, first):
                for n in range(G_F + 1):
                    if n < G_F:
                        gate_up(t, n, first)
                    if n >= 1:
                        down(t, n - 1)

            every_tile(pe, tile)

        @block.scalar
        def _(act):
            def split_x(t):
                wait_past(act, gu_done, t * G_F)
                x = g.xt[:, :, bass.ts(t, TT)]
                act.activation(x_hi[:, :, :], x, ACT.Copy).then_inc(x_high, 1)
                act.activation(x_b[:, :, :], x, ACT.Copy).then_inc(x_high, 1)

            def split_w(n):
                act.wait_ge(w_ready, n + 1)
                act.activation(w_hi[:, n, :, :].rearrange("p b n -> p (b n)"), w32[n % 2], ACT.Copy).then_inc(w_high, 1)

            def copy_y(t):
                act.wait_ge(h_used, (t + 1) * G_F)
                act.activation(g.aux[:, :, bass.ts(t, TT)], y_ps[:, :, :], ACT.Copy).then_inc(y_copied, 1)

            def tile(t, first):
                if not first:
                    split_x(t)
                    copy_y(t - 1)
                for n in range(G_F):
                    k, N = n % 2, t * G_F + n
                    act.wait_ge(gu_done, N + 1)
                    wait_past(act, h_ready, before(t, n))
                    act.activation(h[k][:, :], gate_ps[k][:, :], ACT.Silu).then_inc(silu_done, 1)
                    act.wait_ge(h_done, N + 1)
                    wait_past(act, h_used, before(t, n))
                    act.activation(h_b[k][:, :], h[k][:, :], ACT.Copy)
                    act.activation(h_hi[k][:, :], h[k][:, :], ACT.Copy).then_inc(h_high, 1)
                    if first and n + 2 < G_F:
                        split_w(n + 2)

            split_x(0)
            split_w(0)
            split_w(1)
            every_tile(act, tile)
            copy_y(NT - 1)

        @block.gpsimd
        def _(pool):
            for n in range(G_F):
                pool.wait_ge(w_high, n + 1)
                hi = w_hi[:, n, :, :].rearrange("p b n -> p (b n)").bitcast(F32)
                pool.tensor_tensor(w_lo[:, n, :, :].rearrange("p b n -> p (b n)"), w32[n % 2], hi, ALU.subtract)\
                    .then_inc(w_split, 1)

        @block.vector
        def _(dve):
            step = Chain(dve, step_sem)

            def dequantize(n):
                dve.wait_ge(landed[n % 2], 48 * (n // 2 + 1))
                decode_fp4(dve, step, g, raw[n % 2], tmp)
                if n >= 2:
                    dve.wait_ge(w_split, n - 1)
                dve.scalar_tensor_tensor(w32[n % 2], raw8[n % 2], FP8_GAIN, scales[n % 2], ALU.mult, ALU.mult)\
                   .then_inc(w_ready, 1)

            def split_x(t):
                dve.wait_ge(x_high, 2 * t + 2)
                dve.tensor_tensor(x_lo[:, :, :], g.xt[:, :, bass.ts(t, TT)], x_hi[:, :, :].bitcast(F32), ALU.subtract)\
                   .then_inc(x_ready, 1)

            def tile(t, first):
                if not first:
                    split_x(t)
                for n in range(G_F):
                    k, N = n % 2, t * G_F + n
                    dve.wait_ge(silu_done, N + 1)
                    dve.tensor_tensor(h[k][:, :], h[k][:, :], up_ps[k][:, :], ALU.mult).then_inc(h_done, 1)
                    dve.wait_ge(h_high, N + 1)
                    dve.tensor_tensor(h_lo[k][:, :], h[k][:, :], h_hi[k][:, :].bitcast(F32), ALU.subtract)\
                       .then_inc(h_ready, 1)
                    if first and n + 3 < G_F:
                        dequantize(n + 3)

            dequantize(0)
            split_x(0)
            dequantize(1)
            dequantize(2)
            every_tile(dve, tile)


def rms_residual(nc, g, a):
    with ExitStack() as ctx:
        def sb(name, shape, dt=F32):
            return [ctx.enter_context(nc.sbuf_tensor(f"z_{name}{i}", shape, dt)) for i in range(2)]

        def sem(name):
            return ctx.enter_context(nc.semaphore("z_" + name))

        squares, rs = sb("squares", [P, C, TT]), sb("rs", [P, TT])
        ms_ps = [ctx.enter_context(nc.psum_tensor(f"z_ms{i}", [P, TT], F32)) for i in range(2)]
        squared, summed, logged, rs_ready, step_sem = (
            sem(n) for n in ("squared", "summed", "logged", "rs_ready", "step"))
        eps = g.const("eps")[:, 1:2]
        block = ctx.enter_context(nc.Block())

        def tile(x, t):
            return x[:, :, t * TT:(t + 1) * TT]

        @block.tensor
        def _(pe):
            for t in range(NT):
                pe.wait_ge(squared, t + 1)
                if t >= 2:
                    pe.wait_ge(logged, t - 1)
                for c in range(C):
                    mm = pe.matmul(ms_ps[t % 2][:, :], g.const("mean"), squares[t % 2][:, c, :],
                                   start=c == 0, stop=c == C - 1)
                mm.then_inc(summed, 1)

        @block.scalar
        def _(act):
            def square(t):
                if t >= 2:
                    act.wait_ge(summed, t - 1)
                act.activation(squares[t % 2][:, :, :], tile(g.aux, t), ACT.Square).then_inc(squared, 1)

            square(0)
            for t in range(NT):
                if t + 1 < NT:
                    square(t + 1)
                act.wait_ge(summed, t + 1)
                if t >= 2:
                    act.wait_ge(step_sem, 2 * (t - 2) + 1)
                act.activation(rs[t % 2][:, :], ms_ps[t % 2][:, :], ACT.Ln, bias=eps).then_inc(logged, 1)
                act.wait_ge(logged, t + 1)
                act.activation(rs[t % 2][:, :], rs[t % 2][:, :], ACT.Exp, scale=-0.5).then_inc(rs_ready, 1)

        @block.vector
        def _(dve):
            step = Chain(dve, step_sem)
            for t in range(NT):
                dve.wait_ge(rs_ready, t + 1)
                step(dve.tensor_tensor(tile(g.aux, t), tile(g.aux, t), bc(rs[t % 2][:, :], 1, [P, C, TT]), ALU.mult))
                step(dve.tensor_tensor(tile(g.aux, t), tile(g.aux, t), tile(g.xt, t), ALU.add))


def decoder(nc, a, out, stop=99):
    with ExitStack() as ctx:
        g = Shared()
        g.xt = ctx.enter_context(nc.sbuf_tensor("residual", [P, C, T], F32))
        g.consts = ctx.enter_context(nc.sbuf_tensor("const_tables", [P, N_CONST], F32))
        g.shift = ctx.enter_context(nc.sbuf_tensor("fp4_shifts", [P, 4], I32))
        g.const = lambda name: g.consts[:, COL[name][0]:COL[name][1]]
        g.ln_sems = [ctx.enter_context(nc.semaphore("ln_" + n)) for n in
                     ("mean_ready", "centred_ready", "squares_ready", "var_ready", "ln_ready", "rs_ready", "normed")]
        g.stored = ctx.enter_context(nc.semaphore("stored"))
        g.stored_base = 0
        g.combine_dram = nc.dram_tensor("combine", [E_ROUTED + 1, T], F32, kind="Internal").ap()
        with ExitStack() as inner:
            g.keys = inner.enter_context(nc.sbuf_tensor("keys", [P, C, B, 4 * SLOTS], F32))
            g.values = inner.enter_context(nc.sbuf_tensor("values", [P, B, H0 // 2, 64], F32))
            sparse_select(nc, g, a)
            sparse_attention(nc, g, a)

        def with_aux(n, stage):
            with nc.sbuf_tensor(f"aux{n}", [P, C, T], F32) as g.aux:
                stage()

        def last_stages():
            feed_forward(nc, g, a)
            rms_residual(nc, g, a)
            layer_norm(nc, g, g.aux, g.xt, 5, out)

        plan = [lambda: layer_norm(nc, g, g.xt, g.xt, 0), lambda: with_aux(0, lambda: wkv(nc, g, a)),
                lambda: layer_norm(nc, g, g.xt, g.xt, 1), lambda: route(nc, g, a), lambda: experts(nc, g, a),
                lambda: layer_norm(nc, g, g.xt, g.xt, 2), lambda: causal_attention(nc, g, a),
                lambda: layer_norm(nc, g, g.xt, g.xt, 3), lambda: with_aux(1, lambda: cross_attention(nc, g, a)),
                lambda: layer_norm(nc, g, g.xt, g.xt, 4), lambda: with_aux(2, last_stages)]
        for k, phase in enumerate(plan):
            if k >= stop:
                break
            phase()
        if stop < len(plan):
            with nc.Block() as block:
                @block.sync
                def _(sp):
                    sp.dma_start(out, g.xt[:, :, :]).then_inc(g.stored, 16)
                    sp.wait_ge(g.stored, 16)


def lay_out(i):
    order = feature_order()
    i = {k: np.asarray(v) for k, v in i.items()}

    def chunks(w):
        return w.reshape(w.shape[0] // P, P, *w.shape[1:]).swapaxes(0, 1)

    def residual(w):
        return chunks(w)[order]

    def reorder(w, n=P):
        return w.reshape(*w.shape[:-1], w.shape[-1] // P, P)[..., order].reshape(w.shape)

    def nibbles(packed):
        *lead, rows, n = packed.shape
        b = np.ascontiguousarray(packed).view(np.uint8).reshape(-1, rows // 16, 16, n, 4)
        b = np.ascontiguousarray(b.transpose(0, 2, 4, 1, 3)).view(np.int32)
        return b.reshape(*lead, 64, rows // 16, n // 4)

    x = i["x"].reshape(T, D)
    tables, rope = constants()
    o = {"consts": tables, "rope": rope, "xt": residual(np.ascontiguousarray(x.T)),
         "ct": residual(np.ascontiguousarray(i["ctx_2048"].reshape(T, D).T)),
         "xtok": reorder(x).reshape(T // P, P, D).swapaxes(0, 1)}
    o["wi0"] = residual(i["L0_attn_Wi"])[:, :, 0]
    o["bi0"] = i["L0_attn_bi"].reshape(1, 1)
    for n in "qkv":
        o[f"w{n}0"] = residual(i[f"L0_attn_W{n}"])
    for n in "qk":
        o[f"b{n}0"] = chunks(i[f"L0_attn_b{n}"])
    o["bv0"] = i["L0_attn_bv"].reshape(1, D)
    o["wo0"] = chunks(reorder(i["L0_attn_Wo"]))
    o["bo0"] = residual(i["L0_attn_bo"])
    o["decay"], o["first"] = residual(i["L0_xattn_time_decay"]), residual(i["L0_xattn_time_first"])
    o["gate"] = residual(i["L0_ffn_gate_w"].T)
    o["one_row"] = np.ones((1, T), np.float32)

    def stack(name):
        return np.concatenate([i[f"L0_ffn_{name}"], i[f"L0_ffn_shared_{name}"][None]])

    o["gu"] = nibbles(reorder(stack("gate_up_packed")))
    o["d"] = nibbles(reorder(stack("down_packed")))
    o["gu_s"] = reorder(stack("gate_up_scales")).reshape(E_ROUTED + 1, G_D, 2, G_I, P)\
        .transpose(4, 0, 3, 2, 1).reshape(P, E_ROUTED + 1, 2 * G_I, G_D)
    o["d_s"] = reorder(stack("down_scales")).reshape(E_ROUTED + 1, -1)
    turn = np.concatenate([np.arange(1, D, 2), np.arange(0, D, 2)])
    for k, n in enumerate("qkv"):
        w, b = i["L1_attn_Wqkv"][k * D:(k + 1) * D], i["L1_attn_bqkv"][k * D:(k + 1) * D]
        o[f"w{n}1"] = residual(w.T)
        if n == "v":
            o["bv1"] = b.reshape(1, D)
        else:
            o[f"b{n}1"] = chunks(b)
            o[f"w{n}r1"], o[f"b{n}r1"] = residual(w[turn].T), chunks(b[turn])
    o["wo1"] = chunks(reorder(i["L1_attn_Wout"].T))
    o["bo1"] = residual(i["L1_attn_bout"])
    kv = np.concatenate([i["L1_xattn_Wk"], i["L1_xattn_Wv"]])
    o["wqx"], o["wkx"], o["wvx"] = (residual(w.T) for w in (i["L1_xattn_Wq"], kv[0::2], kv[1::2]))
    gu = nibbles(reorder(i["L1_ffn_gate_up_packed"].T)).reshape(64, C, 2, G_F, P // 4)
    d = nibbles(reorder(i["L1_ffn_down_packed"].T)).reshape(64, G_F, C, P // 4)
    gu_s = reorder(i["L1_ffn_gate_up_scales"]).reshape(C, 2, G_F, P)
    d_s = reorder(i["L1_ffn_down_scales"]).reshape(G_F, C, P)
    gu, gu_s = gu.transpose(0, 3, 2, 1, 4).reshape(64, G_F, 2 * C, P // 4), gu_s.transpose(2, 1, 0, 3).reshape(G_F, 2 * C, P)
    o["ffn"] = np.concatenate([gu, d], axis=2).reshape(64, G_F, 3 * C * P // 4)
    o["ffn_s"] = np.concatenate([gu_s, d_s], axis=1).reshape(1, G_F, 3 * C * P)
    shift = np.zeros((P, 4), np.int64)
    shift[:64, 0] = 4
    shift[:, 1], shift[:, 2], shift[:, 3] = 2, 0x1C1C1C1C, 0x80808080 - (1 << 32)
    o["shift"] = shift.astype(np.int32)
    return {k: np.ascontiguousarray(v) for k, v in o.items()}


def kernel(**inputs):
    import concourse.bacc as _bacc
    from concourse import mybir as _mybir
    from concourse.bass_utils import run_bass_kernel_spmd as _run

    nc = _bacc.Bacc("TRN2", target_bir_lowering=False, num_devices=1)
    arrays = lay_out(inputs)
    args = {n: nc.dram_tensor(n, v.shape, _mybir.dt.from_np(v.dtype), kind="ExternalInput").ap()
            for n, v in arrays.items()}
    out = nc.dram_tensor("out", (P, C, T), F32, kind="ExternalOutput").ap()
    decoder(nc, args, out)
    r = _run(nc, [arrays], core_ids=[0])
    got = np.asarray(r.results[0]["out"])
    natural = np.empty_like(got)
    natural[feature_order()] = got
    return np.ascontiguousarray(natural.swapaxes(0, 1).reshape(D, T).T).reshape(B, S, D)
```
